# Optimizing a Trainium2 kernel written in Bass

```python
import numpy as np
import jax
import jax.numpy as jnp

def _softmax(x, axis=-1):
    return jax.nn.softmax(x, axis=axis)

def _gelu(x):
    return jax.nn.gelu(x, approximate=True)

def _silu(x):
    return jax.nn.silu(x)

def _sigmoid(x):
    return jax.nn.sigmoid(x)

def _layernorm(x, axis=-1, eps=1e-05):
    m = jnp.mean(x, axis=axis, keepdims=True)
    v = jnp.var(x, axis=axis, keepdims=True)
    return (x - m) / jnp.sqrt(v + eps)

def _scatter_add(tgt, idx, src, axis=0):
    return tgt.at[idx].add(src)

def _segment_sum(src, seg, n):
    return jax.ops.segment_sum(src, seg, n)
kernel_name = 'mk_decoder_preln_d2_seqx_r4_e403c4'

def setup_inputs(seed: int=0):
    np.random.seed(seed)
    _w = jnp.asarray

    def _rec_inputs():
        import jax
        import jax.numpy as jnp
        _rk = jax.random.key(seed)
        x = -0.0002928 + 1 * jax.random.normal(jax.random.fold_in(_rk, 1), (16, 256, 256), jnp.float32)
        _lenS = 256 - jax.random.randint(jax.random.fold_in(_rk, 7), (16,), 0, max(1, 256 // 4) + 1, jnp.int32)
        _lenS2 = 256 - jax.random.randint(jax.random.fold_in(_rk, 8), (16,), 0, max(1, 256 // 4) + 1, jnp.int32)
        _ctx_1024P = jax.random.normal(jax.random.fold_in(_rk, 11), (16, 16, 256), jnp.float32)
        _ctx_1024c = jax.random.dirichlet(jax.random.fold_in(_rk, 511), 0.3 * jnp.ones((16,), jnp.float32), (16, 256))
        _ctx_1024t = jnp.einsum('bsk,bkd->bsd', _ctx_1024c, _ctx_1024P)
        _ctx_1024t = _ctx_1024t * jax.lax.rsqrt(jnp.mean(jnp.square(_ctx_1024t)) + 1e-12) * 0.953939
        ctx_1024 = -1.39393e-06 + 0.999914 * (_ctx_1024t + 0.3 * jax.random.normal(jax.random.fold_in(_rk, 611), (16, 256, 256), jnp.float32))
        return (x, ctx_1024)
    x, ctx_1024 = _rec_inputs()

    def _L0_attn_setup():
        import jax, jax.numpy as jnp
        import numpy as np
        import math
        B, T, C = (8, 512, 256)
        H, D = (16, 64)

        def _l2norm(v, axis=-1, eps=1e-12):
            n = jnp.sqrt(jnp.sum(v * v, axis=axis, keepdims=True))
            return v / jnp.maximum(n, eps)

        def _reference_tuple_inner(x, W_r, b_r, W_k, b_k, W_v, b_v, W_g, b_g, W_o, b_o, decay, eta, time_mix_r, time_mix_k, time_mix_v, time_mix_g, gn_weight, gn_bias):
            Bx, Tx, Cx = x.shape
            Hh = decay.shape[0]
            Dd = Cx // Hh
            x_shift = jnp.concatenate([jnp.zeros_like(x[:, :1]), x[:, :-1]], axis=1)
            x_r = x * time_mix_r + x_shift * (1 - time_mix_r)
            x_k = x * time_mix_k + x_shift * (1 - time_mix_k)
            x_v = x * time_mix_v + x_shift * (1 - time_mix_v)
            x_g = x * time_mix_g + x_shift * (1 - time_mix_g)
            r = jax.nn.sigmoid(x_r @ W_r.T + b_r).reshape(Bx, Tx, Hh, Dd)
            k = (x_k @ W_k.T + b_k).reshape(Bx, Tx, Hh, Dd)
            v = (x_v @ W_v.T + b_v).reshape(Bx, Tx, Hh, Dd)
            g = jax.nn.silu(x_g @ W_g.T + b_g)
            k = _l2norm(k)
            v = _l2norm(v)
            dec = jax.nn.sigmoid(decay)
            et = jax.nn.sigmoid(eta)
            max_norm = math.sqrt(Dd) * 2.0
            rs = jnp.transpose(r, (1, 0, 2, 3))
            ks_ = jnp.transpose(k, (1, 0, 2, 3))
            vs = jnp.transpose(v, (1, 0, 2, 3))

            def step(state, rkv):
                r_t, k_t, v_t = rkv
                pred = jnp.einsum('bhij,bhj->bhi', state, k_t)
                err = pred - v_t
                state = dec * state - et * (err[..., :, None] * k_t[..., None, :])
                n = jnp.maximum(jnp.sqrt(jnp.sum(state * state, axis=(-2, -1), keepdims=True)), 1e-08)
                state = state * jnp.where(n > max_norm, max_norm / n, 1.0)
                wkv = jnp.einsum('bhij,bhj->bhi', state, r_t)
                return (state, wkv)
            state0 = jnp.zeros((Bx, Hh, Dd, Dd), jnp.float32)
            state, wkv = jax.lax.scan(step, state0, (rs, ks_, vs))
            wkv = jnp.transpose(wkv, (1, 0, 2, 3))
            mean = jnp.mean(wkv, axis=(1, 3), keepdims=True)
            var = jnp.mean(jnp.square(wkv - mean), axis=(1, 3), keepdims=True)
            wkv_n = ((wkv - mean) / jnp.sqrt(var + 1e-05)).reshape(Bx, Tx, Cx)
            wkv_n = wkv_n * gn_weight + gn_bias
            out = (wkv_n @ W_o.T + b_o) * g
            last_x = x[:, -1:, :]
            return (out, state, last_x)
        key = jax.random.key(seed)
        ks = jax.random.split(key, 20)
        s = 1.0 / math.sqrt(C)
        inp = {'x': jax.random.normal(ks[0], (B, T, C), dtype=jnp.float32), 'W_r': jax.random.normal(ks[1], (C, C), dtype=jnp.float32) * s, 'b_r': jnp.zeros((C,), jnp.float32), 'W_k': jax.random.normal(ks[2], (C, C), dtype=jnp.float32) * s, 'b_k': jnp.zeros((C,), jnp.float32), 'W_v': jax.random.normal(ks[3], (C, C), dtype=jnp.float32) * s, 'b_v': jnp.zeros((C,), jnp.float32), 'W_g': jax.random.normal(ks[4], (C, C), dtype=jnp.float32) * s, 'b_g': jnp.zeros((C,), jnp.float32), 'W_o': jax.random.normal(ks[5], (C, C), dtype=jnp.float32) * s, 'b_o': jnp.zeros((C,), jnp.float32), 'decay': jax.random.uniform(ks[6], (H, 1, 1), jnp.float32, 2.0, 4.0), 'eta': jax.random.uniform(ks[7], (H, 1, 1), jnp.float32, -3.0, -1.0), 'time_mix_r': jnp.full((1, 1, C), 0.5, jnp.float32), 'time_mix_k': jnp.full((1, 1, C), 0.5, jnp.float32), 'time_mix_v': jnp.full((1, 1, C), 0.5, jnp.float32), 'time_mix_g': jnp.full((1, 1, C), 0.5, jnp.float32), 'gn_weight': jnp.ones((C,), jnp.float32), 'gn_bias': jnp.zeros((C,), jnp.float32)}
        return inp
    _L0_attn_all = _L0_attn_setup()
    _L0_attn_in = {k: v for k, v in _L0_attn_all.items() if k in ('W_r', 'b_r', 'W_k', 'b_k', 'W_v', 'b_v', 'W_g', 'b_g', 'W_o', 'b_o', 'decay', 'eta', 'time_mix_r', 'time_mix_k', 'time_mix_v', 'time_mix_g', 'gn_weight', 'gn_bias')}
    del _L0_attn_all

    def _L0_xattn_setup():
        import jax, jax.numpy as jnp
        import numpy as np
        E_PHI = 256
        E_F = 256
        HID = 256
        N_HEADS = 16
        HEAD_DIM = HID // N_HEADS
        key = jax.random.key(seed)
        ks = jax.random.split(key, 9)
        B, S = (2, 512)
        s = 0.02
        return {'q': jax.random.normal(ks[0], (B, S, E_PHI), jnp.float32), 'k': jax.random.normal(ks[1], (B, S, E_PHI), jnp.float32), 'v': jax.random.normal(ks[2], (B, S, E_F), jnp.float32), 'W_q': jax.random.normal(ks[3], (E_PHI, HID), jnp.float32) * s, 'W_k': jax.random.normal(ks[4], (E_PHI, HID), jnp.float32) * s, 'W_v': jax.random.normal(ks[5], (E_F, HID), jnp.float32) * s, 'b_v': jax.random.normal(ks[6], (HID,), jnp.float32) * s, 'W_o': jax.random.normal(ks[7], (HID, E_F), jnp.float32) * s, 'b_o': jax.random.normal(ks[8], (E_F,), jnp.float32) * s}
    _L0_xattn_all = _L0_xattn_setup()
    _L0_xattn_in = {k: v for k, v in _L0_xattn_all.items() if k in ('W_q', 'W_k', 'W_v', 'b_v', 'W_o', 'b_o')}
    del _L0_xattn_all

    def _L0_ffn_setup():
        import jax, jax.numpy as jnp
        import numpy as np
        B, S, D, F, E, R = (4, 512, 256, 1024, 8, 4)
        key = jax.random.key(seed)
        ks = jax.random.split(key, 8)
        s_in = 1.0 / np.sqrt(D)
        s_ff = 1.0 / np.sqrt(F)
        return {'hidden_states': jax.random.normal(ks[0], (B, S, D), jnp.float32), 'gate_W': jax.random.normal(ks[1], (E, D), jnp.float32) * s_in, 'gate_b': jnp.zeros((E,), jnp.float32), 'wi_W': jax.random.normal(ks[2], (F, D), jnp.float32) * s_in, 'wi_b': jnp.zeros((F,), jnp.float32), 'wo_W': jax.random.normal(ks[3], (D, F), jnp.float32) * s_ff, 'wo_b': jnp.zeros((D,), jnp.float32), 'lora_A': jax.random.normal(ks[4], (E, R, D), jnp.float32) * s_in, 'lora_B': jax.random.normal(ks[5], (E, F, R), jnp.float32) * 0.02}
    _L0_ffn_all = _L0_ffn_setup()
    _L0_ffn_in = {k: v for k, v in _L0_ffn_all.items() if k in ('gate_W', 'gate_b', 'wi_W', 'wi_b', 'wo_W', 'wo_b', 'lora_A', 'lora_B')}
    del _L0_ffn_all

    def _L1_attn_setup():
        import jax, jax.numpy as jnp
        import numpy as np
        DIM = 256
        STATE = 64
        KW = 4
        EXPAND = 2
        INNER = DIM * EXPAND
        BATCH = 2
        SEQ = 512
        EPS = 1e-06

        def _ssm_scan(xc, A_log, B_w, C_w, D_param, dt_w, dt_b):
            A = -jnp.exp(A_log)
            Bx = xc @ B_w.T
            Cx = xc @ C_w.T
            dt = jax.nn.softplus(xc @ dt_w.T + dt_b) + 0.0001

            def step(h, inp):
                dt_t, Bx_t, Cx_t, x_t = inp
                dA = jnp.exp(dt_t[..., None] * A)
                h = dA * h + (dt_t * x_t)[..., None] * Bx_t[:, None, :]
                y = jnp.einsum('bdn,bn->bd', h, Cx_t) + D_param * x_t
                return (h, y)
            h0 = jnp.zeros((xc.shape[0], INNER, STATE), dtype=jnp.float32)
            seq_inputs = tuple((jnp.moveaxis(a, 1, 0) for a in (dt, Bx, Cx, xc)))
            _, ys = jax.lax.scan(step, h0, seq_inputs)
            return jnp.moveaxis(ys, 0, 1)
        key = jax.random.key(seed)
        ks = jax.random.split(key, 8)
        rn = lambda k, shape, scale: jax.random.normal(k, shape, dtype=jnp.float32) * scale
        x = jax.random.normal(ks[0], (BATCH, SEQ, DIM), dtype=jnp.float32)
        in_proj_w = rn(ks[1], (2 * INNER, DIM), DIM ** (-0.5))
        conv_w = rn(ks[2], (INNER, 1, KW), 0.5)
        conv_b = jnp.zeros((INNER,), dtype=jnp.float32)
        A_log = jnp.tile(jnp.log(jnp.arange(1, STATE + 1, dtype=jnp.float32))[None, :], (INNER, 1))
        B_w = rn(ks[3], (STATE, INNER), INNER ** (-0.5))
        C_w = rn(ks[4], (STATE, INNER), INNER ** (-0.5))
        D_param = jnp.ones((INNER,), dtype=jnp.float32)
        dt_w = rn(ks[5], (INNER, INNER), 0.01 * INNER ** (-0.5))
        dt_b = jnp.full((INNER,), -3.0, dtype=jnp.float32)
        out_proj_w = rn(ks[6], (DIM, INNER), INNER ** (-0.5))
        norm_w = jnp.ones((DIM,), dtype=jnp.float32)
        return dict(x=x, in_proj_w=in_proj_w, conv_w=conv_w, conv_b=conv_b, A_log=A_log, B_w=B_w, C_w=C_w, D_param=D_param, dt_w=dt_w, dt_b=dt_b, out_proj_w=out_proj_w, norm_w=norm_w)
    _L1_attn_all = _L1_attn_setup()
    _L1_attn_in = {k: v for k, v in _L1_attn_all.items() if k in ('in_proj_w', 'conv_w', 'conv_b', 'A_log', 'B_w', 'C_w', 'D_param', 'dt_w', 'dt_b', 'out_proj_w', 'norm_w')}
    del _L1_attn_all

    def _L1_xattn_setup():
        import jax, jax.numpy as jnp
        import numpy as np
        D = 256
        H = 16
        DH = D // H
        key = jax.random.key(seed)
        ks = jax.random.split(key, 11)
        B, T = (4, 512)
        s = 0.02
        return {'q': jax.random.normal(ks[0], (B, T, D), jnp.float32), 'k': jax.random.normal(ks[1], (B, T, D), jnp.float32), 'v': jax.random.normal(ks[2], (B, T, D), jnp.float32), 'Wq': jax.random.normal(ks[3], (D, D), jnp.float32) * s, 'b_q': jax.random.normal(ks[4], (D,), jnp.float32) * s, 'Wk': jax.random.normal(ks[5], (D, D), jnp.float32) * s, 'b_k': jax.random.normal(ks[6], (D,), jnp.float32) * s, 'Wv': jax.random.normal(ks[7], (D, D), jnp.float32) * s, 'b_v': jax.random.normal(ks[8], (D,), jnp.float32) * s, 'Wo': jax.random.normal(ks[9], (D, D), jnp.float32) * s, 'b_o': jax.random.normal(ks[10], (D,), jnp.float32) * s}
    _L1_xattn_all = _L1_xattn_setup()
    _L1_xattn_in = {k: v for k, v in _L1_xattn_all.items() if k in ('Wq', 'b_q', 'Wk', 'b_k', 'Wv', 'b_v', 'Wo', 'b_o')}
    del _L1_xattn_all

    def _L1_ffn_setup():
        import jax, jax.numpy as jnp
        import numpy as np
        B, S, H = (2, 256, 256)
        KD, NH, K = (128, 8, 8)
        NE = 16384
        NK = 64
        EPS = 1e-05
        key = jax.random.key(seed)
        ks = jax.random.split(key, 5)
        inputs = jax.random.normal(ks[0], (B, S, H), jnp.float32)
        bn_gamma = jnp.ones((H,), jnp.float32)
        bn_beta = jnp.zeros((H,), jnp.float32)
        w_q = jax.random.normal(ks[1], (2 * NH * KD, H), jnp.float32) * (1.0 / np.sqrt(H))
        keys_p = jax.random.normal(ks[2], (NH, NK, 2, KD), jnp.float32) * 0.02
        lim = float(np.sqrt(6.0 / (NE + H)))
        down = jax.random.uniform(ks[3], (NE, H), jnp.float32, -lim, lim)
        up = jax.random.uniform(ks[4], (NE, H), jnp.float32, -lim, lim)
        return {'inputs': inputs, 'bn_gamma': bn_gamma, 'bn_beta': bn_beta, 'w_q': w_q, 'keys_p': keys_p, 'down': down, 'up': up}
    _L1_ffn_all = _L1_ffn_setup()
    _L1_ffn_in = {k: v for k, v in _L1_ffn_all.items() if k in ('bn_gamma', 'bn_beta', 'w_q', 'keys_p', 'down', 'up')}
    del _L1_ffn_all
    return {'x': x, 'ctx_1024': ctx_1024, 'L0_attn_W_r': _L0_attn_in['W_r'], 'L0_attn_b_r': _L0_attn_in['b_r'], 'L0_attn_W_k': _L0_attn_in['W_k'], 'L0_attn_b_k': _L0_attn_in['b_k'], 'L0_attn_W_v': _L0_attn_in['W_v'], 'L0_attn_b_v': _L0_attn_in['b_v'], 'L0_attn_W_g': _L0_attn_in['W_g'], 'L0_attn_b_g': _L0_attn_in['b_g'], 'L0_attn_W_o': _L0_attn_in['W_o'], 'L0_attn_b_o': _L0_attn_in['b_o'], 'L0_attn_decay': _L0_attn_in['decay'], 'L0_attn_eta': _L0_attn_in['eta'], 'L0_attn_time_mix_r': _L0_attn_in['time_mix_r'], 'L0_attn_time_mix_k': _L0_attn_in['time_mix_k'], 'L0_attn_time_mix_v': _L0_attn_in['time_mix_v'], 'L0_attn_time_mix_g': _L0_attn_in['time_mix_g'], 'L0_attn_gn_weight': _L0_attn_in['gn_weight'], 'L0_attn_gn_bias': _L0_attn_in['gn_bias'], 'L0_xattn_W_q': _L0_xattn_in['W_q'], 'L0_xattn_W_k': _L0_xattn_in['W_k'], 'L0_xattn_W_v': _L0_xattn_in['W_v'], 'L0_xattn_b_v': _L0_xattn_in['b_v'], 'L0_xattn_W_o': _L0_xattn_in['W_o'], 'L0_xattn_b_o': _L0_xattn_in['b_o'], 'L0_ffn_gate_W': _L0_ffn_in['gate_W'], 'L0_ffn_gate_b': _L0_ffn_in['gate_b'], 'L0_ffn_wi_W': _L0_ffn_in['wi_W'], 'L0_ffn_wi_b': _L0_ffn_in['wi_b'], 'L0_ffn_wo_W': _L0_ffn_in['wo_W'], 'L0_ffn_wo_b': _L0_ffn_in['wo_b'], 'L0_ffn_lora_A': _L0_ffn_in['lora_A'], 'L0_ffn_lora_B': _L0_ffn_in['lora_B'], 'L1_attn_in_proj_w': _L1_attn_in['in_proj_w'], 'L1_attn_conv_w': _L1_attn_in['conv_w'], 'L1_attn_conv_b': _L1_attn_in['conv_b'], 'L1_attn_A_log': _L1_attn_in['A_log'], 'L1_attn_B_w': _L1_attn_in['B_w'], 'L1_attn_C_w': _L1_attn_in['C_w'], 'L1_attn_D_param': _L1_attn_in['D_param'], 'L1_attn_dt_w': _L1_attn_in['dt_w'], 'L1_attn_dt_b': _L1_attn_in['dt_b'], 'L1_attn_out_proj_w': _L1_attn_in['out_proj_w'], 'L1_attn_norm_w': _L1_attn_in['norm_w'], 'L1_xattn_Wq': _L1_xattn_in['Wq'], 'L1_xattn_b_q': _L1_xattn_in['b_q'], 'L1_xattn_Wk': _L1_xattn_in['Wk'], 'L1_xattn_b_k': _L1_xattn_in['b_k'], 'L1_xattn_Wv': _L1_xattn_in['Wv'], 'L1_xattn_b_v': _L1_xattn_in['b_v'], 'L1_xattn_Wo': _L1_xattn_in['Wo'], 'L1_xattn_b_o': _L1_xattn_in['b_o'], 'L1_ffn_bn_gamma': _L1_ffn_in['bn_gamma'], 'L1_ffn_bn_beta': _L1_ffn_in['bn_beta'], 'L1_ffn_w_q': _L1_ffn_in['w_q'], 'L1_ffn_keys_p': _L1_ffn_in['keys_p'], 'L1_ffn_down': _L1_ffn_in['down'], 'L1_ffn_up': _L1_ffn_in['up']}

def reference(x, ctx_1024, L0_attn_W_r, L0_attn_b_r, L0_attn_W_k, L0_attn_b_k, L0_attn_W_v, L0_attn_b_v, L0_attn_W_g, L0_attn_b_g, L0_attn_W_o, L0_attn_b_o, L0_attn_decay, L0_attn_eta, L0_attn_time_mix_r, L0_attn_time_mix_k, L0_attn_time_mix_v, L0_attn_time_mix_g, L0_attn_gn_weight, L0_attn_gn_bias, L0_xattn_W_q, L0_xattn_W_k, L0_xattn_W_v, L0_xattn_b_v, L0_xattn_W_o, L0_xattn_b_o, L0_ffn_gate_W, L0_ffn_gate_b, L0_ffn_wi_W, L0_ffn_wi_b, L0_ffn_wo_W, L0_ffn_wo_b, L0_ffn_lora_A, L0_ffn_lora_B, L1_attn_in_proj_w, L1_attn_conv_w, L1_attn_conv_b, L1_attn_A_log, L1_attn_B_w, L1_attn_C_w, L1_attn_D_param, L1_attn_dt_w, L1_attn_dt_b, L1_attn_out_proj_w, L1_attn_norm_w, L1_xattn_Wq, L1_xattn_b_q, L1_xattn_Wk, L1_xattn_b_k, L1_xattn_Wv, L1_xattn_b_v, L1_xattn_Wo, L1_xattn_b_o, L1_ffn_bn_gamma, L1_ffn_bn_beta, L1_ffn_w_q, L1_ffn_keys_p, L1_ffn_down, L1_ffn_up):
    import jax
    import jax.numpy as jnp

    def _L0_attn_ref(x, W_r, b_r, W_k, b_k, W_v, b_v, W_g, b_g, W_o, b_o, decay, eta, time_mix_r, time_mix_k, time_mix_v, time_mix_g, gn_weight, gn_bias):
        import jax, jax.numpy as jnp
        import numpy as np
        import math
        B, T, C = (8, 512, 256)
        H, D = (16, 64)

        def _l2norm(v, axis=-1, eps=1e-12):
            n = jnp.sqrt(jnp.sum(v * v, axis=axis, keepdims=True))
            return v / jnp.maximum(n, eps)

        def _reference_tuple_inner(x, W_r, b_r, W_k, b_k, W_v, b_v, W_g, b_g, W_o, b_o, decay, eta, time_mix_r, time_mix_k, time_mix_v, time_mix_g, gn_weight, gn_bias):
            Bx, Tx, Cx = x.shape
            Hh = decay.shape[0]
            Dd = Cx // Hh
            x_shift = jnp.concatenate([jnp.zeros_like(x[:, :1]), x[:, :-1]], axis=1)
            x_r = x * time_mix_r + x_shift * (1 - time_mix_r)
            x_k = x * time_mix_k + x_shift * (1 - time_mix_k)
            x_v = x * time_mix_v + x_shift * (1 - time_mix_v)
            x_g = x * time_mix_g + x_shift * (1 - time_mix_g)
            r = jax.nn.sigmoid(x_r @ W_r.T + b_r).reshape(Bx, Tx, Hh, Dd)
            k = (x_k @ W_k.T + b_k).reshape(Bx, Tx, Hh, Dd)
            v = (x_v @ W_v.T + b_v).reshape(Bx, Tx, Hh, Dd)
            g = jax.nn.silu(x_g @ W_g.T + b_g)
            k = _l2norm(k)
            v = _l2norm(v)
            dec = jax.nn.sigmoid(decay)
            et = jax.nn.sigmoid(eta)
            max_norm = math.sqrt(Dd) * 2.0
            rs = jnp.transpose(r, (1, 0, 2, 3))
            ks_ = jnp.transpose(k, (1, 0, 2, 3))
            vs = jnp.transpose(v, (1, 0, 2, 3))

            def step(state, rkv):
                r_t, k_t, v_t = rkv
                pred = jnp.einsum('bhij,bhj->bhi', state, k_t)
                err = pred - v_t
                state = dec * state - et * (err[..., :, None] * k_t[..., None, :])
                n = jnp.maximum(jnp.sqrt(jnp.sum(state * state, axis=(-2, -1), keepdims=True)), 1e-08)
                state = state * jnp.where(n > max_norm, max_norm / n, 1.0)
                wkv = jnp.einsum('bhij,bhj->bhi', state, r_t)
                return (state, wkv)
            state0 = jnp.zeros((Bx, Hh, Dd, Dd), jnp.float32)
            state, wkv = jax.lax.scan(step, state0, (rs, ks_, vs))
            wkv = jnp.transpose(wkv, (1, 0, 2, 3))
            mean = jnp.mean(wkv, axis=(1, 3), keepdims=True)
            var = jnp.mean(jnp.square(wkv - mean), axis=(1, 3), keepdims=True)
            wkv_n = ((wkv - mean) / jnp.sqrt(var + 1e-05)).reshape(Bx, Tx, Cx)
            wkv_n = wkv_n * gn_weight + gn_bias
            out = (wkv_n @ W_o.T + b_o) * g
            last_x = x[:, -1:, :]
            return (out, state, last_x)
        return _reference_tuple_inner(x, W_r, b_r, W_k, b_k, W_v, b_v, W_g, b_g, W_o, b_o, decay, eta, time_mix_r, time_mix_k, time_mix_v, time_mix_g, gn_weight, gn_bias)[0]

    def _L0_xattn_ref(q, k, v, W_q, W_k, W_v, b_v, W_o, b_o):
        import jax, jax.numpy as jnp
        import numpy as np
        E_PHI = 256
        E_F = 256
        HID = 256
        N_HEADS = 16
        HEAD_DIM = HID // N_HEADS
        B, S, _ = q.shape
        qh = (q @ W_q).reshape(B, S, N_HEADS, HEAD_DIM)
        kh = (k @ W_k).reshape(B, S, N_HEADS, HEAD_DIM)
        vh = (v @ W_v + b_v).reshape(B, S, N_HEADS, HEAD_DIM)
        scale = 1.0 / jnp.sqrt(jnp.float32(HEAD_DIM))
        scores = jnp.einsum('bihd,bjhd->bhij', qh, kh) * scale
        i = jnp.arange(S)[:, None]
        j = jnp.arange(S)[None, :]
        keep = (j < i) | (i == 0) & (j == 0)
        scores = jnp.where(keep, scores, jnp.float32(-jnp.inf))
        probs = jax.nn.softmax(scores, axis=-1)
        attn = jnp.einsum('bhij,bjhd->bihd', probs, vh).reshape(B, S, HID)
        return attn @ W_o + b_o

    def _L0_ffn_ref(hidden_states, gate_W, gate_b, wi_W, wi_b, wo_W, wo_b, lora_A, lora_B):
        import jax, jax.numpy as jnp
        import numpy as np
        B, S, D, F, E, R = (4, 512, 256, 1024, 8, 4)
        x = hidden_states
        logits = jnp.einsum('bsd,ed->bse', x, gate_W) + gate_b
        top1 = jnp.argmax(jax.nn.softmax(logits, axis=-1), axis=-1)
        base = jnp.einsum('bsd,fd->bsf', x, wi_W) + wi_b
        out = jnp.zeros_like(x)
        for i in range(lora_A.shape[0]):
            lora = jnp.einsum('bsr,fr->bsf', jnp.einsum('bsd,rd->bsr', x, lora_A[i]), lora_B[i])
            inter = jax.nn.relu(base + lora)
            expert_out = jnp.einsum('bsf,df->bsd', inter, wo_W) + wo_b
            mask = (top1 == i).astype(x.dtype)[..., None]
            out = out + mask * expert_out
        return out

    def _L1_attn_ref(x, in_proj_w, conv_w, conv_b, A_log, B_w, C_w, D_param, dt_w, dt_b, out_proj_w, norm_w):
        import jax, jax.numpy as jnp
        import numpy as np
        DIM = 256
        STATE = 64
        KW = 4
        EXPAND = 2
        INNER = DIM * EXPAND
        BATCH = 2
        SEQ = 512
        EPS = 1e-06

        def _ssm_scan(xc, A_log, B_w, C_w, D_param, dt_w, dt_b):
            A = -jnp.exp(A_log)
            Bx = xc @ B_w.T
            Cx = xc @ C_w.T
            dt = jax.nn.softplus(xc @ dt_w.T + dt_b) + 0.0001

            def step(h, inp):
                dt_t, Bx_t, Cx_t, x_t = inp
                dA = jnp.exp(dt_t[..., None] * A)
                h = dA * h + (dt_t * x_t)[..., None] * Bx_t[:, None, :]
                y = jnp.einsum('bdn,bn->bd', h, Cx_t) + D_param * x_t
                return (h, y)
            h0 = jnp.zeros((xc.shape[0], INNER, STATE), dtype=jnp.float32)
            seq_inputs = tuple((jnp.moveaxis(a, 1, 0) for a in (dt, Bx, Cx, xc)))
            _, ys = jax.lax.scan(step, h0, seq_inputs)
            return jnp.moveaxis(ys, 0, 1)
        residual = x
        xn = x * jax.lax.rsqrt(jnp.mean(x * x, axis=-1, keepdims=True) + EPS) * norm_w
        xz = xn @ in_proj_w.T
        xc, z = jnp.split(xz, 2, axis=-1)
        xt = jnp.transpose(xc, (0, 2, 1))
        xt = jax.lax.conv_general_dilated(xt, conv_w, window_strides=(1,), padding=[(KW - 1, 0)], feature_group_count=INNER, dimension_numbers=('NCH', 'OIH', 'NCH'))
        xt = xt + conv_b[None, :, None]
        xc = jax.nn.silu(jnp.transpose(xt, (0, 2, 1)))
        y = _ssm_scan(xc, A_log, B_w, C_w, D_param, dt_w, dt_b)
        y = y * jax.nn.silu(z)
        return y @ out_proj_w.T + residual

    def _L1_xattn_ref(q, k, v, Wq, b_q, Wk, b_k, Wv, b_v, Wo, b_o):
        import jax, jax.numpy as jnp
        import numpy as np
        D = 256
        H = 16
        DH = D // H
        B, Tq, _ = q.shape
        Tk = k.shape[1]
        Q = (q @ Wq + b_q).reshape(B, Tq, H, DH)
        K = (k @ Wk + b_k).reshape(B, Tk, H, DH)
        V = (v @ Wv + b_v).reshape(B, Tk, H, DH)
        scores = jnp.einsum('bthd,bshd->bhts', Q, K) / jnp.sqrt(jnp.float32(DH))
        P = jax.nn.softmax(scores, axis=-1)
        out = jnp.einsum('bhts,bshd->bthd', P, V).reshape(B, Tq, D)
        return out @ Wo + b_o

    def _L1_ffn_ref(inputs, bn_gamma, bn_beta, w_q, keys_p, down, up):
        import jax, jax.numpy as jnp
        import numpy as np
        B, S, H = (2, 256, 256)
        KD, NH, K = (128, 8, 8)
        NE = 16384
        NK = 64
        EPS = 1e-05
        b, s, d = inputs.shape
        x = inputs.reshape(b * s, d)
        mean = x.mean(axis=0)
        var = x.var(axis=0)
        xn = (x - mean) * jax.lax.rsqrt(var + EPS) * bn_gamma + bn_beta
        xn = xn.reshape(b, s, d)
        q = (xn @ w_q.T).reshape(b, s, 2, NH, KD).transpose(2, 0, 1, 3, 4)
        sim = jnp.einsum('pbnhd,hkpd->pbnhk', q, keys_p)
        scores, idx = jax.lax.top_k(sim, K)
        all_scores = (scores[0][..., :, None] + scores[1][..., None, :]).reshape(b, s, NH, K * K)
        all_idx = (idx[0][..., :, None] * NK + idx[1][..., None, :]).reshape(b, s, NH, K * K)
        sc, pk = jax.lax.top_k(all_scores, K)
        indices = jnp.take_along_axis(all_idx, pk, axis=-1)
        wd = down[indices]
        hmid = jnp.einsum('bnd,bnhkd->bnhk', inputs, wd)
        hmid = jax.nn.sigmoid(sc) * jax.nn.gelu(hmid, approximate=False)
        wu = up[indices]
        return jnp.einsum('bnhk,bnhkd->bnd', hmid, wu)
    x = x + _L0_attn_ref(_layernorm(x, axis=-1), L0_attn_W_r, L0_attn_b_r, L0_attn_W_k, L0_attn_b_k, L0_attn_W_v, L0_attn_b_v, L0_attn_W_g, L0_attn_b_g, L0_attn_W_o, L0_attn_b_o, L0_attn_decay, L0_attn_eta, L0_attn_time_mix_r, L0_attn_time_mix_k, L0_attn_time_mix_v, L0_attn_time_mix_g, L0_attn_gn_weight, L0_attn_gn_bias)
    x = x + _L0_xattn_ref(_layernorm(x, axis=-1), ctx_1024, ctx_1024, L0_xattn_W_q, L0_xattn_W_k, L0_xattn_W_v, L0_xattn_b_v, L0_xattn_W_o, L0_xattn_b_o)
    x = x + _L0_ffn_ref(_layernorm(x, axis=-1), L0_ffn_gate_W, L0_ffn_gate_b, L0_ffn_wi_W, L0_ffn_wi_b, L0_ffn_wo_W, L0_ffn_wo_b, L0_ffn_lora_A, L0_ffn_lora_B)
    x = x + _L1_attn_ref(_layernorm(x, axis=-1), L1_attn_in_proj_w, L1_attn_conv_w, L1_attn_conv_b, L1_attn_A_log, L1_attn_B_w, L1_attn_C_w, L1_attn_D_param, L1_attn_dt_w, L1_attn_dt_b, L1_attn_out_proj_w, L1_attn_norm_w)
    x = x + _L1_xattn_ref(_layernorm(x, axis=-1), ctx_1024, ctx_1024, L1_xattn_Wq, L1_xattn_b_q, L1_xattn_Wk, L1_xattn_b_k, L1_xattn_Wv, L1_xattn_b_v, L1_xattn_Wo, L1_xattn_b_o)
    x = x + _L1_ffn_ref(_layernorm(x, axis=-1), L1_ffn_bn_gamma, L1_ffn_bn_beta, L1_ffn_w_q, L1_ffn_keys_p, L1_ffn_down, L1_ffn_up)
    return x

_drawn_inputs = setup_inputs


def setup_inputs(seed=0):
    import zlib

    import numpy as np

    out = dict(_drawn_inputs(seed))
    spreads = {'L0_attn_b_r': (0.0, 0.464),
     'L0_attn_b_k': (0.0, 0.1),
     'L0_attn_b_v': (0.0, 0.1),
     'L0_attn_b_g': (0.0, 0.1),
     'L0_attn_b_o': (0.0, 0.1),
     'L0_attn_time_mix_r': (0.5, 0.6),
     'L0_attn_time_mix_k': (0.5, 0.2),
     'L0_attn_time_mix_v': (0.5, 0.2),
     'L0_attn_time_mix_g': (0.5, 0.2),
     'L0_attn_gn_weight': (1.0, 0.2),
     'L0_attn_gn_bias': (0.0, 0.1),
     'L0_ffn_gate_b': (0.0, 0.8),
     'L0_ffn_wi_b': (0.0, 0.1),
     'L0_ffn_wo_b': (0.0, 0.1),
     'L1_attn_conv_b': (0.0, 0.423),
     'L1_attn_D_param': (1.0, 0.2),
     'L1_attn_dt_b': (-3.0, 0.6),
     'L1_attn_norm_w': (1.0, 0.2),
     'L1_ffn_bn_gamma': (1.0, 0.6),
     'L1_ffn_bn_beta': (0.0, 0.8)}
    factors = {'L0_xattn_W_q': 8.0,
     'L0_xattn_W_k': 8.0,
     'L0_xattn_b_v': 8.0,
     'L0_xattn_b_o': 3.262,
     'L0_ffn_gate_W': 2.788,
     'L1_attn_dt_w': 8.0,
     'L1_xattn_Wq': 8.0,
     'L1_xattn_b_q': 8.0,
     'L1_xattn_Wk': 8.0,
     'L1_xattn_b_k': 8.0,
     'L1_xattn_b_v': 8.0,
     'L1_xattn_b_o': 6.452,
     'L1_ffn_w_q': 8.0,
     'L1_ffn_keys_p': 8.0,
     'L1_ffn_down': 8.0,
     'L1_ffn_up': 8.0}
    for name, (base, spread) in spreads.items():
        noise = np.random.default_rng([zlib.crc32(name.encode()), seed]).standard_normal(out[name].shape)
        drawn = base * np.exp(spread * noise) if base else spread * noise
        out[name] = jnp.asarray(drawn.astype(out[name].dtype))
    for name, factor in factors.items():
        out[name] = (out[name] * factor).astype(out[name].dtype)
    return out
```

```python
import math
from contextlib import ExitStack

import numpy as np
import concourse.bass as bass
from concourse import mybir

ALU = mybir.AluOpType
ACT = mybir.ActivationFunctionType
AX = mybir.AxisListType
F32 = mybir.dt.float32
BF16 = mybir.dt.bfloat16
U32 = mybir.dt.uint32

P = 128
B, T, C = 16, 256, 256
NT = T // P
KC = C // P
H, D = 16, 16
E, R, F = 8, 4, 1024
INNER, N = 512, 64
IB = INNER // P
KW = 4
NH, NK, TK, KD = 8, 64, 8, 128
NEG = -1.0e30


def rep(ap, axis, n):
    a = ap.unsqueeze(axis)
    shape = list(a.shape)
    shape[axis] = n
    return a.broadcast_to(shape)


class Lane:
    STEP = 1

    def __init__(self, eng, sem):
        self.eng, self.sem, self.count, self.seen = eng, sem, 0, {}

    def __call__(self, *marks):
        for m in marks:
            if m is not None and self.seen.get(m[0].name, 0) < m[1]:
                self.eng.wait_ge(m[0], m[1])
                self.seen[m[0].name] = m[1]
        return self

    def done(self, ins):
        ins.then_inc(self.sem, self.STEP)
        self.count += self.STEP
        return (self.sem, self.count)

    @property
    def last(self):
        return (self.sem, self.count) if self.count else None


class Queue(Lane):
    STEP = 16

    def __init__(self, lane, sem):
        self.lane, self.sem, self.count = lane, sem, 0

    def __call__(self, *marks):
        self.lane(*marks)
        return self


class Core:

    def __init__(self, nc, ctx):
        self.nc, self.ctx = nc, ctx
        sem = lambda n: ctx.enter_context(nc.semaphore(n))
        self.v = Lane(nc.vector, sem("vector_done"))
        self.s = Lane(nc.scalar, sem("scalar_done"))
        self.pe = Lane(nc.tensor, sem("tensor_done"))
        self.g = Lane(nc.gpsimd, sem("gpsimd_done"))
        self.sp = Lane(nc.sync, sem("sync_done"))
        self.queues = [Queue(self.sp, sem(f"dma_done{n}")) for n in range(8)]
        self.bank = [ctx.enter_context(nc.psum_tensor(f"bank{n}", [P, 512], F32)) for n in range(8)]
        self.drained = {}

    def fence(self):
        lanes = [self.v, self.s, self.pe, self.g, self.sp]
        for lane in lanes:
            lane(lane.last)
        self.sp(*[q.last for q in self.queues])
        numbers = sorted(x.sem.num for x in lanes + self.queues)
        self.nc.all_engine_barrier(sems_to_clear=range(numbers[0], numbers[-1] + 1))
        for x in lanes:
            x.count, x.seen = 0, {}
        for q in self.queues:
            q.count = 0
        self.drained = {}

    def sbuf(self, scope, name, shape, dt=F32):
        return scope.enter_context(self.nc.sbuf_tensor(name, shape, dt))


def constants(k):
    nc, g, v = k.nc, k.g, k.v
    k.ident = k.sbuf(k.ctx, "ident", [P, P])
    k.identb = k.sbuf(k.ctx, "identb", [P, P], BF16)
    k.iota64 = k.sbuf(k.ctx, "iota64", [P, 64])
    m = g().done(nc.gpsimd.memset(k.ident[:, :], 0.0))
    m = g(m).done(nc.gpsimd.affine_select(out=k.ident[:, :], in_=k.ident[:, :], compare_op=ALU.not_equal,
                                          fill=1.0, base=0, pattern=[[-1, P]], channel_multiplier=1))
    v(m).done(nc.vector.tensor_copy(k.identb[:, :], k.ident[:, :]))
    g().done(nc.gpsimd.iota(k.iota64[:, :], [[1, 64]], base=0, channel_multiplier=0,
                            allow_small_or_imprecise_dtypes=True))
    k.fence()


def norm_scratch(k, scope, tag):
    k.ln_stats = k.sbuf(scope, tag + "_ln_stats", [P, NT, 6])
    k.ln_mv = k.sbuf(scope, tag + "_ln_mv", [P, NT, 2])


def layer_norm(k, x, h, ready, eps=1e-5, tiles=NT):
    V, v, s = k.nc.vector, k.v, k.s
    st, mv = k.ln_stats, k.ln_mv
    for t in range(tiles):
        m = v(ready).done(V.bn_stats(st[:, t, :], x[:, t, :]))
    for t in range(tiles):
        m = v(m).done(V.bn_aggr(mv[:, t, :], st[:, t, :]))
    m = v(v.last).done(V.tensor_scalar(mv[:, 0:tiles, 1:2], mv[:, 0:tiles, 1:2], eps, None, ALU.add))
    m = s(m).done(k.nc.scalar.activation(mv[:, 0:tiles, 1:2], mv[:, 0:tiles, 1:2], ACT.Sqrt))
    m = v(m).done(V.reciprocal(mv[:, 0:tiles, 1:2], mv[:, 0:tiles, 1:2]))
    for t in range(tiles):
        r = v(m).done(V.tensor_scalar(h[:, t, :], x[:, t, :], mv[:, t, 0:1], mv[:, t, 1:2],
                                      ALU.subtract, ALU.mult))
    return r


def turn(k, src, bank, ready, tiles=NT, blocks=KC):
    k.pe(ready, k.drained.get(bank))
    for kt in range(blocks):
        for t in range(tiles):
            o = (kt * tiles + t) * P
            m = k.pe.done(k.nc.tensor.transpose(k.bank[bank][:, o:o + P], src[:, t, kt * P:(kt + 1) * P],
                                                k.ident[:, :]))
    return m


def evacuated(k, bank, mark):
    k.drained[bank] = mark
    return mark


def project(k, bank, lhsT, rhs, ready, col=0, stop=True):
    n = rhs[0].shape[-1]
    k.pe(ready, k.drained.get(bank))
    for i, (a, b) in enumerate(zip(lhsT, rhs)):
        m = k.pe.done(k.nc.tensor.matmul(k.bank[bank][0:a.shape[-1], col:col + n], a, b,
                                         start=(i == 0), stop=stop and i == len(rhs) - 1))
    return m


def load_weight(k, tile, dram):
    return k.queues[0]().done(k.nc.sync.dma_start(tile, dram))


def row_to_all(dram, n):
    return dram.unsqueeze(0).broadcast_to([n, dram.shape[0]])


def mixer_inputs(k, io, dr):
    nc, v, s, pe = k.nc, k.v, k.s, k.pe
    V, A = nc.vector, nc.scalar
    with ExitStack() as scope:
        sb = lambda n, sh, dt=F32: k.sbuf(scope, "mi_" + n, sh, dt)
        norm_scratch(k, scope, "mi")
        w = sb("w", [P, 4, KC, C])
        bias = sb("bias", [P, 4, C])
        mixw = sb("mixw", [P, 4, KC])
        unmix = sb("unmix", [P, 4, KC])
        x, h = sb("x", [P, NT, C]), sb("h", [P, NT, C])
        hT = sb("hT", [P, KC, T + 1])
        tmp, mix = sb("tmp", [P, 4, KC, T]), sb("mix", [P, 4, KC, T])
        out = sb("out", [P, 4, NT, C])
        sq, n2 = sb("sq", [P, 2, NT * C]), sb("n2", [P, 2, NT * H])
        res = sb("res", [P, 4, NT, C])
        for i, c in enumerate("rkvg"):
            load_weight(k, w[:, i, :, :], io[f"w_{c}"].rearrange("(k p) n -> p k n", p=P))
            load_weight(k, bias[:, i, :], row_to_all(io[f"L0_attn_b_{c}"], P))
            m = load_weight(k, mixw[:, i, :], io[f"time_mix_{c}"].rearrange("(k p) -> p k", p=P))
        v().done(V.memset(hT[:, :, 0:1], 0.0))
        v(m).done(V.tensor_scalar(unmix[:, :, :], mixw[:, :, :], -1.0, 1.0, ALU.mult, ALU.add))
        k.fence()
        with nc.Fori(0, B) as b:
            m = k.queues[0]().done(nc.sync.dma_start(x[:, :, :], io["x"][b].rearrange("(t p) c -> p t c", p=P)))
            m = layer_norm(k, x, h, m)
            m = turn(k, h, 0, m)
            m = evacuated(k, 0, v(m).done(V.tensor_copy(
                hT[:, :, 1:T + 1], k.bank[0][:, :].rearrange("p (k t) -> p k t", k=KC))))
            for i in range(4):
                for kt in range(KC):
                    a = v(m).done(V.tensor_scalar(tmp[:, i, kt, :], hT[:, kt, 0:T], unmix[:, i, kt:kt + 1],
                                                  None, ALU.mult))
                for kt in range(KC):
                    a = v(a).done(V.scalar_tensor_tensor(mix[:, i, kt, :], hT[:, kt, 1:T + 1],
                                                         mixw[:, i, kt:kt + 1], tmp[:, i, kt, :],
                                                         ALU.mult, ALU.add))
                for t in range(NT):
                    p = project(k, 1 + i, [mix[:, i, kt, t * P:(t + 1) * P] for kt in range(KC)],
                                [w[:, i, kt, :] for kt in range(KC)], a, col=t * C)
                r = evacuated(k, 1 + i, v(p).done(V.tensor_tensor(
                    out[:, i, :, :], k.bank[1 + i][:, :].rearrange("p (t c) -> p t c", t=NT),
                    rep(bias[:, i, :], 1, NT), ALU.add)))
                if i == 0:
                    r_act = s(r).done(A.activation(res[:, 0, :, :], out[:, 0, :, :], ACT.Sigmoid))
            g_act = s(r).done(A.activation(res[:, 3, :, :], out[:, 3, :, :], ACT.Silu))
            kv = out[:, 1:3, :, :].rearrange("p a t c -> p (a t c)")
            sqf = sq[:, :, :].rearrange("p a n -> p (a n)")
            n2f = n2[:, :, :].rearrange("p a n -> p (a n)")
            a = v(r).done(V.tensor_tensor(sqf, kv, kv, ALU.mult))
            a = v(a).done(V.tensor_reduce(n2f, sqf.rearrange("p (n d) -> p n d", d=D), AX.X, ALU.add))
            a = v(a).done(V.tensor_scalar(n2f, n2f, 1e-24, None, ALU.max))
            a = s(a).done(A.activation(n2f, n2f, ACT.Sqrt))
            a = v(a).done(V.reciprocal(n2f, n2f))
            a = v(a).done(V.tensor_tensor(
                res[:, 1:3, :, :].rearrange("p a t c -> p (a t c)").rearrange("p (n d) -> p n d", d=D),
                kv.rearrange("p (n d) -> p n d", d=D), rep(n2f, 2, D), ALU.mult))
            for i, c in enumerate("rkvg"):
                k.queues[1](a, r_act, g_act).done(nc.sync.dma_start(
                    dr[c][b].rearrange("(t p) c -> p t c", p=P), res[:, i, :, :]))
            k.fence()


def mixer_scan(k, io, dr):
    nc, v, s = k.nc, k.v, k.s
    V, A = nc.vector, nc.scalar
    HP = H // 2
    max_norm = math.sqrt(D) * 2.0
    UN = 16
    with ExitStack() as scope:
        sb = lambda n, sh, dt=F32: k.sbuf(scope, "ms_" + n, sh, dt)
        KR = sb("KR", [P, T + 1, 2, 2, D])
        VV = sb("VV", [P, T, 2, D])
        PR = sb("PR", [P, T + 1, 2, 2 * D])
        FF = sb("FF", [P, T + 1, 2])
        CO = sb("CO", [P, T, 2, 2])
        S = sb("S", [P, 2, D, D])
        prod, outer = sb("prod", [P, 2, 2, D, D]), sb("outer", [P, 2, D, D])
        pe_, ee = sb("prederr", [P, 2, 2 * D]), sb("ee", [P, 2 * D])
        Q, terms = sb("Q", [P, 2, 2 * D]), sb("terms", [P, 3, 2])
        R4, N2 = sb("R4", [P, 4]), sb("N2", [P, 2])
        root, inv, fdec = sb("root", [P, 2]), sb("inv", [P, 2]), sb("fdec", [P, 2])
        dec, et, et32, dec2 = sb("dec", [P, 2]), sb("et", [P, 2]), sb("et32", [P, 2, D]), sb("dec2", [P, 2])
        cst, one32 = sb("cst", [P, 2, 2]), sb("one32", [P, 2, D])
        stat = sb("stat", [P, 4, 2])
        v().done(V.memset(KR[:, 0, 1, :, :], 0.0))
        v().done(V.memset(KR[:, T, 0, :, :], 0.0))
        v().done(V.memset(S[:, :, :, :], 0.0))
        v().done(V.memset(FF[:, 0, :], 1.0))
        v().done(V.memset(N2[:, :], 0.0))
        z = v().done(V.memset(one32[:, :, :], 1.0))
        with nc.allow_non_contiguous_dma("heads of a sequence go to partitions"):
            for b in range(B):
                ps = slice(b * HP, (b + 1) * HP)
                k.queues[0]().done(nc.sync.dma_start(KR[ps, 0:T, 0, :, :].rearrange("h t e d -> h t (e d)"), dr["k"][b].rearrange("t (h x) -> h t x", h=HP)))
                k.queues[0]().done(nc.sync.dma_start(KR[ps, 1:T + 1, 1, :, :].rearrange("h t e d -> h t (e d)"), dr["r"][b].rearrange("t (h x) -> h t x", h=HP)))
                k.queues[0]().done(nc.sync.dma_start(VV[ps, :, :, :].rearrange("h t e d -> h t (e d)"), dr["v"][b].rearrange("t (h x) -> h t x", h=HP)))
                k.queues[0]().done(nc.sync.dma_start(dec[ps, :], io["L0_attn_decay"].rearrange("(h e) a b -> h (e a b)", e=2)))
                m = k.queues[0]().done(nc.sync.dma_start(et[ps, :], io["L0_attn_eta"].rearrange("(h e) a b -> h (e a b)", e=2)))
        a = s(m).done(A.activation(dec[:, :], dec[:, :], ACT.Sigmoid))
        a = s().done(A.activation(et[:, :], et[:, :], ACT.Sigmoid))
        b1 = v(a, z).done(V.tensor_tensor(et32[:, :, :], one32[:, :, :], rep(et[:, :], 2, D), ALU.mult))
        c1 = v().done(V.tensor_tensor(dec2[:, :], dec[:, :], dec[:, :], ALU.mult))
        c2 = v().done(V.tensor_tensor(cst[:, 0, :], dec[:, :], et[:, :], ALU.mult))
        c2 = v(c2).done(V.tensor_scalar(cst[:, 0, :], cst[:, 0, :], -2.0, None, ALU.mult))
        c3 = v().done(V.tensor_tensor(cst[:, 1, :], et[:, :], et[:, :], ALU.mult))
        kk = PR[:, 0:T, 0, :].rearrange("p t (e d) -> p t e d", e=2)
        a = v(m).done(V.tensor_tensor(kk, KR[:, 0:T, 0, :, :], KR[:, 0:T, 0, :, :], ALU.mult))
        a = v(a).done(V.tensor_reduce(CO[:, :, 1, :], kk, AX.X, ALU.add))
        a = v(a, c3).done(V.tensor_tensor(CO[:, :, 1, :], CO[:, :, 1, :], rep(cst[:, 1, :], 1, T), ALU.mult))
        a = v().done(V.memset(CO[:, :, 0, :], 1.0))
        a = v(a).done(V.tensor_tensor(CO[:, :, 0, :], CO[:, :, 0, :], rep(cst[:, 0, :], 1, T), ALU.mult))
        k.fence()
        flat = lambda ap: ap.rearrange("p e i j -> p (e i j)")
        with nc.Fori(0, T // UN) as it:
            state, f_ready, n_ready = None, None, None
            for u in range(UN):
                t = it * UN + u
                kr = KR[:, t, :, :, :]
                for a_ in range(2):
                    m = v(state).done(V.tensor_tensor(prod[:, a_, :, :, :], S[:, :, :, :],
                                                      rep(kr[:, a_, :, :], 2, D), ALU.mult))
                m = v(m).done(V.tensor_reduce(PR[:, t, :, :], prod[:, :, :, :, :].rearrange(
                    "p a e i j -> p (a e i) j"), AX.X, ALU.add))
                if f_ready is not None:
                    r = v(f_ready).done(V.reciprocal(inv[:, :], root[:, :]))
                    f_ready = v(r).done(V.tensor_scalar(FF[:, t, :], inv[:, :], max_norm, 1.0, ALU.mult, ALU.min))
                fd = v(f_ready).done(V.tensor_tensor(fdec[:, :], FF[:, t, :], dec[:, :], ALU.mult))
                tn = v(n_ready).done(V.tensor_scalar(terms[:, 2, :], N2[:, :], max_norm * max_norm, None, ALU.min))
                tn = v(tn).done(V.tensor_tensor(terms[:, 2, :], terms[:, 2, :], dec2[:, :], ALU.mult))
                m = v(m, f_ready).done(V.tensor_tensor(
                    pe_[:, 0, :].rearrange("p (e i) -> p e i", e=2),
                    PR[:, t, 0, :].rearrange("p (e i) -> p e i", e=2), rep(FF[:, t, :], 2, D), ALU.mult))
                m = v(m).done(V.tensor_tensor(pe_[:, 1, :], pe_[:, 0, :],
                                              VV[:, t, :, :].rearrange("p e i -> p (e i)"), ALU.subtract))
                e_ = v(m).done(V.tensor_tensor(ee[:, :], pe_[:, 1, :], et32[:, :, :].rearrange("p e i -> p (e i)"), ALU.mult))
                q = v(m).done(V.tensor_tensor(Q[:, :, :], pe_[:, :, :], rep(pe_[:, 1, :], 1, 2), ALU.mult))
                o = v(e_).done(V.tensor_tensor(
                    outer[:, :, :, :], rep(ee[:, :].rearrange("p (e i) -> p e i", e=2), 3, D),
                    rep(kr[:, 0, :, :], 2, D), ALU.mult))
                q = v(q).done(V.tensor_reduce(R4[:, :], Q[:, :, :].rearrange("p a (e i) -> p (a e) i", e=2), AX.X, ALU.add))
                for e in range(2):
                    state = v(o, fd).done(V.scalar_tensor_tensor(
                        S[:, e, :, :].rearrange("p i j -> p (i j)"), S[:, e, :, :].rearrange("p i j -> p (i j)"),
                        fdec[:, e:e + 1], outer[:, e, :, :].rearrange("p i j -> p (i j)"), ALU.mult, ALU.subtract))
                    if e == 0:
                        q = v(q).done(V.tensor_tensor(terms[:, 0:2, :].rearrange("p a e -> p (a e)"), R4[:, :],
                                                      CO[:, t, :, :].rearrange("p a e -> p (a e)"), ALU.mult))
                n_ready = v(q, tn).done(V.tensor_reduce(N2[:, :], terms[:, :, :].rearrange("p a e -> p e a"), AX.X, ALU.add))
                q = v(n_ready).done(V.tensor_scalar(inv[:, :], N2[:, :], 1e-16, None, ALU.max))
                f_ready = s(q).done(A.activation(root[:, :], inv[:, :], ACT.Sqrt))
            r = v(f_ready).done(V.reciprocal(inv[:, :], root[:, :]))
            v(r).done(V.tensor_scalar(FF[:, it * UN + UN, :], inv[:, :], max_norm, 1.0, ALU.mult, ALU.min))
            k.fence()
        m = v().done(V.tensor_tensor(prod[:, 0, :, :, :], S[:, :, :, :], rep(KR[:, T, 1, :, :], 2, D), ALU.mult))
        m = v(m).done(V.tensor_reduce(PR[:, T, 1, :], prod[:, 0, :, :, :].rearrange("p e i j -> p (e i) j"), AX.X, ALU.add))
        m = v(m).done(V.tensor_tensor(VV[:, :, :, :], PR[:, 1:T + 1, 1, :].rearrange("p t (e i) -> p t e i", e=2),
                                      rep(FF[:, 1:T + 1, :], 3, D), ALU.mult))
        sqr = KR[:, 0:T, 0, :, :]
        by_head = lambda ap: ap.rearrange("p t e i -> p e t i")
        m = v(m).done(V.tensor_reduce(stat[:, 0, :], by_head(VV[:, :, :, :]), AX.XY, ALU.add))
        m = v(m).done(V.tensor_scalar(stat[:, 1, :], stat[:, 0, :], 1.0 / (T * D), None, ALU.mult))
        mean_all = rep(stat[:, 1, :], 1, T)
        m = v(m).done(V.tensor_tensor(VV[:, :, :, :], VV[:, :, :, :], rep(mean_all, 3, D), ALU.subtract))
        m = v(m).done(V.tensor_tensor(sqr, VV[:, :, :, :], VV[:, :, :, :], ALU.mult))
        m = v(m).done(V.tensor_reduce(stat[:, 2, :], by_head(sqr), AX.XY, ALU.add))
        m = v(m).done(V.tensor_scalar(stat[:, 2, :], stat[:, 2, :], 1.0 / (T * D), 1e-5, ALU.mult, ALU.add))
        m = s(m).done(A.activation(stat[:, 3, :], stat[:, 2, :], ACT.Sqrt))
        m = v(m).done(V.reciprocal(stat[:, 3, :], stat[:, 3, :]))
        m = v(m).done(V.tensor_tensor(VV[:, :, :, :], VV[:, :, :, :], rep(rep(stat[:, 3, :], 1, T), 3, D), ALU.mult))
        with nc.allow_non_contiguous_dma("heads of a sequence come from partitions"):
            for b in range(B):
                k.queues[1](m).done(nc.sync.dma_start(dr["wkv"][b].rearrange("t (h x) -> h t x", h=HP),
                                                      VV[b * HP:(b + 1) * HP, :, :, :].rearrange("h t e d -> h t (e d)")))
        k.fence()


class Attention:

    def __init__(self, k, io, scope, tag, causal, biased):
        nc, self.k, self.causal = k.nc, k, causal
        sb = lambda n, sh, dt=F32: k.sbuf(scope, "at_" + tag + n, sh, dt)
        self.w = {c: sb("w" + c, [P, KC, C]) for c in "qkvo"}
        self.bq, self.bk = sb("bq", [P, KC]), sb("bk", [P, KC])
        self.bv, self.bo = sb("bv", [P, C]), sb("bo", [P, C])
        self.qT = sb("qT", [P, KC, T])
        self.kT = sb("kT", [P, H, T])
        self.own = sb("own", [P, H // KC])
        self.bko = sb("bko", [P, H])
        self.va = sb("va", [P, NT, H, D + 1])
        self.nmax = sb("nmax", [P, NT, P])
        self.nmaxT = sb("nmaxT", [P, T], BF16)
        self.pT = sb("pT", [P, NT, H, T])
        self.rden = sb("rden", [P, NT, H])
        self.att = sb("att", [P, NT, C])
        self.attT = sb("attT", [P, KC, T])
        g, v = k.g, k.v
        g().done(nc.gpsimd.memset(self.va[:, :, :, :], 1.0))
        g().done(nc.gpsimd.memset(self.nmax[:, :, :], 0.0))
        v().done(nc.vector.memset(self.bq[:, :], 0.0))
        z = v().done(nc.vector.memset(self.bk[:, :], 0.0))
        own = v().done(nc.vector.tensor_reduce(self.own[:, :], k.ident[:, :].rearrange("p (h d) -> p h d", d=D), AX.X, ALU.add))
        for c in "qkvo":
            load_weight(k, self.w[c][:, :, :], io[tag + "w" + c].rearrange("(k p) n -> p k n", p=P))
        if biased:
            k.queues[5](z).done(nc.sync.dma_start(self.bq[:, :], io[tag + "bq"].rearrange("(k p) -> p k", p=P)))
            z = k.queues[5](z).done(nc.sync.dma_start(self.bk[:, :], io[tag + "bk"].rearrange("(k p) -> p k", p=P)))
        for kt in range(KC):
            v(z, own).done(nc.vector.tensor_scalar(self.bko[:, kt * 8:kt * 8 + 8], self.own[:, :], self.bk[:, kt:kt + 1],
                                                   None, ALU.mult))
        load_weight(k, self.bv[:, :], row_to_all(io[tag + "bv"], P))
        load_weight(k, self.bo[:, :], row_to_all(io[tag + "bo"], P))
        if causal:
            self.mask, self.maskT = sb("mask", [P, NT, T], BF16), sb("maskT", [P, NT, T], BF16)
            m1 = g().done(nc.gpsimd.memset(self.mask[:, :, :], 0.0))
            m2 = g().done(nc.gpsimd.memset(self.maskT[:, :, :], 0.0))
            for t in range(NT):
                g(m1).done(nc.gpsimd.affine_select(out=self.mask[:, t, :], in_=self.mask[:, t, :], compare_op=ALU.is_gt,
                                                   fill=NEG, base=t * P, pattern=[[-1, T]], channel_multiplier=1))
                m = g(m2).done(nc.gpsimd.affine_select(out=self.maskT[:, t, :], in_=self.maskT[:, t, :], compare_op=ALU.is_gt,
                                                       fill=NEG, base=-t * P, pattern=[[1, T]], channel_multiplier=-1))
            v(m).done(nc.vector.memset(self.mask[0:1, 0, 0:1], 0.0))
            v(m).done(nc.vector.memset(self.maskT[0:1, 0, 0:1], 0.0))

    def run(self, hT, cT, ready):
        k, nc = self.k, self.k.nc
        v, s, pe, V, A = k.v, k.s, k.pe, k.nc.vector, k.nc.scalar
        for kt in range(KC):
            for i, (c, src) in enumerate((("q", hT), ("k", cT))):
                m = project(k, 6 + i, [self.w[c][:, j, kt * P:(kt + 1) * P] for j in range(KC)],
                            [src[:, j, :] for j in range(KC)], ready, col=kt * T)
        qm = evacuated(k, 6, v(m).done(V.tensor_tensor(self.qT[:, :, :], k.bank[6][:, :].rearrange("p (k t) -> p k t", k=KC),
                                                       rep(self.bq[:, :], 2, T), ALU.add)))
        for h_ in range(H):
            km = s(m).done(A.activation(self.kT[:, h_, :], k.bank[7][:, (h_ // 8) * T:(h_ // 8 + 1) * T], ACT.Identity,
                                        scale=self.own[:, h_ % 8:h_ % 8 + 1], bias=self.bko[:, h_:h_ + 1]))
        evacuated(k, 7, km)
        for t in range(NT):
            m = project(k, 4, [cT[:, kt, t * P:(t + 1) * P] for kt in range(KC)],
                        [self.w["v"][:, kt, :] for kt in range(KC)], ready, col=t * C)
        for t in range(NT):
            va = v(m).done(V.tensor_tensor(
                self.va[:, t, :, 0:D], k.bank[4][:, t * C:(t + 1) * C].rearrange("p (h d) -> p h d", h=H),
                self.bv[:, :].rearrange("p (h d) -> p h d", h=H), ALU.add))
        evacuated(k, 4, va)

        def scores(bank, c, tile, keys_down, more):
            pe(qm, km, k.drained.get(bank))
            for n in range(2):
                q, kk = self.qT[:, (c + n) // 8, :], self.kT[:, c + n, :]
                down, row = (kk, q) if keys_down else (q, kk)
                dst = k.bank[bank][:, n * T:(n + 1) * T]
                extra = more(c + n)
                m = pe.done(nc.tensor.matmul(dst, down[:, tile * P:(tile + 1) * P], row, start=True, stop=not extra))
                for i, (a, b) in enumerate(extra):
                    m = pe.done(nc.tensor.matmul(dst, a, b, start=False, stop=i == len(extra) - 1))
            return m

        n = 0
        for it in range(NT):
            add = [(k.identb[:, :], self.mask[:, it, :])] if self.causal else []
            for c in range(0, H, 2):
                bank = n % 4
                n += 1
                m = scores(bank, c, it, False, lambda head: add)
                mx = evacuated(k, bank, v(m).done(V.tensor_reduce(
                    self.nmax[:, it, c:c + 2], k.bank[bank][:, :].rearrange("p (n j) -> p n j", n=2),
                    AX.X, ALU.max, negate=True)))
        pe(mx, k.drained.get(5))
        for it in range(NT):
            m = pe.done(nc.tensor.transpose(k.bank[5][:, it * P:(it + 1) * P], self.nmax[:, it, :], k.ident[:, :]))
        nt = evacuated(k, 5, v(m).done(V.tensor_copy(self.nmaxT[:, :], k.bank[5][:, 0:T])))
        pe(nt)
        ex = {}
        n = 0
        for c in range(0, H, 2):
            for jt in range(NT):
                bank = n % 4
                n += 1
                mk = [(k.identb[:, :], self.maskT[:, jt, :])] if self.causal else []
                m = scores(bank, c, jt, True,
                           lambda head: mk + [(k.identb[:, head:head + 1].broadcast_to([P, P]), self.nmaxT[:, :])])
                ex[c] = evacuated(k, bank, s(m).done(A.activation(
                    self.pT[:, jt, c:c + 2, :], k.bank[bank][:, :].rearrange("p (n i) -> p n i", n=2),
                    ACT.Exp, scale=1.0 / math.sqrt(D))))
        for it in range(NT):
            pe(va, k.drained.get(4 + it))
            for c in range(H):
                pe(ex[c - c % 2])
                for jt in range(NT):
                    m = pe.done(nc.tensor.matmul(k.bank[4 + it][:, c * (D + 1):(c + 1) * (D + 1)],
                                                 self.pT[:, jt, c, it * P:(it + 1) * P], self.va[:, jt, c, :],
                                                 start=jt == 0, stop=jt == NT - 1))
            o = k.bank[4 + it][:, 0:H * (D + 1)].rearrange("p (c d) -> p c d", c=H)
            r = v(m).done(V.reciprocal(self.rden[:, it, :], o[:, :, D:D + 1].rearrange("p c o -> p (c o)")))
            at = v(r).done(V.tensor_tensor(self.att[:, it, :].rearrange("p (h d) -> p h d", h=H), o[:, :, 0:D],
                                           rep(self.rden[:, it, :], 2, D), ALU.mult))
            evacuated(k, 4 + it, at)
        m = turn(k, self.att, 6, at)
        m = evacuated(k, 6, v(m).done(V.tensor_copy(self.attT[:, :, :].rearrange("p k t -> p (k t)"), k.bank[6][:, :])))
        for t in range(NT):
            m = project(k, 7, [self.attT[:, kt, t * P:(t + 1) * P] for kt in range(KC)],
                        [self.w["o"][:, kt, :] for kt in range(KC)], m if t == 0 else None, col=t * C)
        return m


def two(ap):
    return ap.rearrange("p (t c) -> p t c", t=NT)


def flat2(ap):
    return ap.rearrange("p t c -> p (t c)")


def add_rows(k, x, bank, bias, mark, out=None):
    v, V = k.v, k.nc.vector
    m = evacuated(k, bank, v(mark).done(V.tensor_tensor(x[:, :, :], x[:, :, :], two(k.bank[bank][:, :]), ALU.add)))
    if bias is not None:
        m = v(m).done(V.tensor_tensor(x[:, :, :], x[:, :, :], rep(bias[:, :], 1, NT), ALU.add))
    return m


def context_turned(k, io, b, c, cT):
    m = k.queues[2]().done(k.nc.sync.dma_start(c[:, :, :], io["ctx_1024"][b].rearrange("(t p) c -> p t c", p=P)))
    m = turn(k, c, 1, m)
    return evacuated(k, 1, k.v(m).done(k.nc.vector.tensor_copy(cT[:, :, :].rearrange("p k t -> p (k t)"), k.bank[1][:, :])))


def hidden_turned(k, h, hT, m, bank=0):
    m = turn(k, h, bank, m)
    return evacuated(k, bank, k.v(m).done(k.nc.vector.tensor_copy(hT[:, :, :].rearrange("p k t -> p (k t)"), k.bank[bank][:, :])))


def layer0_rest(k, io, dr):
    nc, v, s, pe = k.nc, k.v, k.s, k.pe
    V, A = nc.vector, nc.scalar
    FB = F // P
    with ExitStack() as scope:
        sb = lambda n, sh, dt=F32: k.sbuf(scope, "l0_" + n, sh, dt)
        norm_scratch(k, scope, "l0")
        at = Attention(k, io, scope, "l0x_", True, False)
        wo, bo = sb("wo", [P, KC, C]), sb("bo", [P, C])
        gnw, gnb = sb("gnw", [P, KC]), sb("gnb", [P, KC])
        x, h, hT = sb("x", [P, NT, C]), sb("h", [P, NT, C]), sb("hT", [P, KC, T])
        c, cT = sb("c", [P, NT, C]), sb("cT", [P, KC, T])
        wkv, gate, wT = sb("wkv", [P, NT, C]), sb("gate", [P, NT, C]), sb("wT", [P, KC, T])
        ga = sb("ga", [P, KC, E + E * R])
        gb = sb("gb", [P, E])
        wi, wib = sb("wi", [P, KC, F]), sb("wib", [P, FB])
        lb = sb("lb", [P, F])
        w2, w2b = sb("w2", [P, FB, C]), sb("w2b", [P, C])
        lg, mx, ix = sb("lg", [P, NT, E]), sb("mx", [P, NT, 8]), sb("ix", [P, NT, 8], U32)
        ixf, oh = sb("ixf", [P, NT]), sb("oh", [P, NT, E])
        am, amT = sb("am", [P, NT, P]), sb("amT", [P, T])
        mid = sb("mid", [P, FB, T])
        kp = lambda a: a.rearrange("(k p) n -> p k n", p=P)
        load_weight(k, wo[:, :, :], kp(io["w_o"]))
        load_weight(k, bo[:, :], row_to_all(io["L0_attn_b_o"], P))
        with nc.allow_non_contiguous_dma("vectors by partition"):
            load_weight(k, gnw[:, :], io["L0_attn_gn_weight"].rearrange("(k p) -> p k", p=P))
            load_weight(k, gnb[:, :], io["L0_attn_gn_bias"].rearrange("(k p) -> p k", p=P))
            load_weight(k, wib[:, :], io["L0_ffn_wi_b"].rearrange("(k p) -> p k", p=P))
            load_weight(k, ga[:, :, 0:E], kp(io["gate_wT"]))
            load_weight(k, ga[:, :, E:], kp(io["lora_aT"]))
        load_weight(k, gb[:, :], row_to_all(io["L0_ffn_gate_b"], P))
        load_weight(k, wi[:, :, :], kp(io["wiT"]))
        z = v().done(V.memset(lb[:, :], 0.0))
        v().done(V.memset(am[:, :, :], 0.0))
        k.queues[0](z).done(nc.sync.dma_start(lb[0:E * R, :], io["lora_bT"]))
        load_weight(k, w2[:, :, :], kp(io["woT"]))
        load_weight(k, w2b[:, :], row_to_all(io["L0_ffn_wo_b"], P))
        k.fence()
        rows = lambda a: a.rearrange("(t p) c -> p t c", p=P)
        with nc.Fori(0, B) as b:
            mw = k.queues[0]().done(nc.sync.dma_start(wkv[:, :, :], rows(dr["wkv"][b])))
            mg = k.queues[1]().done(nc.sync.dma_start(gate[:, :, :], rows(dr["g"][b])))
            mx_ = k.queues[3]().done(nc.sync.dma_start(x[:, :, :], rows(io["x"][b])))
            ct = context_turned(k, io, b, c, cT)
            m = turn(k, wkv, 0, mw)
            for kt in range(KC):
                a = v(m).done(V.tensor_scalar(wT[:, kt, :], k.bank[0][:, kt * T:(kt + 1) * T], gnw[:, kt:kt + 1],
                                              gnb[:, kt:kt + 1], ALU.mult, ALU.add))
            evacuated(k, 0, a)
            for t in range(NT):
                m = project(k, 2, [wT[:, kt, t * P:(t + 1) * P] for kt in range(KC)], [wo[:, kt, :] for kt in range(KC)],
                            a, col=t * C)
            m = evacuated(k, 2, v(m).done(V.tensor_tensor(wkv[:, :, :], two(k.bank[2][:, :]), rep(bo[:, :], 1, NT), ALU.add)))
            m = v(m, mg).done(V.tensor_tensor(wkv[:, :, :], wkv[:, :, :], gate[:, :, :], ALU.mult))
            m = v(m, mx_).done(V.tensor_tensor(x[:, :, :], x[:, :, :], wkv[:, :, :], ALU.add))
            m = layer_norm(k, x, h, m)
            m = hidden_turned(k, h, hT, m)
            m = at.run(hT, cT, m)
            m = add_rows(k, x, 7, at.bo, m)
            m = layer_norm(k, x, h, m)
            m = hidden_turned(k, h, hT, m)
            for t in range(NT):
                p = project(k, 1, [hT[:, kt, t * P:(t + 1) * P] for kt in range(KC)], [ga[:, kt, :] for kt in range(KC)],
                            m, col=t * 64)
            cut = k.bank[1][:, 0:NT * 64].rearrange("p (t c) -> p t c", t=NT)
            a = v(p).done(V.tensor_tensor(lg[:, :, :], cut[:, :, 0:E], rep(gb[:, :], 1, NT), ALU.add))
            for t in range(NT):
                q = v(a).done(V.max(mx[:, t, :], lg[:, t, :]))
            for t in range(NT):
                q = v(q).done(V.max_index(ix[:, t, :], mx[:, t, :], lg[:, t, :]))
            q = v(q).done(V.tensor_copy(ixf[:, :], ix[:, :, 0:1].rearrange("p t o -> p (t o)")))
            q = v(q).done(V.tensor_tensor(oh[:, :, :], rep(k.iota64[:, 0:E], 1, NT), rep(ixf[:, :], 2, E), ALU.is_equal))
            for t in range(NT):
                q = v(q).done(V.tensor_tensor(am[:, t, 0:E * R].rearrange("p (e r) -> p e r", e=E), cut[:, t, E:E + E * R].rearrange("p (e r) -> p e r", e=E),
                                              rep(oh[:, t, :], 2, R), ALU.mult))
            evacuated(k, 1, q)
            pe(q, k.drained.get(2))
            for t in range(NT):
                q = pe.done(nc.tensor.transpose(k.bank[2][:, t * P:(t + 1) * P], am[:, t, :], k.ident[:, :]))
            q = evacuated(k, 2, v(q).done(V.tensor_copy(amT[:, :], k.bank[2][:, 0:T])))
            for f in range(FB):
                bank = 3 + f % 3
                fs = slice(f * P, (f + 1) * P)
                p = project(k, bank, [wi[:, kt, fs] for kt in range(KC)] + [lb[:, fs]],
                            [hT[:, kt, :] for kt in range(KC)] + [amT[:, :]], q)
                r = evacuated(k, bank, v(p).done(V.tensor_scalar(mid[:, f, :], k.bank[bank][:, 0:T], wib[:, f:f + 1], 0.0,
                                                                 ALU.add, ALU.max)))
            for t in range(NT):
                p = project(k, 6, [mid[:, f, t * P:(t + 1) * P] for f in range(FB)], [w2[:, f, :] for f in range(FB)],
                            r, col=t * C)
            m = add_rows(k, x, 6, w2b, p)
            k.queues[4](m).done(nc.sync.dma_start(rows(dr["x1"][b]), x[:, :, :]))
            k.fence()


def ssm_inputs(k, io, dr):
    nc, v, s, pe = k.nc, k.v, k.s, k.pe
    V, A = nc.vector, nc.scalar
    with ExitStack() as scope:
        sb = lambda n, sh, dt=F32: k.sbuf(scope, "si_" + n, sh, dt)
        norm_scratch(k, scope, "si")
        x, h, hT = sb("x", [P, NT, C]), sb("h", [P, NT, C]), sb("hT", [P, KC, T])
        sq, ms = sb("sq", [P, NT, C]), sb("ms", [P, NT])
        nw = sb("nw", [P, KC])
        win = sb("win", [P, KC, 2 * INNER])
        cw, cb, db = sb("cw", [P, IB, KW]), sb("cb", [P, IB]), sb("db", [P, IB])
        wdt, wbc = sb("wdt", [P, IB, INNER]), sb("wbc", [P, IB, 2 * N])
        xpad = sb("xpad", [P, IB, T + KW - 1])
        acc = sb("acc", [P, 2, IB, T])
        xc, zs = sb("xc", [P, IB, T]), sb("zs", [P, IB, T])
        u, ab, dt = sb("u", [P, IB, T]), sb("ab", [P, IB, T]), sb("dt", [P, IB, T])
        ub, dx = sb("ub", [P, IB, T]), sb("dx", [P, IB, T])
        bc, rest = sb("bc", [P, 3, T], BF16), sb("rest", [P, 2, T])
        kp = lambda a: a.rearrange("(k p) n -> p k n", p=P)
        with nc.allow_non_contiguous_dma("vectors by partition"):
            load_weight(k, nw[:, :], io["L1_attn_norm_w"].rearrange("(k p) -> p k", p=P))
            load_weight(k, cw[:, :, :], io["L1_attn_conv_w"].rearrange("(k p) o w -> p k (o w)", p=P))
            load_weight(k, cb[:, :], io["L1_attn_conv_b"].rearrange("(k p) -> p k", p=P))
            load_weight(k, db[:, :], io["L1_attn_dt_b"].rearrange("(k p) -> p k", p=P))
            load_weight(k, wbc[:, :, 0:N], kp(io["b_wT"]))
            load_weight(k, wbc[:, :, N:], kp(io["c_wT"]))
        load_weight(k, win[:, :, :], kp(io["in_projT"]))
        load_weight(k, wdt[:, :, :], kp(io["dt_wT"]))
        v().done(V.memset(xpad[:, :, 0:KW - 1], 0.0))
        k.fence()
        rows = lambda a: a.rearrange("(t p) c -> p t c", p=P)
        with nc.Fori(0, B) as b:
            m = k.queues[0]().done(nc.sync.dma_start(x[:, :, :], rows(dr["x1"][b])))
            m = layer_norm(k, x, h, m)
            hm = m
            m = v(m).done(V.tensor_tensor(sq[:, :, :], h[:, :, :], h[:, :, :], ALU.mult))
            m = v(m).done(V.tensor_reduce(ms[:, :], sq[:, :, :], AX.X, ALU.add))
            m = v(m).done(V.tensor_scalar(ms[:, :], ms[:, :], 1.0 / C, 1e-6, ALU.mult, ALU.add))
            m = s(m).done(A.activation(ms[:, :], ms[:, :], ACT.Sqrt))
            m = v(m).done(V.reciprocal(ms[:, :], ms[:, :]))
            m = v(m).done(V.tensor_tensor(sq[:, :, :], h[:, :, :], rep(ms[:, :], 2, C), ALU.mult))
            q = v(hm).done(V.tensor_tensor(x[:, :, :], x[:, :, :], h[:, :, :], ALU.add))
            k.queues[1](q).done(nc.sync.dma_start(rows(dr["x2"][b]), x[:, :, :]))
            m = turn(k, sq, 0, m)
            for kt in range(KC):
                a = v(m).done(V.tensor_scalar(hT[:, kt, :], k.bank[0][:, kt * T:(kt + 1) * T], nw[:, kt:kt + 1], None, ALU.mult))
            evacuated(k, 0, a)
            for j in range(IB):
                bank = 1 + j % 2
                for i, o in ((0, 0), (1, INNER)):
                    p = project(k, bank, [win[:, kt, o + j * P:o + (j + 1) * P] for kt in range(KC)],
                                [hT[:, kt, :] for kt in range(KC)], a, col=i * T)
                c = v(p).done(V.tensor_copy(xpad[:, j, KW - 1:], k.bank[bank][:, 0:T]))
                z = evacuated(k, bank, s(c).done(A.activation(zs[:, j, :], k.bank[bank][:, T:2 * T], ACT.Silu)))
                c = v(c).done(V.tensor_scalar(acc[:, 0, j, :], xpad[:, j, 0:T], cw[:, j, 0:1], None, ALU.mult))
                for w in range(1, KW):
                    c = v(c).done(V.scalar_tensor_tensor(acc[:, w % 2, j, :], xpad[:, j, w:w + T], cw[:, j, w:w + 1],
                                                         acc[:, 1 - w % 2, j, :], ALU.mult, ALU.add))
                cx = s(c).done(A.activation(xc[:, j, :], acc[:, (KW - 1) % 2, j, :], ACT.Silu, bias=cb[:, j:j + 1]))
            k.queues[2](cx).done(nc.sync.dma_start(dr["xc"][b], xc[:, :, :].rearrange("p j t -> p (j t)")))
            k.queues[2](z).done(nc.sync.dma_start(dr["zs"][b], zs[:, :, :].rearrange("p j t -> p (j t)")))
            for j in range(IB):
                bank = 3 + j // 2
                p = project(k, bank, [wdt[:, kt, j * P:(j + 1) * P] for kt in range(IB)], [xc[:, kt, :] for kt in range(IB)],
                            cx, col=(j % 2) * T)
                p = v(p).done(V.tensor_scalar(ub[:, j, :], k.bank[bank][:, (j % 2) * T:(j % 2 + 1) * T], db[:, j:j + 1],
                                              None, ALU.add))
                pe(p)
            fl = lambda a: a[:, :, :].rearrange("p j t -> p (j t)")
            m = v(p).done(V.tensor_scalar(fl(u), fl(ub), -1.0, None, ALU.mult))
            m = v(m).done(V.tensor_tensor(fl(ab), fl(ub), fl(u), ALU.min))
            m = s(m).done(A.activation(fl(ab), fl(ab), ACT.Exp))
            m = v(m).done(V.tensor_scalar(fl(ab), fl(ab), 1.0, None, ALU.add))
            m = s(m).done(A.activation(fl(ab), fl(ab), ACT.Ln))
            n_ = v(m).done(V.tensor_scalar(fl(u), fl(ub), 0.0, 1e-4, ALU.max, ALU.add))
            m = v(n_).done(V.tensor_tensor(fl(dt), fl(u), fl(ab), ALU.add))
            q = v(m).done(V.tensor_tensor(fl(dx), fl(dt), fl(xc), ALU.mult))
            k.queues[3](m).done(nc.sync.dma_start(dr["dt"][b], fl(dt)))
            k.queues[3](q).done(nc.sync.dma_start(dr["dx"][b], fl(dx)))
            p = project(k, 5, [wbc[:, kt, :] for kt in range(IB)], [xc[:, kt, :] for kt in range(IB)], cx)
            src = k.bank[5][:, 0:T]
            m = v(p).done(V.tensor_copy(bc[:, 0, :], src))
            m = v(m).done(V.tensor_tensor(rest[:, 0, :], src, bc[:, 0, :], ALU.subtract))
            m = v(m).done(V.tensor_copy(bc[:, 1, :], rest[:, 0, :]))
            m = v(m).done(V.tensor_tensor(rest[:, 1, :], rest[:, 0, :], bc[:, 1, :], ALU.subtract))
            m = v(m).done(V.tensor_copy(bc[:, 2, :], rest[:, 1, :]))
            k.queues[4](m).done(nc.sync.dma_start(dr["bc"][b], bc[:, :, :].rearrange("p a t -> p (a t)")))
            k.fence()


def ssm_scan(k, io, dr):
    nc, v, s, pe, g = k.nc, k.v, k.s, k.pe, k.g
    V, A = nc.vector, nc.scalar
    G = 2
    W = G * T
    UN = 16
    with ExitStack() as scope:
        sb = lambda n, sh, dt=F32: k.sbuf(scope, "ss_" + n, sh, dt)
        neg_a = sb("neg_a", [P, IB, N])
        dpar = sb("dpar", [P, IB])
        dt, dx = sb("dt", [P, IB, G, T]), sb("dx", [P, IB, G, T])
        xc, zs = sb("xc", [P, IB, G, T]), sb("zs", [P, IB, G, T])
        bc = sb("bc", [P, 3, G, T], BF16)
        a_now, pick_now = sb("a_now", [P, IB, UN]), sb("pick_now", [P, 2, UN], BF16)
        da = [sb(f"da{i}", [P, IB, G, T]) for i in range(3)]
        bs = [sb(f"bs{i}", [P, W]) for i in range(2)]
        uu = [sb(f"uu{i}", [P, IB, W]) for i in range(3)]
        hh = [sb(f"hh{i}", [P, IB, W]) for i in range(2)]
        hc = [sb(f"hc{i}", [P, IB, W]) for i in range(3)]
        with nc.allow_non_contiguous_dma("vectors by partition"):
            load_weight(k, neg_a[:, :, :], io["L1_attn_A_log"].rearrange("(j p) n -> p j n", p=P))
            m = load_weight(k, dpar[:, :], io["L1_attn_D_param"].rearrange("(j p) -> p j", p=P))
        m = s(m).done(A.activation(neg_a[:, :, :], neg_a[:, :, :], ACT.Exp))
        v(m).done(V.tensor_scalar(neg_a[:, :, :], neg_a[:, :, :], -1.0, None, ALU.mult))
        for t in da:
            g().done(nc.gpsimd.memset(t[:, :, :, 0:1], 0.0))
        k.fence()
        fl = lambda a: a[:, :, :, :].rearrange("p j g t -> p (j g t)")
        with nc.Fori(0, B // G) as cb:
            for q, (name, t) in enumerate((("dt", dt), ("dx", dx), ("xc", xc), ("zs", zs))):
                for i in range(G):
                    m = k.queues[q]().done(nc.sync.dma_start(t[:, :, i, :], dr[name][cb * G + i].rearrange("p (j t) -> p j t", j=IB)))
            for i in range(G):
                k.queues[4]().done(nc.sync.dma_start(bc[:, :, i, :], dr["bc"][cb * G + i].rearrange("p (a t) -> p a t", a=3)))
            for j in range(IB):
                m = v(k.queues[2].last).done(V.tensor_scalar(hc[0][:, j, :], xc[:, j, :, :].rearrange("p g t -> p (g t)"),
                                                             dpar[:, j:j + 1], None, ALU.mult))
            pe(m)
            for j in range(IB):
                pe.done(nc.tensor.matmul(k.bank[j][:, :], k.ident[:, :], hc[0][:, j, :], start=True, stop=False,
                                         skip_group_check=True))
            k.fence()
            with nc.Fori(0, N // UN) as nb:
                m1 = s().done(A.copy(a_now[:, :, :], neg_a[:, :, bass.ds(nb * UN, UN)]))
                m2 = v().done(V.tensor_copy(pick_now[:, 0, :], k.identb[:, bass.ds(nb * UN, UN)]))
                m2 = v().done(V.tensor_copy(pick_now[:, 1, :], k.identb[:, bass.ds(nb * UN + N, UN)]))
                s(m1)
                pe(m2)
                marks = []
                for n in range(UN):
                    cur = {}
                    old = marks[n - 2] if n >= 2 else {}
                    old3 = marks[n - 3] if n >= 3 else {}
                    for i, bank in ((0, 4 + n % 2), (1, 6 + n % 2)):
                        pe(old.get("b_free") if i == 0 else old.get("hc"))
                        for part in range(3):
                            cur[i] = pe.done(nc.tensor.matmul(
                                k.bank[bank][:, :], pick_now[:, i, n:n + 1].broadcast_to([P, P]),
                                bc[:, part, :, :].rearrange("p g t -> p (g t)"), start=part == 0, stop=part == 2))
                    cur["b_free"] = s(cur[0], old.get("u")).done(A.copy(bs[n % 2][:, :], k.bank[4 + n % 2][:, :]))
                    s(old3.get("scan"))
                    for j in range(IB):
                        cur["da"] = s().done(A.activation(da[n % 3][:, j, :, 1:T], dt[:, j, :, 1:T], ACT.Exp,
                                                          scale=a_now[:, j, n:n + 1]))
                    cur["u"] = g(cur["b_free"], old3.get("scan")).done(nc.gpsimd.tensor_tensor(
                        uu[n % 3][:, :, :], dx[:, :, :, :].rearrange("p j g t -> p j (g t)"), rep(bs[n % 2][:, :], 1, IB),
                        ALU.mult))
                    cur["scan"] = v(cur["u"], cur["da"], old.get("hc")).done(V.tensor_tensor_scan(
                        hh[n % 2][:, :, :].rearrange("p j w -> p (j w)"), fl(da[n % 3]),
                        uu[n % 3][:, :, :].rearrange("p j w -> p (j w)"), 0.0, ALU.mult, ALU.add))
                    cur["hc"] = v(cur["scan"], cur[1], old3.get("y")).done(V.tensor_tensor(
                        hc[n % 3][:, :, :], hh[n % 2][:, :, :], rep(k.bank[6 + n % 2][:, :], 1, IB), ALU.mult))
                    marks.append(cur)
                    for late in ([n - 1] if n else []) + ([n] if n == UN - 1 else []):
                        pe(marks[late]["hc"])
                        for j in range(IB):
                            marks[late]["y"] = pe.done(nc.tensor.matmul(
                                k.bank[j][:, :], k.ident[:, :], hc[late % 3][:, j, :], start=False, stop=False,
                                skip_group_check=True))
                k.fence()
            for j in range(IB):
                m = v().done(V.tensor_tensor(hc[0][:, j, :], k.bank[j][:, :], zs[:, j, :, :].rearrange("p g t -> p (g t)"), ALU.mult))
            for i in range(G):
                k.queues[5](m).done(nc.sync.dma_start(dr["ys"][cb * G + i].rearrange("p (j t) -> p j t", j=IB),
                                                      hc[0][:, :, i * T:(i + 1) * T]))
            k.fence()


def layer1_attention(k, io, dr, keep):
    nc, v, s, pe = k.nc, k.v, k.s, k.pe
    V, A = nc.vector, nc.scalar
    with ExitStack() as scope:
        sb = lambda n, sh, dt=F32: k.sbuf(scope, "l1_" + n, sh, dt)
        norm_scratch(k, scope, "l1")
        at = Attention(k, io, scope, "l1x_", False, True)
        wout = sb("wout", [P, IB, C])
        x, h, hT = sb("x", [P, NT, C]), sb("h", [P, NT, C]), sb("hT", [P, KC, T])
        c, cT = sb("c", [P, NT, C]), sb("cT", [P, KC, T])
        ys = sb("ys", [P, IB, T])
        load_weight(k, wout[:, :, :], io["out_projT"].rearrange("(k p) n -> p k n", p=P))
        k.fence()
        rows = lambda a: a.rearrange("(t p) c -> p t c", p=P)
        with nc.Fori(0, B) as b:
            mx = k.queues[0]().done(nc.sync.dma_start(x[:, :, :], rows(dr["x2"][b])))
            my = k.queues[1]().done(nc.sync.dma_start(ys[:, :, :].rearrange("p j t -> p (j t)"), dr["ys"][b]))
            context_turned(k, io, b, c, cT)
            for t in range(NT):
                m = project(k, 2, [ys[:, j, t * P:(t + 1) * P] for j in range(IB)], [wout[:, j, :] for j in range(IB)],
                            my, col=t * C)
            v(mx)
            m = add_rows(k, x, 2, None, m)
            m = layer_norm(k, x, h, m)
            m = hidden_turned(k, h, hT, m)
            m = at.run(hT, cT, m)
            m = add_rows(k, x, 7, at.bo, m)
            k.queues[3](m).done(nc.sync.dma_start(rows(dr["x3"][b]), x[:, :, :]))
            m = layer_norm(k, x, h, m)
            m = hidden_turned(k, h, hT, m)
            for kt in range(KC):
                v(m).done(V.bn_stats(keep["stats"][:, kt, bass.ds(b * 6, 6)], hT[:, kt, :]))
            k.fence()


def product_keys(k, io, dr, keep):
    nc, v, s, pe, g = k.nc, k.v, k.s, k.pe, k.g
    V, A = nc.vector, nc.scalar
    NE = NK * NK
    EB = NE // P
    HK = NH * TK
    with ExitStack() as scope:
        sb = lambda n, sh, dt=F32: k.sbuf(scope, "pk_" + n, sh, dt)
        norm_scratch(k, scope, "pk")
        wk = sb("wk", [P, KC, 2 * NH * NK])
        bg, bb, mv = sb("bg", [P, KC]), sb("bb", [P, KC]), sb("mv", [P, KC, 2])
        bscale, bshift = sb("bscale", [P, KC]), sb("bshift", [P, KC])
        io8 = k.iota64[:, 0:TK]
        with ExitStack() as first:
            wq = k.sbuf(first, "pk_wq", [P, 2 * NH, C])
            keys = k.sbuf(first, "pk_keys", [P, 2 * NH, NK])
            with nc.allow_non_contiguous_dma("vectors by partition"):
                load_weight(k, bg[:, :], io["L1_ffn_bn_gamma"].rearrange("(k p) -> p k", p=P))
                load_weight(k, bb[:, :], io["L1_ffn_bn_beta"].rearrange("(k p) -> p k", p=P))
            load_weight(k, wq[:, :, :], io["L1_ffn_w_q"].rearrange("(g p) n -> p g n", p=P))
            m = load_weight(k, keys[:, :, :], io["keysT"])
            for kt in range(KC):
                for half in range(2):
                    bank = kt * 2 + half
                    pe(m)
                    for q in range(NH):
                        p = pe.done(nc.tensor.matmul(k.bank[bank][:, q * NK:(q + 1) * NK],
                                                     wq[:, half * NH + q, kt * P:(kt + 1) * P], keys[:, half * NH + q, :],
                                                     start=True, stop=True))
                    v(p).done(V.tensor_copy(wk[:, kt, half * 512:(half + 1) * 512], k.bank[bank][:, :]))
            for kt in range(KC):
                m = v().done(V.bn_aggr(mv[:, kt, :], keep["stats"][:, kt, :]))
            m = v(m).done(V.tensor_scalar(bscale[:, :], mv[:, :, 1:2].rearrange("p k o -> p (k o)"), 1e-5, None, ALU.add))
            m = s(m).done(A.activation(bscale[:, :], bscale[:, :], ACT.Sqrt))
            m = v(m).done(V.reciprocal(bscale[:, :], bscale[:, :]))
            m = v(m).done(V.tensor_tensor(bscale[:, :], bscale[:, :], bg[:, :], ALU.mult))
            m = v(m).done(V.tensor_tensor(bshift[:, :], mv[:, :, 0:1].rearrange("p k o -> p (k o)"), bscale[:, :], ALU.mult))
            m = v(m).done(V.tensor_tensor(bshift[:, :], bb[:, :], bshift[:, :], ALU.subtract))
            k.fence()
        down, up = sb("down", [P, KC, EB, P]), sb("up", [P, EB, C])
        x, h = sb("x", [P, 1, C]), sb("h", [P, 1, C])
        hT, xn = sb("hT", [P, KC, P]), sb("xn", [P, KC, P])
        sim = sb("sim", [P, 2, NH, NK])
        top, tix, tif = sb("top", [P, 2, NH, TK]), sb("tix", [P, 2 * NH, TK], U32), sb("tif", [P, 2, NH, TK])
        comb = sb("comb", [P, NH, TK, TK])
        sc, pk = sb("sc", [P, NH, TK]), sb("pk", [P, NH, TK], U32)
        sel, self_ = sb("sel", [P, 2, HK], U32), sb("self", [P, 2, HK])
        eq = sb("eq", [P, HK, TK])
        chosen, upper = sb("chosen", [P, 2, HK]), sb("upper", [P, HK])
        vals = sb("vals", [P, 3, 2, HK])
        turned = sb("turned", [P, 3, 64])
        rowhot = sb("rowhot", [P, 64, P])
        blockhot = sb("blockhot", [P, 64, EB])
        iota128 = sb("iota128", [P, P])
        g().done(nc.gpsimd.iota(iota128[:, :], [[1, P]], base=0, channel_multiplier=0,
                                allow_small_or_imprecise_dtypes=True))
        act = sb("act", [P, EB, P])
        load_weight(k, down[:, :, :, :], io["downT"].rearrange("(k p) (j e) -> p k j e", p=P, e=P))
        load_weight(k, up[:, :, :], io["upT"])
        k.fence()
        with nc.Fori(0, B * NT) as tile:
            row = bass.ds(tile * P, P)
            m = k.queues[0]().done(nc.sync.dma_start(x[:, 0, :], dr["x3"].rearrange("b t c -> (b t) c")[row, :]))
            m = layer_norm(k, x, h, m, tiles=1)
            m = turn(k, h, 0, m, tiles=1)
            ht = v(m).done(V.tensor_copy(hT[:, :, :].rearrange("p k t -> p (k t)"), k.bank[0][:, 0:KC * P]))
            for kt in range(KC):
                m = v(ht).done(V.tensor_scalar(xn[:, kt, :], hT[:, kt, :], bscale[:, kt:kt + 1], bshift[:, kt:kt + 1],
                                               ALU.mult, ALU.add))
            k.drained[0] = m
            for half in range(2):
                p = project(k, 1 + half, [xn[:, kt, :] for kt in range(KC)],
                            [wk[:, kt, half * 512:(half + 1) * 512] for kt in range(KC)], m)
                q = s(p).done(A.copy(sim[:, half, :, :].rearrange("p h n -> p (h n)"), k.bank[1 + half][:, :]))
            for jb in range(EB // 4):
                bank = 3 + jb % 2
                pe(ht, k.drained.get(bank))
                for j in range(4 * jb, 4 * jb + 4):
                    p = project(k, bank, [down[:, kt, j, :] for kt in range(KC)], [hT[:, kt, :] for kt in range(KC)],
                                None, col=(j % 4) * P)
                ga = evacuated(k, bank, s(p).done(A.activation(
                    act[:, 4 * jb:4 * jb + 4, :].rearrange("p j t -> p (j t)"), k.bank[bank][:, :], ACT.Gelu)))
            m = q
            for i in range(2 * NH):
                t_ = v(m).done(V.max(top[:, i // NH, i % NH, :], sim[:, i // NH, i % NH, :]))
            for i in range(2 * NH):
                t_ = v(t_).done(V.max_index(tix[:, i, :], top[:, i // NH, i % NH, :], sim[:, i // NH, i % NH, :]))
            ti = v(t_).done(V.tensor_copy(tif[:, :, :, :].rearrange("p a h n -> p (a h n)"),
                                          tix[:, :, :].rearrange("p a n -> p (a n)")))
            for hd in range(NH):
                m = v(t_).done(V.tensor_tensor(comb[:, hd, :, :], rep(top[:, 0, hd, :], 2, TK), rep(top[:, 1, hd, :], 1, TK),
                                               ALU.add))
            cflat = comb[:, :, :, :].rearrange("p h a b -> p h (a b)")
            for hd in range(NH):
                m2 = v(m).done(V.max(sc[:, hd, :], cflat[:, hd, :]))
            for hd in range(NH):
                m3 = v(m2).done(V.max_index(pk[:, hd, :], sc[:, hd, :], cflat[:, hd, :]))
            gate = s(m2).done(A.activation(vals[:, 2, 0, :], sc[:, :, :].rearrange("p h n -> p (h n)"), ACT.Sigmoid))
            gate = s(m2).done(A.activation(vals[:, 2, 1, :], sc[:, :, :].rearrange("p h n -> p (h n)"), ACT.Sigmoid))
            pkf = pk[:, :, :].rearrange("p h n -> p (h n)")
            a = v(m3).done(V.tensor_scalar(sel[:, 0, :], pkf, 3, None, ALU.logical_shift_right))
            a = v(m3).done(V.tensor_scalar(sel[:, 1, :], pkf, 7, None, ALU.bitwise_and))
            a = v(a).done(V.tensor_copy(self_[:, :, :], sel[:, :, :]))
            for i in range(2):
                e = v(a).done(V.tensor_tensor(eq[:, :, :], rep(self_[:, i, :], 2, TK), rep(io8, 1, HK), ALU.is_equal))
                for hd in range(NH):
                    e2 = v(e, ti).done(V.tensor_tensor(eq[:, hd * TK:(hd + 1) * TK, :], eq[:, hd * TK:(hd + 1) * TK, :],
                                                       rep(tif[:, i, hd, :], 1, TK), ALU.mult))
                e2 = a = v(e2).done(V.tensor_reduce(chosen[:, i, :], eq[:, :, :], AX.X, ALU.add))
            u_ = v(e2).done(V.tensor_scalar(upper[:, :], chosen[:, 1, :], float(EB), None, ALU.is_ge))
            for two_ in range(2):
                vl = v(u_).done(V.scalar_tensor_tensor(vals[:, 0, two_, :], upper[:, :], float(NK), chosen[:, 0, :],
                                                       ALU.mult, ALU.add))
                vl = v(u_).done(V.scalar_tensor_tensor(vals[:, 1, two_, :], upper[:, :], -float(EB), chosen[:, 1, :],
                                                       ALU.mult, ALU.add))
            pe(vl, gate, k.drained.get(5))
            for i in range(3):
                p = pe.done(nc.tensor.transpose(k.bank[5][:, i * P:(i + 1) * P],
                                                vals[:, i, :, :].rearrange("p a n -> p (a n)"), k.ident[:, :]))
            tb = k.bank[5][:, 0:3 * P].rearrange("p (i t) -> p i t", i=3)
            v(p).done(V.tensor_copy(turned[0:64, :, :], tb[0:64, :, 0:64]))
            m = evacuated(k, 5, v(p).done(V.tensor_copy(turned[64:P, :, :], tb[64:P, :, 64:P])))
            v(m).done(V.tensor_tensor(rowhot[:, :, :], rep(turned[:, 0, :], 2, P), rep(iota128[:, :], 1, 64), ALU.is_equal))
            o2 = v(m).done(V.tensor_tensor(blockhot[:, :, :], rep(turned[:, 1, :], 2, EB), rep(iota128[:, 0:EB], 1, 64),
                                           ALU.is_equal))
            o2 = v(o2).done(V.tensor_tensor(blockhot[:, :, :], blockhot[:, :, :], rep(turned[:, 2, :], 2, EB), ALU.mult))
            per = 512 // EB
            for tg in range(P // per):
                bank = 6 + tg % 2
                pe(o2, k.drained.get(bank))
                for u in range(per):
                    tok = tg * per + u
                    ps = slice(0, 64) if tok < 64 else slice(64, P)
                    p = pe.done(nc.tensor.matmul(k.bank[bank][:, u * EB:(u + 1) * EB], rowhot[ps, tok % 64, :],
                                                 blockhot[ps, tok % 64, :], start=True, stop=True))
                a_ = act[:, :, tg * per:(tg + 1) * per].rearrange("p j t -> p t j")
                w = evacuated(k, bank, v(p, ga).done(V.tensor_tensor(
                    a_, a_, k.bank[bank][:, :].rearrange("p (t n) -> p t n", n=EB), ALU.mult)))
            m = project(k, 5, [act[:, j, :] for j in range(EB)], [up[:, j, :] for j in range(EB)], w)
            m = v(m).done(V.tensor_tensor(x[:, 0, :], x[:, 0, :], k.bank[5][:, 0:C], ALU.add))
            k.queues[1](m).done(nc.sync.dma_start(io["out"].rearrange("b t c -> (b t) c")[row, :], x[:, 0, :]))
            k.fence()


def build(nc, io):
    dram = lambda n, sh, dt=F32: nc.dram_tensor("keep_" + n, sh, dt, kind="Internal").ap()
    dr = {n: dram(n, (B, T, C)) for n in ("r", "k", "v", "g", "wkv", "x1", "x2", "x3")}
    dr |= {n: dram(n, (B, P, IB * T)) for n in ("xc", "zs", "dt", "dx", "ys")}
    dr["bc"] = dram("bc", (B, P, 3 * T), BF16)
    with ExitStack() as ctx:
        ctx.enter_context(nc.allow_non_contiguous_dma("small vectors and head slices go to partitions"))
        k = Core(nc, ctx)
        constants(k)
        keep = {"stats": k.sbuf(ctx, "bn_statistics", [P, KC, B * 6])}
        todo = [lambda: mixer_inputs(k, io, dr), lambda: mixer_scan(k, io, dr), lambda: layer0_rest(k, io, dr),
                lambda: ssm_inputs(k, io, dr), lambda: ssm_scan(k, io, dr),
                lambda: layer1_attention(k, io, dr, keep), lambda: product_keys(k, io, dr, keep)]
        for stage in todo:
            stage()


def laid_out(i):
    c = np.ascontiguousarray
    a = {n: c(np.asarray(x)) for n, x in i.items()}
    out = {n: a[n] for n in (
        "x", "ctx_1024", "L0_attn_b_r", "L0_attn_b_k", "L0_attn_b_v", "L0_attn_b_g", "L0_attn_b_o", "L0_attn_decay",
        "L0_attn_eta", "L0_attn_gn_weight", "L0_attn_gn_bias", "L0_ffn_gate_b", "L0_ffn_wi_b", "L0_ffn_wo_b",
        "L1_attn_conv_w", "L1_attn_conv_b", "L1_attn_A_log", "L1_attn_D_param", "L1_attn_dt_b", "L1_attn_norm_w",
        "L1_ffn_bn_gamma", "L1_ffn_bn_beta", "L1_ffn_w_q")}
    for n in "rkvgo":
        out["w_" + n] = c(a["L0_attn_W_" + n].T)
    for n in "rkvg":
        out["time_mix_" + n] = c(a["L0_attn_time_mix_" + n].reshape(C))
    for n, m in (("wq", "W_q"), ("wk", "W_k"), ("wv", "W_v"), ("bv", "b_v"), ("wo", "W_o"), ("bo", "b_o")):
        out["l0x_" + n] = a["L0_xattn_" + m]
    for n, m in (("wq", "Wq"), ("bq", "b_q"), ("wk", "Wk"), ("bk", "b_k"), ("wv", "Wv"), ("bv", "b_v"), ("wo", "Wo"),
                 ("bo", "b_o")):
        out["l1x_" + n] = a["L1_xattn_" + m]
    out["gate_wT"] = c(a["L0_ffn_gate_W"].T)
    out["lora_aT"] = c(a["L0_ffn_lora_A"].reshape(E * R, C).T)
    out["lora_bT"] = c(a["L0_ffn_lora_B"].transpose(0, 2, 1).reshape(E * R, F))
    out["wiT"], out["woT"] = c(a["L0_ffn_wi_W"].T), c(a["L0_ffn_wo_W"].T)
    out["in_projT"], out["out_projT"] = c(a["L1_attn_in_proj_w"].T), c(a["L1_attn_out_proj_w"].T)
    out["b_wT"], out["c_wT"], out["dt_wT"] = (c(a["L1_attn_" + n].T) for n in ("B_w", "C_w", "dt_w"))
    out["keysT"] = c(a["L1_ffn_keys_p"].transpose(3, 2, 0, 1).reshape(KD, 2 * NH, NK))
    cut = lambda w: w[:NK * NK].reshape(NK, 2, NK // 2, C)
    out["downT"] = c(cut(a["L1_ffn_down"]).transpose(3, 2, 1, 0).reshape(C, NK * NK))
    out["upT"] = c(cut(a["L1_ffn_up"]).transpose(1, 0, 2, 3).reshape(P, NK // 2, C))
    return out


def kernel(**inputs):
    import concourse.bacc as bacc
    from concourse.bass_utils import run_bass_kernel_spmd

    arrays = laid_out(inputs)
    nc = bacc.Bacc("TRN2", target_bir_lowering=False, num_devices=1)
    io = {n: nc.dram_tensor(n, a.shape, mybir.dt.from_np(a.dtype), kind="ExternalInput").ap() for n, a in arrays.items()}
    io["out"] = nc.dram_tensor("out", (B, T, C), F32, kind="ExternalOutput").ap()
    build(nc, io)
    r = run_bass_kernel_spmd(nc, [arrays], core_ids=[0])
    return r.results[0]["out"]
```

```python
import math
from contextlib import ExitStack

import numpy as np
import concourse.bass as bass
from concourse import mybir

ALU = mybir.AluOpType
ACT = mybir.ActivationFunctionType
AX = mybir.AxisListType
F32 = mybir.dt.float32
BF16 = mybir.dt.bfloat16
U32 = mybir.dt.uint32

P = 128
B, T, C = 16, 256, 256
NT = T // P
KC = C // P
H, D = 16, 16
E, R, F = 8, 4, 1024
INNER, N = 512, 64
IB = INNER // P
KW = 4
NH, NK, TK, KD = 8, 64, 8, 128
NEG = -1.0e30
SLOT_QUEUES = 6


def rep(ap, axis, n):
    a = ap.unsqueeze(axis)
    shape = list(a.shape)
    shape[axis] = n
    return a.broadcast_to(shape)


class Lane:
    STEP = 1

    def __init__(self, eng, sem):
        self.eng, self.sem, self.count, self.seen = eng, sem, 0, {}

    def __call__(self, *marks):
        for m in marks:
            if m is not None and self.seen.get(m[0].name, 0) < m[1]:
                self.eng.wait_ge(m[0], m[1])
                self.seen[m[0].name] = m[1]
        return self

    def done(self, ins):
        ins.then_inc(self.sem, self.STEP)
        self.count += self.STEP
        return (self.sem, self.count)

    @property
    def last(self):
        return (self.sem, self.count) if self.count else None


class Queue(Lane):
    STEP = 16

    def __init__(self, lane, sem):
        self.lane, self.sem, self.count = lane, sem, 0

    def __call__(self, *marks):
        self.lane(*marks)
        return self


class Core:

    def __init__(self, nc, ctx):
        self.nc, self.ctx = nc, ctx
        sem = lambda n: ctx.enter_context(nc.semaphore(n))
        self.v = Lane(nc.vector, sem("vector_done"))
        self.s = Lane(nc.scalar, sem("scalar_done"))
        self.pe = Lane(nc.tensor, sem("tensor_done"))
        self.g = Lane(nc.gpsimd, sem("gpsimd_done"))
        self.sp = Lane(nc.sync, sem("sync_done"))
        self.queues = [Queue(self.sp, sem(f"dma_done{n}")) for n in range(2 * SLOT_QUEUES)]
        self.states = {n: sem("states_" + n) for n in ("b", "c", "copied", "decay", "input", "scan", "weighed", "summed")}
        self.bank = [ctx.enter_context(nc.psum_tensor(f"bank{n}", [P, 512], F32)) for n in range(8)]
        self.drained = {}

    def fence(self):
        lanes = [self.v, self.s, self.pe, self.g, self.sp]
        for lane in lanes:
            lane(lane.last)
        self.sp(*[q.last for q in self.queues])
        numbers = sorted([x.sem.num for x in lanes + self.queues] + [x.num for x in self.states.values()])
        self.nc.all_engine_barrier(sems_to_clear=range(numbers[0], numbers[-1] + 1))
        for x in lanes:
            x.count, x.seen = 0, {}
        for q in self.queues:
            q.count = 0
        self.drained = {}

    def sbuf(self, scope, name, shape, dt=F32):
        return scope.enter_context(self.nc.sbuf_tensor(name, shape, dt))


class Slot:

    def __init__(self, k, scope, tag, n):
        self.k, self.scope, self.tag, self.n = k, scope, f"{tag}{n}_", n
        self.banks = [4 * n + i for i in range(4)]
        self.queues = k.queues[n * SLOT_QUEUES:(n + 1) * SLOT_QUEUES]
        self.ln_stats = self.sb("ln_stats", [P, NT, 6])
        self.ln_mv = self.sb("ln_mv", [P, NT, 2])

    def sb(self, name, shape, dt=F32):
        return self.k.sbuf(self.scope, self.tag + name, shape, dt)

    def load(self, q, dst, src, *ready):
        return self.queues[q](*ready).done(self.k.nc.sync.dma_start(dst, src))


def together(*passes, pace=(1, 1)):
    left = dict(enumerate(passes))
    while left:
        for n in list(left):
            for _ in range(pace[n]):
                if n in left and next(left[n], left) is left:
                    del left[n]


def sequences(k, slots, one):
    with k.nc.Fori(0, B // 2) as pair:
        together(*(one(pair * 2 + n, slot) for n, slot in enumerate(slots)))
        k.fence()


def constants(k):
    nc, g, v = k.nc, k.g, k.v
    k.ident = k.sbuf(k.ctx, "ident", [P, P])
    k.identb = k.sbuf(k.ctx, "identb", [P, P], BF16)
    k.iota64 = k.sbuf(k.ctx, "iota64", [P, 64])
    m = g().done(nc.gpsimd.memset(k.ident[:, :], 0.0))
    m = g(m).done(nc.gpsimd.affine_select(out=k.ident[:, :], in_=k.ident[:, :], compare_op=ALU.not_equal,
                                          fill=1.0, base=0, pattern=[[-1, P]], channel_multiplier=1))
    v(m).done(nc.vector.tensor_copy(k.identb[:, :], k.ident[:, :]))
    g().done(nc.gpsimd.iota(k.iota64[:, :], [[1, 64]], base=0, channel_multiplier=0,
                            allow_small_or_imprecise_dtypes=True))
    k.fence()


def layer_norm(k, z, x, h, ready, eps=1e-5, tiles=NT):
    V, v, s = k.nc.vector, k.v, k.s
    st, mv = z.ln_stats, z.ln_mv
    for t in range(tiles):
        m = v(ready).done(V.bn_stats(st[:, t, :], x[:, t, :]))
    yield
    for t in range(tiles):
        m = v(m).done(V.bn_aggr(mv[:, t, :], st[:, t, :]))
    yield
    m = v(m).done(V.tensor_scalar(mv[:, 0:tiles, 1:2], mv[:, 0:tiles, 1:2], eps, None, ALU.add))
    m = s(m).done(k.nc.scalar.activation(mv[:, 0:tiles, 1:2], mv[:, 0:tiles, 1:2], ACT.Sqrt))
    yield
    m = v(m).done(V.reciprocal(mv[:, 0:tiles, 1:2], mv[:, 0:tiles, 1:2]))
    yield
    for t in range(tiles):
        r = v(m).done(V.tensor_scalar(h[:, t, :], x[:, t, :], mv[:, t, 0:1], mv[:, t, 1:2],
                                      ALU.subtract, ALU.mult))
    yield
    return r


def turn(k, src, bank, ready, tiles=NT, blocks=KC):
    k.pe(ready, k.drained.get(bank))
    for kt in range(blocks):
        for t in range(tiles):
            o = (kt * tiles + t) * P
            m = k.pe.done(k.nc.tensor.transpose(k.bank[bank][:, o:o + P], src[:, t, kt * P:(kt + 1) * P],
                                                k.ident[:, :]))
    return m


def evacuated(k, bank, mark):
    k.drained[bank] = mark
    return mark


def project(k, bank, lhsT, rhs, ready, col=0, stop=True):
    n = rhs[0].shape[-1]
    k.pe(ready, k.drained.get(bank))
    for i, (a, b) in enumerate(zip(lhsT, rhs)):
        m = k.pe.done(k.nc.tensor.matmul(k.bank[bank][0:a.shape[-1], col:col + n], a, b,
                                         start=(i == 0), stop=stop and i == len(rhs) - 1))
    return m


def load_weight(k, tile, dram):
    return k.queues[0]().done(k.nc.sync.dma_start(tile, dram))


def row_to_all(dram, n):
    return dram.unsqueeze(0).broadcast_to([n, dram.shape[0]])


def mixer_inputs(k, io, dr):
    nc, v, s, pe = k.nc, k.v, k.s, k.pe
    V, A = nc.vector, nc.scalar
    with ExitStack() as scope:
        sb = lambda n, sh, dt=F32: k.sbuf(scope, "mi_" + n, sh, dt)
        w = sb("w", [P, 4, KC, C])
        bias = sb("bias", [P, 4, C])
        mixw, unmix = sb("mixw", [P, 4, KC]), sb("unmix", [P, 4, KC])
        slots = [Slot(k, scope, "mi", n) for n in range(2)]
        for z in slots:
            z.x, z.h = z.sb("x", [P, NT, C]), z.sb("h", [P, NT, C])
            z.hT = z.sb("hT", [P, KC, T + 1])
            z.tmp, z.mix = z.sb("tmp", [P, 4, KC, T]), z.sb("mix", [P, 4, KC, T])
            z.out, z.res = z.sb("out", [P, 4, NT, C]), z.sb("res", [P, 4, NT, C])
            z.sq, z.n2 = z.sb("sq", [P, 2 * NT * C]), z.sb("n2", [P, 2 * NT * H])
            v().done(V.memset(z.hT[:, :, 0:1], 0.0))
        for i, c in enumerate("rkvg"):
            load_weight(k, w[:, i, :, :], io[f"w_{c}"].rearrange("(k p) n -> p k n", p=P))
            load_weight(k, bias[:, i, :], row_to_all(io[f"L0_attn_b_{c}"], P))
            m = load_weight(k, mixw[:, i, :], io[f"time_mix_{c}"].rearrange("(k p) -> p k", p=P))
        v(m).done(V.tensor_scalar(unmix[:, :, :], mixw[:, :, :], -1.0, 1.0, ALU.mult, ALU.add))
        k.fence()

        def one(b, z):
            m = z.load(0, z.x[:, :, :], io["x"][b].rearrange("(t p) c -> p t c", p=P))
            m = yield from layer_norm(k, z, z.x, z.h, m)
            m = turn(k, z.h, z.banks[0], m)
            yield
            m = evacuated(k, z.banks[0], v(m).done(V.tensor_copy(
                z.hT[:, :, 1:T + 1], k.bank[z.banks[0]][:, :].rearrange("p (k t) -> p k t", k=KC))))
            yield
            for i in range(4):
                bank = z.banks[i]
                for kt in range(KC):
                    a = s(m).done(A.activation(z.tmp[:, i, kt, :], z.hT[:, kt, 0:T], ACT.Copy,
                                               scale=unmix[:, i, kt:kt + 1]))
                yield
                for kt in range(KC):
                    a = v(a).done(V.scalar_tensor_tensor(z.mix[:, i, kt, :], z.hT[:, kt, 1:T + 1],
                                                         mixw[:, i, kt:kt + 1], z.tmp[:, i, kt, :],
                                                         ALU.mult, ALU.add))
                for t in range(NT):
                    p = project(k, bank, [z.mix[:, i, kt, t * P:(t + 1) * P] for kt in range(KC)],
                                [w[:, i, kt, :] for kt in range(KC)], a, col=t * C)
                yield
                r = evacuated(k, bank, v(p).done(V.tensor_tensor(
                    z.out[:, i, :, :], two(k.bank[bank][:, :]), rep(bias[:, i, :], 1, NT), ALU.add)))
                if i == 0:
                    r_act = s(r).done(A.activation(z.res[:, 0, :, :], z.out[:, 0, :, :], ACT.Sigmoid))
                yield
            g_act = s(r).done(A.activation(z.res[:, 3, :, :], z.out[:, 3, :, :], ACT.Silu))
            kv = z.out[:, 1:3, :, :].rearrange("p a t c -> p (a t c)")
            a = v(r).done(V.tensor_tensor(z.sq[:, :], kv, kv, ALU.mult))
            yield
            a = v(a).done(V.tensor_reduce(z.n2[:, :], z.sq[:, :].rearrange("p (n d) -> p n d", d=D), AX.X, ALU.add))
            yield
            a = v(a).done(V.tensor_scalar(z.n2[:, :], z.n2[:, :], 1e-24, None, ALU.max))
            a = s(a).done(A.activation(z.n2[:, :], z.n2[:, :], ACT.Sqrt))
            yield
            a = v(a).done(V.reciprocal(z.n2[:, :], z.n2[:, :]))
            yield
            a = v(a).done(V.tensor_tensor(
                z.res[:, 1:3, :, :].rearrange("p a t c -> p (a t c)").rearrange("p (n d) -> p n d", d=D),
                kv.rearrange("p (n d) -> p n d", d=D), rep(z.n2[:, :], 2, D), ALU.mult))
            for i, c in enumerate("rkvg"):
                z.load(1, dr[c][b].rearrange("(t p) c -> p t c", p=P), z.res[:, i, :, :], a, r_act, g_act)

        sequences(k, slots, one)


def mixer_scan(k, io, dr):
    nc, v, s = k.nc, k.v, k.s
    V, A = nc.vector, nc.scalar
    HP = H // 2
    max_norm = math.sqrt(D) * 2.0
    UN = 16
    with ExitStack() as scope:
        sb = lambda n, sh, dt=F32: k.sbuf(scope, "ms_" + n, sh, dt)
        KR = sb("KR", [P, T + 1, 2, 2, D])
        VV = sb("VV", [P, T, 2, D])
        PR = sb("PR", [P, T + 1, 2, 2 * D])
        FF = sb("FF", [P, T + 1, 2])
        CO = sb("CO", [P, T, 2, 2])
        S = sb("S", [P, 2, D, D])
        prod, outer = sb("prod", [P, 2, 2, D, D]), sb("outer", [P, 2, D, D])
        pe_, ee = sb("prederr", [P, 2, 2 * D]), sb("ee", [P, 2 * D])
        Q, terms = sb("Q", [P, 2, 2 * D]), sb("terms", [P, 3, 2])
        R4, N2 = sb("R4", [P, 4]), sb("N2", [P, 2])
        root, inv, fdec = sb("root", [P, 2]), sb("inv", [P, 2]), sb("fdec", [P, 2])
        dec, et, et32, dec2 = sb("dec", [P, 2]), sb("et", [P, 2]), sb("et32", [P, 2, D]), sb("dec2", [P, 2])
        cst, one32 = sb("cst", [P, 2, 2]), sb("one32", [P, 2, D])
        stat = sb("stat", [P, 4, 2])
        v().done(V.memset(KR[:, 0, 1, :, :], 0.0))
        v().done(V.memset(KR[:, T, 0, :, :], 0.0))
        v().done(V.memset(S[:, :, :, :], 0.0))
        v().done(V.memset(FF[:, 0, :], 1.0))
        v().done(V.memset(N2[:, :], 0.0))
        z = v().done(V.memset(one32[:, :, :], 1.0))
        with nc.allow_non_contiguous_dma("heads of a sequence go to partitions"):
            for b in range(B):
                ps = slice(b * HP, (b + 1) * HP)
                k.queues[0]().done(nc.sync.dma_start(KR[ps, 0:T, 0, :, :].rearrange("h t e d -> h t (e d)"), dr["k"][b].rearrange("t (h x) -> h t x", h=HP)))
                k.queues[0]().done(nc.sync.dma_start(KR[ps, 1:T + 1, 1, :, :].rearrange("h t e d -> h t (e d)"), dr["r"][b].rearrange("t (h x) -> h t x", h=HP)))
                k.queues[0]().done(nc.sync.dma_start(VV[ps, :, :, :].rearrange("h t e d -> h t (e d)"), dr["v"][b].rearrange("t (h x) -> h t x", h=HP)))
                k.queues[0]().done(nc.sync.dma_start(dec[ps, :], io["L0_attn_decay"].rearrange("(h e) a b -> h (e a b)", e=2)))
                m = k.queues[0]().done(nc.sync.dma_start(et[ps, :], io["L0_attn_eta"].rearrange("(h e) a b -> h (e a b)", e=2)))
        a = s(m).done(A.activation(dec[:, :], dec[:, :], ACT.Sigmoid))
        a = s().done(A.activation(et[:, :], et[:, :], ACT.Sigmoid))
        b1 = v(a, z).done(V.tensor_tensor(et32[:, :, :], one32[:, :, :], rep(et[:, :], 2, D), ALU.mult))
        c1 = v().done(V.tensor_tensor(dec2[:, :], dec[:, :], dec[:, :], ALU.mult))
        c2 = v().done(V.tensor_tensor(cst[:, 0, :], dec[:, :], et[:, :], ALU.mult))
        c2 = v(c2).done(V.tensor_scalar(cst[:, 0, :], cst[:, 0, :], -2.0, None, ALU.mult))
        c3 = v().done(V.tensor_tensor(cst[:, 1, :], et[:, :], et[:, :], ALU.mult))
        kk = PR[:, 0:T, 0, :].rearrange("p t (e d) -> p t e d", e=2)
        a = v(m).done(V.tensor_tensor(kk, KR[:, 0:T, 0, :, :], KR[:, 0:T, 0, :, :], ALU.mult))
        a = v(a).done(V.tensor_reduce(CO[:, :, 1, :], kk, AX.X, ALU.add))
        a = v(a, c3).done(V.tensor_tensor(CO[:, :, 1, :], CO[:, :, 1, :], rep(cst[:, 1, :], 1, T), ALU.mult))
        a = v().done(V.memset(CO[:, :, 0, :], 1.0))
        a = v(a).done(V.tensor_tensor(CO[:, :, 0, :], CO[:, :, 0, :], rep(cst[:, 0, :], 1, T), ALU.mult))
        k.fence()
        flat = lambda ap: ap.rearrange("p e i j -> p (e i j)")
        with nc.Fori(0, T // UN) as it:
            state, f_ready, n_ready = None, None, None
            for u in range(UN):
                t = it * UN + u
                kr = KR[:, t, :, :, :]
                for a_ in range(2):
                    m = v(state).done(V.tensor_tensor(prod[:, a_, :, :, :], S[:, :, :, :],
                                                      rep(kr[:, a_, :, :], 2, D), ALU.mult))
                m = v(m).done(V.tensor_reduce(PR[:, t, :, :], prod[:, :, :, :, :].rearrange(
                    "p a e i j -> p (a e i) j"), AX.X, ALU.add))
                if f_ready is not None:
                    r = v(f_ready).done(V.reciprocal(inv[:, :], root[:, :]))
                    f_ready = v(r).done(V.tensor_scalar(FF[:, t, :], inv[:, :], max_norm, 1.0, ALU.mult, ALU.min))
                fd = v(f_ready).done(V.tensor_tensor(fdec[:, :], FF[:, t, :], dec[:, :], ALU.mult))
                tn = v(n_ready).done(V.tensor_scalar(terms[:, 2, :], N2[:, :], max_norm * max_norm, None, ALU.min))
                tn = v(tn).done(V.tensor_tensor(terms[:, 2, :], terms[:, 2, :], dec2[:, :], ALU.mult))
                m = v(m, f_ready).done(V.tensor_tensor(
                    pe_[:, 0, :].rearrange("p (e i) -> p e i", e=2),
                    PR[:, t, 0, :].rearrange("p (e i) -> p e i", e=2), rep(FF[:, t, :], 2, D), ALU.mult))
                m = v(m).done(V.tensor_tensor(pe_[:, 1, :], pe_[:, 0, :],
                                              VV[:, t, :, :].rearrange("p e i -> p (e i)"), ALU.subtract))
                e_ = v(m).done(V.tensor_tensor(ee[:, :], pe_[:, 1, :], et32[:, :, :].rearrange("p e i -> p (e i)"), ALU.mult))
                q = v(m).done(V.tensor_tensor(Q[:, :, :], pe_[:, :, :], rep(pe_[:, 1, :], 1, 2), ALU.mult))
                o = v(e_).done(V.tensor_tensor(
                    outer[:, :, :, :], rep(ee[:, :].rearrange("p (e i) -> p e i", e=2), 3, D),
                    rep(kr[:, 0, :, :], 2, D), ALU.mult))
                q = v(q).done(V.tensor_reduce(R4[:, :], Q[:, :, :].rearrange("p a (e i) -> p (a e) i", e=2), AX.X, ALU.add))
                for e in range(2):
                    state = v(o, fd).done(V.scalar_tensor_tensor(
                        S[:, e, :, :].rearrange("p i j -> p (i j)"), S[:, e, :, :].rearrange("p i j -> p (i j)"),
                        fdec[:, e:e + 1], outer[:, e, :, :].rearrange("p i j -> p (i j)"), ALU.mult, ALU.subtract))
                    if e == 0:
                        q = v(q).done(V.tensor_tensor(terms[:, 0:2, :].rearrange("p a e -> p (a e)"), R4[:, :],
                                                      CO[:, t, :, :].rearrange("p a e -> p (a e)"), ALU.mult))
                n_ready = v(q, tn).done(V.tensor_reduce(N2[:, :], terms[:, :, :].rearrange("p a e -> p e a"), AX.X, ALU.add))
                q = v(n_ready).done(V.tensor_scalar(inv[:, :], N2[:, :], 1e-16, None, ALU.max))
                f_ready = s(q).done(A.activation(root[:, :], inv[:, :], ACT.Sqrt))
            r = v(f_ready).done(V.reciprocal(inv[:, :], root[:, :]))
            v(r).done(V.tensor_scalar(FF[:, it * UN + UN, :], inv[:, :], max_norm, 1.0, ALU.mult, ALU.min))
            k.fence()
        m = v().done(V.tensor_tensor(prod[:, 0, :, :, :], S[:, :, :, :], rep(KR[:, T, 1, :, :], 2, D), ALU.mult))
        m = v(m).done(V.tensor_reduce(PR[:, T, 1, :], prod[:, 0, :, :, :].rearrange("p e i j -> p (e i) j"), AX.X, ALU.add))
        m = v(m).done(V.tensor_tensor(VV[:, :, :, :], PR[:, 1:T + 1, 1, :].rearrange("p t (e i) -> p t e i", e=2),
                                      rep(FF[:, 1:T + 1, :], 3, D), ALU.mult))
        sqr = KR[:, 0:T, 0, :, :]
        by_head = lambda ap: ap.rearrange("p t e i -> p e t i")
        m = v(m).done(V.tensor_reduce(stat[:, 0, :], by_head(VV[:, :, :, :]), AX.XY, ALU.add))
        m = v(m).done(V.tensor_scalar(stat[:, 1, :], stat[:, 0, :], 1.0 / (T * D), None, ALU.mult))
        mean_all = rep(stat[:, 1, :], 1, T)
        m = v(m).done(V.tensor_tensor(VV[:, :, :, :], VV[:, :, :, :], rep(mean_all, 3, D), ALU.subtract))
        m = v(m).done(V.tensor_tensor(sqr, VV[:, :, :, :], VV[:, :, :, :], ALU.mult))
        m = v(m).done(V.tensor_reduce(stat[:, 2, :], by_head(sqr), AX.XY, ALU.add))
        m = v(m).done(V.tensor_scalar(stat[:, 2, :], stat[:, 2, :], 1.0 / (T * D), 1e-5, ALU.mult, ALU.add))
        m = s(m).done(A.activation(stat[:, 3, :], stat[:, 2, :], ACT.Sqrt))
        m = v(m).done(V.reciprocal(stat[:, 3, :], stat[:, 3, :]))
        m = v(m).done(V.tensor_tensor(VV[:, :, :, :], VV[:, :, :, :], rep(rep(stat[:, 3, :], 1, T), 3, D), ALU.mult))
        with nc.allow_non_contiguous_dma("heads of a sequence come from partitions"):
            for b in range(B):
                k.queues[1](m).done(nc.sync.dma_start(dr["wkv"][b].rearrange("t (h x) -> h t x", h=HP),
                                                      VV[b * HP:(b + 1) * HP, :, :, :].rearrange("h t e d -> h t (e d)")))
        k.fence()


class Attention:

    def __init__(self, k, io, scope, tag, causal, biased, slots):
        nc, self.k, self.causal = k.nc, k, causal
        sb = lambda n, sh, dt=F32: k.sbuf(scope, "at_" + tag + n, sh, dt)
        self.w = {c: sb("w" + c, [P, KC, C]) for c in "qkvo"}
        self.bq, self.bk = sb("bq", [P, KC]), sb("bk", [P, KC])
        self.bv, self.bo = sb("bv", [P, C]), sb("bo", [P, C])
        self.own = sb("own", [P, H // KC])
        self.bko = sb("bko", [P, H])
        for z in slots:
            z.qT = z.sb("qT", [P, KC, T])
            z.kT = z.sb("kT", [P, H, T])
            z.va = z.sb("va", [P, NT, H, D + 1])
            z.nmax = z.sb("nmax", [P, NT, P])
            z.nmaxT = z.sb("nmaxT", [P, T], BF16)
            z.pT = z.sb("pT", [P, NT, H, T])
            z.rden = z.sb("rden", [P, NT, H])
            z.att, z.attT = z.sb("att", [P, NT, C]), z.sb("attT", [P, KC, T])
        g, v = k.g, k.v
        for z in slots:
            g().done(nc.gpsimd.memset(z.va[:, :, :, :], 1.0))
            g().done(nc.gpsimd.memset(z.nmax[:, :, :], 0.0))
        v().done(nc.vector.memset(self.bq[:, :], 0.0))
        z = v().done(nc.vector.memset(self.bk[:, :], 0.0))
        own = v().done(nc.vector.tensor_reduce(self.own[:, :], k.ident[:, :].rearrange("p (h d) -> p h d", d=D), AX.X, ALU.add))
        for c in "qkvo":
            load_weight(k, self.w[c][:, :, :], io[tag + "w" + c].rearrange("(k p) n -> p k n", p=P))
        if biased:
            k.queues[5](z).done(nc.sync.dma_start(self.bq[:, :], io[tag + "bq"].rearrange("(k p) -> p k", p=P)))
            z = k.queues[5](z).done(nc.sync.dma_start(self.bk[:, :], io[tag + "bk"].rearrange("(k p) -> p k", p=P)))
        for kt in range(KC):
            v(z, own).done(nc.vector.tensor_scalar(self.bko[:, kt * 8:kt * 8 + 8], self.own[:, :], self.bk[:, kt:kt + 1],
                                                   None, ALU.mult))
        load_weight(k, self.bv[:, :], row_to_all(io[tag + "bv"], P))
        load_weight(k, self.bo[:, :], row_to_all(io[tag + "bo"], P))
        if causal:
            self.mask, self.maskT = sb("mask", [P, NT, P], BF16), sb("maskT", [P, NT, P], BF16)
            m1 = g().done(nc.gpsimd.memset(self.mask[:, :, :], 0.0))
            m2 = g().done(nc.gpsimd.memset(self.maskT[:, :, :], 0.0))
            for t in range(NT):
                g(m1).done(nc.gpsimd.affine_select(out=self.mask[:, t, :], in_=self.mask[:, t, :], compare_op=ALU.is_gt,
                                                   fill=NEG, base=0, pattern=[[-1, P]], channel_multiplier=1))
                m = g(m2).done(nc.gpsimd.affine_select(out=self.maskT[:, t, :], in_=self.maskT[:, t, :], compare_op=ALU.is_gt,
                                                       fill=NEG, base=0, pattern=[[1, P]], channel_multiplier=-1))
            v(m).done(nc.vector.memset(self.mask[0:1, 0, 0:1], 0.0))
            v(m).done(nc.vector.memset(self.maskT[0:1, 0, 0:1], 0.0))

    def run(self, z, hT, cT, ready):
        k, nc = self.k, self.k.nc
        v, s, pe, V, A = k.v, k.s, k.pe, k.nc.vector, k.nc.scalar
        b0, b1, b2, b3 = z.banks
        for kt in range(KC):
            for i, (c, src) in enumerate((("q", hT), ("k", cT))):
                m = project(k, z.banks[2 + i], [self.w[c][:, j, kt * P:(kt + 1) * P] for j in range(KC)],
                            [src[:, j, :] for j in range(KC)], ready, col=kt * T)
            yield
        qm = evacuated(k, b2, v(m).done(V.tensor_tensor(z.qT[:, :, :], k.bank[b2][:, :].rearrange("p (k t) -> p k t", k=KC),
                                                        rep(self.bq[:, :], 2, T), ALU.add)))
        for h_ in range(H):
            km = s(m).done(A.activation(z.kT[:, h_, :], k.bank[b3][:, (h_ // 8) * T:(h_ // 8 + 1) * T], ACT.Identity,
                                        scale=self.own[:, h_ % 8:h_ % 8 + 1], bias=self.bko[:, h_:h_ + 1]))
        evacuated(k, b3, km)
        for t in range(NT):
            m = project(k, b0, [cT[:, kt, t * P:(t + 1) * P] for kt in range(KC)],
                        [self.w["v"][:, kt, :] for kt in range(KC)], ready, col=t * C)
        yield
        for t in range(NT):
            va = v(m).done(V.tensor_tensor(
                z.va[:, t, :, 0:D], k.bank[b0][:, t * C:(t + 1) * C].rearrange("p (h d) -> p h d", h=H),
                self.bv[:, :].rearrange("p (h d) -> p h d", h=H), ALU.add))
        evacuated(k, b0, va)
        yield

        def scores(bank, c, tile, keys_down, cols, mask, last=None):
            pe(qm, km, k.drained.get(bank))
            for n in range(2):
                q, kk = z.qT[:, (c + n) // 8, :], z.kT[:, c + n, :]
                down, row = (kk, q) if keys_down else (q, kk)
                at = lambda cs: k.bank[bank][:, n * T + cs.start:n * T + cs.stop]
                todo = [(at(cols), down[:, tile * P:(tile + 1) * P], row[:, cols])]
                if self.causal:
                    diagonal = slice(tile * P, (tile + 1) * P)
                    todo.append((at(diagonal), k.identb[:, :], mask[:, tile, :]))
                if last:
                    todo.append((at(cols), *last(c + n)))
                for i, (dst, a, b) in enumerate(todo):
                    m = pe.done(nc.tensor.matmul(dst, a, b, start=i == 0, stop=i == len(todo) - 1))
            return m

        for it in range(NT):
            cols = slice(0, (it + 1) * P if self.causal else T)
            for c in range(0, H, 2):
                bank = z.banks[c // 2 % 2]
                m = scores(bank, c, it, False, cols, self.mask if self.causal else None)
                mx = evacuated(k, bank, v(m).done(V.tensor_reduce(
                    z.nmax[:, it, c:c + 2], k.bank[bank][:, :].rearrange("p (n j) -> p n j", n=2)[:, :, cols],
                    AX.X, ALU.max, negate=True)))
                yield
        pe(mx, k.drained.get(b2))
        for it in range(NT):
            m = pe.done(nc.tensor.transpose(k.bank[b2][:, it * P:(it + 1) * P], z.nmax[:, it, :], k.ident[:, :]))
        yield
        nt = evacuated(k, b2, v(m).done(V.tensor_copy(z.nmaxT[:, :], k.bank[b2][:, 0:T])))
        yield
        pe(nt)
        pick = lambda cols: lambda head: (k.identb[:, head:head + 1].broadcast_to([P, P]), z.nmaxT[:, cols])
        ex = {}

        def weigh(c):
            pe(va, ex[c], k.drained.get(b2) if c == 0 else None, k.drained.get(b3) if c == 0 else None)
            for it in range(NT):
                keys = range(it + 1 if self.causal else NT)
                for jt in keys:
                    m = pe.done(nc.tensor.matmul(k.bank[z.banks[2 + it]][:, c * (D + 1):(c + 1) * (D + 1)],
                                                 z.pT[:, jt, c, it * P:(it + 1) * P], z.va[:, jt, c, :],
                                                 start=jt == 0, stop=jt == keys[-1]))
            return m

        for c in range(0, H, 2):
            for jt in range(NT):
                cols = slice(jt * P if self.causal else 0, T)
                bank = z.banks[jt]
                m = scores(bank, c, jt, True, cols, self.maskT if self.causal else None, pick(cols))
                ex[c] = ex[c + 1] = evacuated(k, bank, s(m).done(A.activation(
                    z.pT[:, jt, c:c + 2, cols], k.bank[bank][:, :].rearrange("p (n i) -> p n i", n=2)[:, :, cols],
                    ACT.Exp, scale=1.0 / math.sqrt(D))))
                yield
            if c:
                weigh(c - 2)
                weigh(c - 1)
        weigh(H - 2)
        m = weigh(H - 1)
        yield
        for it in range(NT):
            bank = z.banks[2 + it]
            o = k.bank[bank][:, 0:H * (D + 1)].rearrange("p (c d) -> p c d", c=H)
            r = v(m).done(V.reciprocal(z.rden[:, it, :], o[:, :, D:D + 1].rearrange("p c o -> p (c o)")))
            yield
            at = v(r).done(V.tensor_tensor(z.att[:, it, :].rearrange("p (h d) -> p h d", h=H), o[:, :, 0:D],
                                           rep(z.rden[:, it, :], 2, D), ALU.mult))
            evacuated(k, bank, at)
        m = yield from hidden_turned(k, z.att, z.attT, at, b0)
        for t in range(NT):
            m = project(k, b1, [z.attT[:, kt, t * P:(t + 1) * P] for kt in range(KC)],
                        [self.w["o"][:, kt, :] for kt in range(KC)], m if t == 0 else None, col=t * C)
        yield
        return m


def two(ap):
    return ap.rearrange("p (t c) -> p t c", t=NT)


def flat2(ap):
    return ap.rearrange("p t c -> p (t c)")


def add_rows(k, x, bank, bias, mark):
    v, V = k.v, k.nc.vector
    m = evacuated(k, bank, v(mark).done(V.tensor_tensor(x[:, :, :], x[:, :, :], two(k.bank[bank][:, :]), ALU.add)))
    yield
    if bias is not None:
        m = v(m).done(V.tensor_tensor(x[:, :, :], x[:, :, :], rep(bias[:, :], 1, NT), ALU.add))
        yield
    return m


def hidden_turned(k, h, hT, m, bank):
    m = turn(k, h, bank, m)
    yield
    m = evacuated(k, bank, k.s(m).done(k.nc.scalar.copy(hT[:, :, :].rearrange("p k t -> p (k t)"), k.bank[bank][:, :])))
    yield
    return m


rows = lambda a: a.rearrange("(t p) c -> p t c", p=P)
kp = lambda a: a.rearrange("(k p) n -> p k n", p=P)


def layer0_rest(k, io, dr):
    nc, v, s, pe = k.nc, k.v, k.s, k.pe
    V, A = nc.vector, nc.scalar
    FB = F // P
    with ExitStack() as scope:
        sb = lambda n, sh, dt=F32: k.sbuf(scope, "l0_" + n, sh, dt)
        slots = [Slot(k, scope, "l0", n) for n in range(2)]
        at = Attention(k, io, scope, "l0x_", True, False, slots)
        wo, bo = sb("wo", [P, KC, C]), sb("bo", [P, C])
        gnw, gnb = sb("gnw", [P, KC]), sb("gnb", [P, KC])
        ga, gb = sb("ga", [P, KC, E + E * R]), sb("gb", [P, E])
        wi, wib = sb("wi", [P, KC, F]), sb("wib", [P, FB])
        lb = sb("lb", [P, F])
        w2, w2b = sb("w2", [P, FB, C]), sb("w2b", [P, C])
        for z in slots:
            z.x, z.h, z.hT = z.sb("x", [P, NT, C]), z.sb("h", [P, NT, C]), z.sb("hT", [P, KC, T])
            z.c, z.cT = z.sb("c", [P, NT, C]), z.sb("cT", [P, KC, T])
            z.wkv, z.gate, z.wT = z.sb("wkv", [P, NT, C]), z.sb("gate", [P, NT, C]), z.sb("wT", [P, KC, T])
            z.lg, z.mx, z.ix = z.sb("lg", [P, NT, E]), z.sb("mx", [P, NT, 8]), z.sb("ix", [P, NT, 8], U32)
            z.ixf, z.oh = z.sb("ixf", [P, NT]), z.sb("oh", [P, NT, E])
            z.am, z.amT = z.sb("am", [P, NT, P]), z.sb("amT", [P, T])
            z.mid = z.sb("mid", [P, FB, T])
            v().done(V.memset(z.am[:, :, :], 0.0))
        load_weight(k, wo[:, :, :], kp(io["w_o"]))
        load_weight(k, bo[:, :], row_to_all(io["L0_attn_b_o"], P))
        load_weight(k, gnw[:, :], io["L0_attn_gn_weight"].rearrange("(k p) -> p k", p=P))
        load_weight(k, gnb[:, :], io["L0_attn_gn_bias"].rearrange("(k p) -> p k", p=P))
        load_weight(k, wib[:, :], io["L0_ffn_wi_b"].rearrange("(k p) -> p k", p=P))
        load_weight(k, ga[:, :, 0:E], kp(io["gate_wT"]))
        load_weight(k, ga[:, :, E:], kp(io["lora_aT"]))
        load_weight(k, gb[:, :], row_to_all(io["L0_ffn_gate_b"], P))
        load_weight(k, wi[:, :, :], kp(io["wiT"]))
        zero = v().done(V.memset(lb[:, :], 0.0))
        k.queues[0](zero).done(nc.sync.dma_start(lb[0:E * R, :], io["lora_bT"]))
        load_weight(k, w2[:, :, :], kp(io["woT"]))
        load_weight(k, w2b[:, :], row_to_all(io["L0_ffn_wo_b"], P))
        k.fence()

        def one(b, z):
            b0, b1, b2, b3 = z.banks
            m_wkv = z.load(0, z.wkv[:, :, :], rows(dr["wkv"][b]))
            m_c = z.load(1, z.c[:, :, :], rows(io["ctx_1024"][b]))
            m_gate = z.load(2, z.gate[:, :, :], rows(dr["g"][b]))
            m_x = z.load(3, z.x[:, :, :], rows(io["x"][b]))
            m = turn(k, z.wkv, b0, m_wkv)
            yield
            for kt in range(KC):
                a = v(m).done(V.tensor_scalar(z.wT[:, kt, :], k.bank[b0][:, kt * T:(kt + 1) * T], gnw[:, kt:kt + 1],
                                              gnb[:, kt:kt + 1], ALU.mult, ALU.add))
            evacuated(k, b0, a)
            yield
            for t in range(NT):
                m = project(k, b1, [z.wT[:, kt, t * P:(t + 1) * P] for kt in range(KC)], [wo[:, kt, :] for kt in range(KC)],
                            a, col=t * C)
            yield from hidden_turned(k, z.c, z.cT, m_c, b3)
            m = evacuated(k, b1, v(m).done(V.tensor_tensor(z.wkv[:, :, :], two(k.bank[b1][:, :]), rep(bo[:, :], 1, NT), ALU.add)))
            yield
            m = v(m, m_gate).done(V.tensor_tensor(z.wkv[:, :, :], z.wkv[:, :, :], z.gate[:, :, :], ALU.mult))
            yield
            m = v(m, m_x).done(V.tensor_tensor(z.x[:, :, :], z.x[:, :, :], z.wkv[:, :, :], ALU.add))
            yield
            m = yield from layer_norm(k, z, z.x, z.h, m)
            m = yield from hidden_turned(k, z.h, z.hT, m, b0)
            m = yield from at.run(z, z.hT, z.cT, m)
            m = yield from add_rows(k, z.x, b1, at.bo, m)
            m = yield from layer_norm(k, z, z.x, z.h, m)
            m = yield from hidden_turned(k, z.h, z.hT, m, b0)
            for t in range(NT):
                p = project(k, b1, [z.hT[:, kt, t * P:(t + 1) * P] for kt in range(KC)], [ga[:, kt, :] for kt in range(KC)],
                            m, col=t * 64)
            yield
            cut = k.bank[b1][:, 0:NT * 64].rearrange("p (t c) -> p t c", t=NT)
            a = v(p).done(V.tensor_tensor(z.lg[:, :, :], cut[:, :, 0:E], rep(gb[:, :], 1, NT), ALU.add))
            yield
            for t in range(NT):
                q = v(a).done(V.max(z.mx[:, t, :], z.lg[:, t, :]))
            yield
            for t in range(NT):
                q = v(q).done(V.max_index(z.ix[:, t, :], z.mx[:, t, :], z.lg[:, t, :]))
            yield
            q = v(q).done(V.tensor_copy(z.ixf[:, :], z.ix[:, :, 0:1].rearrange("p t o -> p (t o)")))
            yield
            q = v(q).done(V.tensor_tensor(z.oh[:, :, :], rep(k.iota64[:, 0:E], 1, NT), rep(z.ixf[:, :], 2, E), ALU.is_equal))
            yield
            for t in range(NT):
                q = v(q).done(V.tensor_tensor(z.am[:, t, 0:E * R].rearrange("p (e r) -> p e r", e=E),
                                              cut[:, t, E:E + E * R].rearrange("p (e r) -> p e r", e=E),
                                              rep(z.oh[:, t, :], 2, R), ALU.mult))
            evacuated(k, b1, q)
            yield
            pe(q, k.drained.get(b2))
            for t in range(NT):
                q = pe.done(nc.tensor.transpose(k.bank[b2][:, t * P:(t + 1) * P], z.am[:, t, :], k.ident[:, :]))
            yield
            q = evacuated(k, b2, v(q).done(V.tensor_copy(z.amT[:, :], k.bank[b2][:, 0:T])))
            yield
            for f in range(FB):
                bank = z.banks[1 + f % 3]
                fs = slice(f * P, (f + 1) * P)
                p = project(k, bank, [wi[:, kt, fs] for kt in range(KC)] + [lb[:, fs]],
                            [z.hT[:, kt, :] for kt in range(KC)] + [z.amT[:, :]], q)
                r = evacuated(k, bank, v(p).done(V.tensor_scalar(z.mid[:, f, :], k.bank[bank][:, 0:T], wib[:, f:f + 1], 0.0,
                                                                 ALU.add, ALU.max)))
                yield
            for t in range(NT):
                p = project(k, b0, [z.mid[:, f, t * P:(t + 1) * P] for f in range(FB)], [w2[:, f, :] for f in range(FB)],
                            r, col=t * C)
            yield
            m = yield from add_rows(k, z.x, b0, w2b, p)
            z.load(4, rows(dr["x1"][b]), z.x[:, :, :], m)

        sequences(k, slots, one)


def ssm_inputs(k, io, dr):
    nc, v, s, pe = k.nc, k.v, k.s, k.pe
    V, A = nc.vector, nc.scalar
    with ExitStack() as scope:
        sb = lambda n, sh, dt=F32: k.sbuf(scope, "si_" + n, sh, dt)
        nw = sb("nw", [P, KC])
        win = sb("win", [P, KC, 2 * INNER])
        cw, cb, db = sb("cw", [P, IB, KW]), sb("cb", [P, IB]), sb("db", [P, IB])
        wdt, wbc = sb("wdt", [P, IB, INNER]), sb("wbc", [P, IB, 2 * N])
        slots = [Slot(k, scope, "si", n) for n in range(2)]
        for z in slots:
            z.x, z.h, z.hT = z.sb("x", [P, NT, C]), z.sb("h", [P, NT, C]), z.sb("hT", [P, KC, T])
            z.sq, z.ms = z.sb("sq", [P, NT, C]), z.sb("ms", [P, NT])
            z.xpad = z.sb("xpad", [P, IB, T + KW - 1])
            z.acc = z.sb("acc", [P, 2, IB, T])
            z.xc, z.zs, z.u = z.sb("xc", [P, IB, T]), z.sb("zs", [P, IB, T]), z.sb("u", [P, IB, T])
            z.ab, z.dt = z.sb("ab", [P, IB, T]), z.sb("dt", [P, IB, T])
            z.ub, z.dx = z.sb("ub", [P, IB, T]), z.sb("dx", [P, IB, T])
            z.bc, z.rest = z.sb("bc", [P, 3, T], BF16), z.sb("rest", [P, 2, T])
            v().done(V.memset(z.xpad[:, :, 0:KW - 1], 0.0))
        load_weight(k, nw[:, :], io["L1_attn_norm_w"].rearrange("(k p) -> p k", p=P))
        load_weight(k, cw[:, :, :], io["L1_attn_conv_w"].rearrange("(k p) o w -> p k (o w)", p=P))
        load_weight(k, cb[:, :], io["L1_attn_conv_b"].rearrange("(k p) -> p k", p=P))
        load_weight(k, db[:, :], io["L1_attn_dt_b"].rearrange("(k p) -> p k", p=P))
        load_weight(k, wbc[:, :, 0:N], kp(io["b_wT"]))
        load_weight(k, wbc[:, :, N:], kp(io["c_wT"]))
        load_weight(k, win[:, :, :], kp(io["in_projT"]))
        load_weight(k, wdt[:, :, :], kp(io["dt_wT"]))
        k.fence()
        fl = lambda a: a[:, :, :].rearrange("p j t -> p (j t)")

        def one(b, z):
            b0, b1, b2, b3 = z.banks
            m = z.load(0, z.x[:, :, :], rows(dr["x1"][b]))
            m = hm = yield from layer_norm(k, z, z.x, z.h, m)
            m = v(m).done(V.tensor_tensor(z.sq[:, :, :], z.h[:, :, :], z.h[:, :, :], ALU.mult))
            yield
            m = v(m).done(V.tensor_reduce(z.ms[:, :], z.sq[:, :, :], AX.X, ALU.add))
            yield
            m = v(m).done(V.tensor_scalar(z.ms[:, :], z.ms[:, :], 1.0 / C, 1e-6, ALU.mult, ALU.add))
            m = s(m).done(A.activation(z.ms[:, :], z.ms[:, :], ACT.Sqrt))
            yield
            m = v(m).done(V.reciprocal(z.ms[:, :], z.ms[:, :]))
            yield
            m = v(m).done(V.tensor_tensor(z.sq[:, :, :], z.h[:, :, :], rep(z.ms[:, :], 2, C), ALU.mult))
            q = v(hm).done(V.tensor_tensor(z.x[:, :, :], z.x[:, :, :], z.h[:, :, :], ALU.add))
            z.load(1, rows(dr["x2"][b]), z.x[:, :, :], q)
            m = turn(k, z.sq, b0, m)
            yield
            for kt in range(KC):
                a = v(m).done(V.tensor_scalar(z.hT[:, kt, :], k.bank[b0][:, kt * T:(kt + 1) * T], nw[:, kt:kt + 1], None, ALU.mult))
            evacuated(k, b0, a)
            yield
            for j in range(IB):
                bank = z.banks[j % 2]
                for i, o in ((0, 0), (1, INNER)):
                    p = project(k, bank, [win[:, kt, o + j * P:o + (j + 1) * P] for kt in range(KC)],
                                [z.hT[:, kt, :] for kt in range(KC)], a, col=i * T)
                yield
                c = v(p).done(V.tensor_copy(z.xpad[:, j, KW - 1:], k.bank[bank][:, 0:T]))
                zm = evacuated(k, bank, s(c).done(A.activation(z.zs[:, j, :], k.bank[bank][:, T:2 * T], ACT.Silu)))
                yield
                c = v(c).done(V.tensor_scalar(z.acc[:, 0, j, :], z.xpad[:, j, 0:T], cw[:, j, 0:1], None, ALU.mult))
                for w in range(1, KW):
                    yield
                    c = v(c).done(V.scalar_tensor_tensor(z.acc[:, w % 2, j, :], z.xpad[:, j, w:w + T], cw[:, j, w:w + 1],
                                                         z.acc[:, 1 - w % 2, j, :], ALU.mult, ALU.add))
                cx = s(c).done(A.activation(z.xc[:, j, :], z.acc[:, (KW - 1) % 2, j, :], ACT.Silu, bias=cb[:, j:j + 1]))
            z.load(2, dr["xc"][b], fl(z.xc), cx)
            z.load(2, dr["zs"][b], fl(z.zs), zm)
            yield
            for j in range(IB):
                bank = z.banks[2 + j % 2]
                p = project(k, bank, [wdt[:, kt, j * P:(j + 1) * P] for kt in range(IB)], [z.xc[:, kt, :] for kt in range(IB)], cx)
                yield
                p = evacuated(k, bank, v(p).done(V.tensor_scalar(z.ub[:, j, :], k.bank[bank][:, 0:T], db[:, j:j + 1],
                                                                 None, ALU.add)))
            m = v(p).done(V.tensor_scalar(fl(z.u), fl(z.ub), -1.0, None, ALU.mult))
            yield
            m = v(m).done(V.tensor_tensor(fl(z.ab), fl(z.ub), fl(z.u), ALU.min))
            m = s(m).done(A.activation(fl(z.ab), fl(z.ab), ACT.Exp))
            yield
            n_ = v(m).done(V.tensor_scalar(fl(z.u), fl(z.ub), 0.0, 1e-4, ALU.max, ALU.add))
            m = s(m).done(A.activation(fl(z.ab), fl(z.ab), ACT.Ln, bias=1.0))
            yield
            p = project(k, b0, [wbc[:, kt, :] for kt in range(IB)], [z.xc[:, kt, :] for kt in range(IB)], cx)
            m = v(n_, m).done(V.tensor_tensor(fl(z.dt), fl(z.u), fl(z.ab), ALU.add))
            yield
            q = v(m).done(V.tensor_tensor(fl(z.dx), fl(z.dt), fl(z.xc), ALU.mult))
            z.load(3, dr["dt"][b], fl(z.dt), m)
            z.load(3, dr["dx"][b], fl(z.dx), q)
            src = k.bank[b0][:, 0:T]
            m = v(p).done(V.tensor_copy(z.bc[:, 0, :], src))
            yield
            m = v(m).done(V.tensor_tensor(z.rest[:, 0, :], src, z.bc[:, 0, :], ALU.subtract))
            yield
            m = v(m).done(V.tensor_copy(z.bc[:, 1, :], z.rest[:, 0, :]))
            yield
            m = v(m).done(V.tensor_tensor(z.rest[:, 1, :], z.rest[:, 0, :], z.bc[:, 1, :], ALU.subtract))
            yield
            m = v(m).done(V.tensor_copy(z.bc[:, 2, :], z.rest[:, 1, :]))
            z.load(4, dr["bc"][b], z.bc[:, :, :].rearrange("p a t -> p (a t)"), m)

        sequences(k, slots, one)


def ssm_scan(k, io, dr):
    nc, v, s, pe, g = k.nc, k.v, k.s, k.pe, k.g
    V, A = nc.vector, nc.scalar
    G = 2
    W = G * T
    UN = 4
    with ExitStack() as scope:
        sb = lambda n, sh, dt=F32: k.sbuf(scope, "ss_" + n, sh, dt)
        neg_a = sb("neg_a", [P, IB, N])
        dpar = sb("dpar", [P, IB])
        dt, dx = sb("dt", [P, IB, G, T]), sb("dx", [P, IB, G, T])
        xc, zs = sb("xc", [P, IB, G, T]), sb("zs", [P, IB, G, T])
        bc = sb("bc", [P, 3, G, T], BF16)
        decay = [sb(f"decay{i}", [P, IB, G, T]) for i in range(UN)]
        b_all = [sb(f"b_all{i}", [P, W]) for i in range(2)]
        inp = [sb(f"inp{i}", [P, IB, W]) for i in range(UN)]
        h = [sb(f"h{i}", [P, IB, W]) for i in range(2)]
        ch = [sb(f"ch{i}", [P, IB, W]) for i in range(UN)]
        load_weight(k, neg_a[:, :, :], io["L1_attn_A_log"].rearrange("(j p) n -> p j n", p=P))
        m = load_weight(k, dpar[:, :], io["L1_attn_D_param"].rearrange("(j p) -> p j", p=P))
        m = s(m).done(A.activation(neg_a[:, :, :], neg_a[:, :, :], ACT.Exp))
        v(m).done(V.tensor_scalar(neg_a[:, :, :], neg_a[:, :, :], -1.0, None, ALU.mult))
        for t in decay:
            g().done(nc.gpsimd.memset(t[:, :, :, 0:1], 0.0))
        k.fence()
        flat = lambda a: a.rearrange("p j w -> p (j w)")
        done = k.states

        def wait(lane, step, count, static):
            if not static or count > 0:
                lane.eng.wait_ge(done[step], count)

        def spread(n, u, row, bank, step, static):
            for part in range(3):
                m = nc.tensor.matmul(k.bank[bank][:, :], k.identb[:, bass.ds(n + row, 1)].broadcast_to([P, P]),
                                     bc[:, part, :, :].rearrange("p g t -> p (g t)"), start=part == 0, stop=part == 2)
            m.then_inc(done[step], 1)

        def first(n, u, static):
            wait(pe, "copied", n - 1, static)
            spread(n, u, 0, 4 + u % 2, "b", static)
            wait(s, "input", n - 1, static)
            wait(s, "b", n + 1, static)
            A.copy(b_all[u % 2][:, :], k.bank[4 + u % 2][:, :]).then_inc(done["copied"], 1)
            wait(s, "scan", n - 3, static)
            for j in range(IB):
                m = A.activation(decay[u][:, j, :, 1:T], dt[:, j, :, 1:T], ACT.Exp, scale=neg_a[:, j, bass.ds(n, 1)])
            m.then_inc(done["decay"], 1)
            wait(g, "copied", n + 1, static)
            wait(g, "scan", n - 3, static)
            nc.gpsimd.tensor_tensor(inp[u][:, :, :], dx[:, :, :, :].rearrange("p j g t -> p j (g t)"),
                                    rep(b_all[u % 2][:, :], 1, IB), ALU.mult).then_inc(done["input"], 1)

        def second(n, u, static):
            wait(pe, "weighed", n - 1, static)
            spread(n, u, N, 6 + u % 2, "c", static)
            wait(v, "input", n + 1, static)
            wait(v, "decay", n + 1, static)
            wait(v, "weighed", n - 1, static)
            V.tensor_tensor_scan(flat(h[u % 2][:, :, :]), decay[u][:, :, :, :].rearrange("p j g t -> p (j g t)"),
                                 flat(inp[u][:, :, :]), 0.0, ALU.mult, ALU.add).then_inc(done["scan"], 1)
            wait(v, "scan", n + 1, static)
            wait(v, "c", n + 1, static)
            wait(v, "summed", n - 3, static)
            V.tensor_tensor(ch[u][:, :, :], h[u % 2][:, :, :], rep(k.bank[6 + u % 2][:, :], 1, IB),
                            ALU.mult).then_inc(done["weighed"], 1)

        def third(n, u, static):
            wait(pe, "weighed", n + 1, static)
            for j in range(IB):
                m = nc.tensor.matmul(k.bank[j][:, :], k.ident[:, :], ch[u][:, j, :], start=False, stop=False,
                                     skip_group_check=True)
            m.then_inc(done["summed"], 1)

        with nc.Fori(0, B // G) as cb:
            for q, (name, t) in enumerate((("dt", dt), ("dx", dx), ("xc", xc), ("zs", zs))):
                for i in range(G):
                    m = k.queues[q]().done(nc.sync.dma_start(t[:, :, i, :], dr[name][cb * G + i].rearrange("p (j t) -> p j t", j=IB)))
            for i in range(G):
                k.queues[4]().done(nc.sync.dma_start(bc[:, :, i, :], dr["bc"][cb * G + i].rearrange("p (a t) -> p a t", a=3)))
            for j in range(IB):
                m = v(k.queues[2].last).done(V.tensor_scalar(ch[0][:, j, :], xc[:, j, :, :].rearrange("p g t -> p (g t)"),
                                                             dpar[:, j:j + 1], None, ALU.mult))
            pe(m)
            for j in range(IB):
                pe.done(nc.tensor.matmul(k.bank[j][:, :], k.ident[:, :], ch[0][:, j, :], start=True, stop=False,
                                         skip_group_check=True))
            k.fence()

            def step(n, u, static):
                if not static or n < N:
                    first(n, u, static)
                if not static or 1 <= n <= N:
                    second(n - 1, (u - 1) % UN, static)
                if not static or 2 <= n:
                    third(n - 2, (u - 2) % UN, static)

            for n in range(UN):
                step(n, n, True)
            with nc.Fori(1, N // UN) as block:
                for u in range(UN):
                    step(block * UN + u, u, False)
            for n in range(N, N + 2):
                step(n, n % UN, True)
            v.eng.wait_ge(done["summed"], N)
            for j in range(IB):
                m = v().done(V.tensor_tensor(ch[0][:, j, :], k.bank[j][:, :], zs[:, j, :, :].rearrange("p g t -> p (g t)"), ALU.mult))
            for i in range(G):
                k.queues[5](m).done(nc.sync.dma_start(dr["ys"][cb * G + i].rearrange("p (j t) -> p j t", j=IB),
                                                      ch[0][:, :, i * T:(i + 1) * T]))
            k.fence()


def layer1_attention(k, io, dr, keep):
    nc, v, s, pe = k.nc, k.v, k.s, k.pe
    V = nc.vector
    with ExitStack() as scope:
        slots = [Slot(k, scope, "l1", n) for n in range(2)]
        at = Attention(k, io, scope, "l1x_", False, True, slots)
        wout = k.sbuf(scope, "l1_wout", [P, IB, C])
        for z in slots:
            z.x, z.h, z.hT = z.sb("x", [P, NT, C]), z.sb("h", [P, NT, C]), z.sb("hT", [P, KC, T])
            z.c, z.cT, z.ys = z.sb("c", [P, NT, C]), z.sb("cT", [P, KC, T]), z.sb("ys", [P, IB, T])
        load_weight(k, wout[:, :, :], kp(io["out_projT"]))
        k.fence()

        def one(b, z):
            b0, b1, b2, b3 = z.banks
            my = z.load(0, z.ys[:, :, :].rearrange("p j t -> p (j t)"), dr["ys"][b])
            mx = z.load(1, z.x[:, :, :], rows(dr["x2"][b]))
            mc = z.load(2, z.c[:, :, :], rows(io["ctx_1024"][b]))
            for t in range(NT):
                m = project(k, b1, [z.ys[:, j, t * P:(t + 1) * P] for j in range(IB)], [wout[:, j, :] for j in range(IB)],
                            my, col=t * C)
            yield
            v(mx)
            m = yield from add_rows(k, z.x, b1, None, m)
            yield from hidden_turned(k, z.c, z.cT, mc, b3)
            m = yield from layer_norm(k, z, z.x, z.h, m)
            m = yield from hidden_turned(k, z.h, z.hT, m, b0)
            m = yield from at.run(z, z.hT, z.cT, m)
            m = yield from add_rows(k, z.x, b1, at.bo, m)
            z.load(3, rows(dr["x3"][b]), z.x[:, :, :], m)
            m = yield from layer_norm(k, z, z.x, z.h, m)
            m = yield from hidden_turned(k, z.h, z.hT, m, b0)
            for kt in range(KC):
                v(m).done(V.bn_stats(keep["stats"][:, kt, bass.ds(b * 6, 6)], z.hT[:, kt, :]))

        sequences(k, slots, one)


def product_keys(k, io, dr, keep):
    nc, v, s, pe, g = k.nc, k.v, k.s, k.pe, k.g
    V, A = nc.vector, nc.scalar
    NE = NK * NK
    EB = NE // P
    HK = NH * TK
    TILES = B * NT
    with ExitStack() as scope:
        sb = lambda n, sh, dt=F32: k.sbuf(scope, "pk_" + n, sh, dt)
        wk = sb("wk", [P, KC, 2 * NH * NK])
        bg, bb, mv = sb("bg", [P, KC]), sb("bb", [P, KC]), sb("mv", [P, KC, 2])
        bscale, bshift = sb("bscale", [P, KC]), sb("bshift", [P, KC])
        iota128 = sb("iota128", [P, P])
        g().done(nc.gpsimd.iota(iota128[:, :], [[1, P]], base=0, channel_multiplier=0,
                                allow_small_or_imprecise_dtypes=True))
        with ExitStack() as first:
            wq = k.sbuf(first, "pk_wq", [P, 2 * NH, C])
            keys = k.sbuf(first, "pk_keys", [P, 2 * NH, NK])
            load_weight(k, bg[:, :], io["L1_ffn_bn_gamma"].rearrange("(k p) -> p k", p=P))
            load_weight(k, bb[:, :], io["L1_ffn_bn_beta"].rearrange("(k p) -> p k", p=P))
            load_weight(k, wq[:, :, :], io["L1_ffn_w_q"].rearrange("(g p) n -> p g n", p=P))
            m = load_weight(k, keys[:, :, :], io["keysT"])
            for kt in range(KC):
                for half in range(2):
                    bank = kt * 2 + half
                    pe(m)
                    for q in range(NH):
                        p = pe.done(nc.tensor.matmul(k.bank[bank][:, q * NK:(q + 1) * NK],
                                                     wq[:, half * NH + q, kt * P:(kt + 1) * P], keys[:, half * NH + q, :],
                                                     start=True, stop=True))
                    v(p).done(V.tensor_copy(wk[:, kt, half * 512:(half + 1) * 512], k.bank[bank][:, :]))
            for kt in range(KC):
                m = v().done(V.bn_aggr(mv[:, kt, :], keep["stats"][:, kt, :]))
            m = v(m).done(V.tensor_scalar(bscale[:, :], mv[:, :, 1:2].rearrange("p k o -> p (k o)"), 1e-5, None, ALU.add))
            m = s(m).done(A.activation(bscale[:, :], bscale[:, :], ACT.Sqrt))
            m = v(m).done(V.reciprocal(bscale[:, :], bscale[:, :]))
            m = v(m).done(V.tensor_tensor(bscale[:, :], bscale[:, :], bg[:, :], ALU.mult))
            m = v(m).done(V.tensor_tensor(bshift[:, :], mv[:, :, 0:1].rearrange("p k o -> p (k o)"), bscale[:, :], ALU.mult))
            m = v(m).done(V.tensor_tensor(bshift[:, :], bb[:, :], bshift[:, :], ALU.subtract))
            k.fence()
        down, up = sb("down", [P, KC, EB, P]), sb("up", [P, EB, C])
        slots = [Slot(k, scope, "pk", n) for n in range(2)]
        for z in slots:
            z.x, z.h, z.hT = z.sb("x", [P, 1, C]), z.sb("h", [P, 1, C]), z.sb("hT", [P, KC, P])
            z.rowhot = z.sb("rowhot", [P, 64, P], BF16)
            z.blockhot = z.sb("blockhot", [P, 3, 64, EB], BF16)
        xn = sb("xn", [P, KC, P])
        sim = sb("sim", [P, 2, NH, NK])
        top, tix, tif = sb("top", [P, 2, NH, TK]), sb("tix", [P, 2 * NH, TK], U32), sb("tif", [P, 2, NH, TK])
        comb = sb("comb", [P, NH, TK, TK])
        sc, pk = sb("sc", [P, NH, TK]), sb("pk", [P, NH, TK], U32)
        sel, self_ = sb("sel", [P, 2, HK], U32), sb("self", [P, 2, HK])
        eq = sb("eq", [P, HK, TK])
        chosen, upper = sb("chosen", [P, 2, HK]), sb("upper", [P, HK])
        vals = sb("vals", [P, 3, 2, HK])
        turned = sb("turned", [P, 3, 64])
        onehot, parts, left_ = sb("onehot", [P, 64, EB], BF16), sb("parts", [P, 3, 64], BF16), sb("left", [P, 2, 64])
        act = sb("act", [P, EB, P])
        load_weight(k, down[:, :, :, :], io["downT"].rearrange("(k p) (j e) -> p k j e", p=P, e=P))
        load_weight(k, up[:, :, :], io["upT"])
        k.fence()
        by_token = lambda a: a.rearrange("b t c -> (b t) c")

        def choose(tile, z):
            m = z.load(0, z.x[:, 0, :], by_token(dr["x3"])[bass.ds(tile * P, P), :])
            m = yield from layer_norm(k, z, z.x, z.h, m, tiles=1)
            m = turn(k, z.h, 0, m, tiles=1)
            yield
            ht = v(m).done(V.tensor_copy(z.hT[:, :, :].rearrange("p k t -> p (k t)"), k.bank[0][:, 0:KC * P]))
            yield
            for kt in range(KC):
                m = v(ht).done(V.tensor_scalar(xn[:, kt, :], z.hT[:, kt, :], bscale[:, kt:kt + 1], bshift[:, kt:kt + 1],
                                               ALU.mult, ALU.add))
            evacuated(k, 0, m)
            for half in range(2):
                p = project(k, 1 + half, [xn[:, kt, :] for kt in range(KC)],
                            [wk[:, kt, half * 512:(half + 1) * 512] for kt in range(KC)], m)
                yield
                q = evacuated(k, 1 + half, s(p).done(A.copy(sim[:, half, :, :].rearrange("p h n -> p (h n)"), k.bank[1 + half][:, :])))
            yield
            m = q
            for i in range(2 * NH):
                t_ = v(m).done(V.max(top[:, i // NH, i % NH, :], sim[:, i // NH, i % NH, :]))
                if i % 4 == 3:
                    yield
            for i in range(2 * NH):
                x_ = v(t_).done(V.max_index(tix[:, i, :], top[:, i // NH, i % NH, :], sim[:, i // NH, i % NH, :]))
                if i % 4 == 3:
                    yield
            ti = s(x_).done(A.copy(tif[:, :, :, :].rearrange("p a h n -> p (a h n)"),
                                   tix[:, :, :].rearrange("p a n -> p (a n)")))
            for hd in range(NH):
                m = v(t_).done(V.tensor_tensor(comb[:, hd, :, :], rep(top[:, 0, hd, :], 2, TK), rep(top[:, 1, hd, :], 1, TK),
                                               ALU.add))
                if i % 4 == 3:
                    yield
            cflat = comb[:, :, :, :].rearrange("p h a b -> p h (a b)")
            for hd in range(NH):
                m2 = v(m).done(V.max(sc[:, hd, :], cflat[:, hd, :]))
            yield
            for two_ in range(2):
                gate = s(m2).done(A.activation(vals[:, 2, two_, :], sc[:, :, :].rearrange("p h n -> p (h n)"), ACT.Sigmoid))
            for hd in range(NH):
                m3 = v(m2).done(V.max_index(pk[:, hd, :], sc[:, hd, :], cflat[:, hd, :]))
            yield
            pkf = pk[:, :, :].rearrange("p h n -> p (h n)")
            a = v(m3).done(V.tensor_scalar(sel[:, 0, :], pkf, 3, None, ALU.logical_shift_right))
            a = v(m3).done(V.tensor_scalar(sel[:, 1, :], pkf, 7, None, ALU.bitwise_and))
            yield
            a = v(a).done(V.tensor_copy(self_[:, :, :], sel[:, :, :]))
            yield
            for i in range(2):
                e = v(a).done(V.tensor_tensor(eq[:, :, :], rep(self_[:, i, :], 2, TK), rep(iota128[:, 0:TK], 1, HK), ALU.is_equal))
                yield
                for hd in range(NH):
                    e2 = v(e, ti).done(V.tensor_tensor(eq[:, hd * TK:(hd + 1) * TK, :], eq[:, hd * TK:(hd + 1) * TK, :],
                                                       rep(tif[:, i, hd, :], 1, TK), ALU.mult))
                yield
                e2 = a = v(e2).done(V.tensor_reduce(chosen[:, i, :], eq[:, :, :], AX.X, ALU.add))
                yield
            u_ = v(e2).done(V.tensor_scalar(upper[:, :], chosen[:, 1, :], float(EB), None, ALU.is_ge))
            yield
            for two_ in range(2):
                vl = v(u_).done(V.scalar_tensor_tensor(vals[:, 0, two_, :], upper[:, :], float(NK), chosen[:, 0, :],
                                                       ALU.mult, ALU.add))
                vl = v(u_).done(V.scalar_tensor_tensor(vals[:, 1, two_, :], upper[:, :], -float(EB), chosen[:, 1, :],
                                                       ALU.mult, ALU.add))
            pe(vl, gate, k.drained.get(0))
            for i in range(3):
                p = pe.done(nc.tensor.transpose(k.bank[0][:, i * P:(i + 1) * P],
                                                vals[:, i, :, :].rearrange("p a n -> p (a n)"), k.ident[:, :]))
            yield
            tb = k.bank[0][:, 0:3 * P].rearrange("p (i t) -> p i t", i=3)
            v(p).done(V.tensor_copy(turned[0:64, :, :], tb[0:64, :, 0:64]))
            m = evacuated(k, 0, v(p).done(V.tensor_copy(turned[64:P, :, :], tb[64:P, :, 64:P])))
            yield
            for cut in range(4):
                ts = slice(cut * 16, cut * 16 + 16)
                v(m).done(V.tensor_tensor(z.rowhot[:, ts, :], rep(turned[:, 0, ts], 2, P), rep(iota128[:, :], 1, 16), ALU.is_equal))
                yield
            o2 = v(m).done(V.tensor_tensor(onehot[:, :, :], rep(turned[:, 1, :], 2, EB), rep(iota128[:, 0:EB], 1, 64),
                                           ALU.is_equal))
            yield
            for part in range(3):
                if part:
                    rest = turned[:, 2, :] if part == 1 else left_[:, 0, :]
                    m = v(m).done(V.tensor_tensor(left_[:, part - 1, :], rest, parts[:, part - 1, :], ALU.subtract))
                m = v(m).done(V.tensor_copy(parts[:, part, :], left_[:, part - 1, :] if part else turned[:, 2, :]))
                mul = g(o2, m).done(nc.gpsimd.tensor_tensor(z.blockhot[:, part, :, :], onehot[:, :, :],
                                                            rep(parts[:, part, :], 2, EB), ALU.mult))
                yield
            v(mul)
            o2 = mul
            z.chosen, z.ready = o2, ht

        def apply(tile, z):
            chosen_, ht = (z.chosen, z.ready)
            for jb in range(EB // 4):
                bank = 3 + jb % 2
                pe(ht, k.drained.get(bank))
                for j in range(4 * jb, 4 * jb + 4):
                    p = project(k, bank, [down[:, kt, j, :] for kt in range(KC)], [z.hT[:, kt, :] for kt in range(KC)],
                                None, col=(j % 4) * P)
                ga = evacuated(k, bank, s(p).done(A.activation(
                    act[:, 4 * jb:4 * jb + 4, :].rearrange("p j t -> p (j t)"), k.bank[bank][:, :], ACT.Gelu)))
                yield
            per = 512 // EB
            for tg in range(P // per):
                bank = 6 + tg % 2
                pe(chosen_, k.drained.get(bank))
                for u in range(per):
                    tok = tg * per + u
                    ps = slice(0, 64) if tok < 64 else slice(64, P)
                    for part in range(3):
                        p = pe.done(nc.tensor.matmul(k.bank[bank][:, u * EB:(u + 1) * EB], z.rowhot[ps, tok % 64, :],
                                                     z.blockhot[ps, part, tok % 64, :], start=part == 0, stop=part == 2))
                yield
                a_ = act[:, :, tg * per:(tg + 1) * per].rearrange("p j t -> p t j")
                w = evacuated(k, bank, v(p, ga).done(V.tensor_tensor(
                    a_, a_, k.bank[bank][:, :].rearrange("p (t n) -> p t n", n=EB), ALU.mult)))
            yield
            m = project(k, 5, [act[:, j, :] for j in range(EB)], [up[:, j, :] for j in range(EB)], w)
            k.s(m)
            yield
            m = evacuated(k, 5, v(m).done(V.tensor_tensor(z.x[:, 0, :], z.x[:, 0, :], k.bank[5][:, 0:C], ALU.add)))
            z.stored = z.load(1, by_token(io["out"])[bass.ds(tile * P, P), :], z.x[:, 0, :], m)

        PACE = (1, 3)
        together(choose(0, slots[0]))
        k.fence()
        a, b = slots
        a.chosen = a.ready = None
        with nc.Fori(0, TILES // 2 - 1) as pair:
            together(apply(pair * 2, a), choose(pair * 2 + 1, b), pace=PACE)
            k.sp(a.stored)
            together(apply(pair * 2 + 1, b), choose(pair * 2 + 2, a), pace=PACE)
            k.fence()
            a.chosen = a.ready = None
        together(apply(TILES - 2, a), choose(TILES - 1, b), pace=PACE)
        together(apply(TILES - 1, b))
        k.fence()


def build(nc, io):
    dram = lambda n, sh, dt=F32: nc.dram_tensor("keep_" + n, sh, dt, kind="Internal").ap()
    dr = {n: dram(n, (B, T, C)) for n in ("r", "k", "v", "g", "wkv", "x1", "x2", "x3")}
    dr |= {n: dram(n, (B, P, IB * T)) for n in ("xc", "zs", "dt", "dx", "ys")}
    dr["bc"] = dram("bc", (B, P, 3 * T), BF16)
    with ExitStack() as ctx:
        ctx.enter_context(nc.allow_non_contiguous_dma("small vectors and head slices go to partitions"))
        k = Core(nc, ctx)
        constants(k)
        keep = {"stats": k.sbuf(ctx, "bn_statistics", [P, KC, B * 6])}
        todo = [lambda: mixer_inputs(k, io, dr), lambda: mixer_scan(k, io, dr), lambda: layer0_rest(k, io, dr),
                lambda: ssm_inputs(k, io, dr), lambda: ssm_scan(k, io, dr),
                lambda: layer1_attention(k, io, dr, keep), lambda: product_keys(k, io, dr, keep)]
        for stage in todo:
            stage()


def laid_out(i):
    c = np.ascontiguousarray
    a = {n: c(np.asarray(x)) for n, x in i.items()}
    out = {n: a[n] for n in (
        "x", "ctx_1024", "L0_attn_b_r", "L0_attn_b_k", "L0_attn_b_v", "L0_attn_b_g", "L0_attn_b_o", "L0_attn_decay",
        "L0_attn_eta", "L0_attn_gn_weight", "L0_attn_gn_bias", "L0_ffn_gate_b", "L0_ffn_wi_b", "L0_ffn_wo_b",
        "L1_attn_conv_w", "L1_attn_conv_b", "L1_attn_A_log", "L1_attn_D_param", "L1_attn_dt_b", "L1_attn_norm_w",
        "L1_ffn_bn_gamma", "L1_ffn_bn_beta", "L1_ffn_w_q")}
    for n in "rkvgo":
        out["w_" + n] = c(a["L0_attn_W_" + n].T)
    for n in "rkvg":
        out["time_mix_" + n] = c(a["L0_attn_time_mix_" + n].reshape(C))
    for n, m in (("wq", "W_q"), ("wk", "W_k"), ("wv", "W_v"), ("bv", "b_v"), ("wo", "W_o"), ("bo", "b_o")):
        out["l0x_" + n] = a["L0_xattn_" + m]
    for n, m in (("wq", "Wq"), ("bq", "b_q"), ("wk", "Wk"), ("bk", "b_k"), ("wv", "Wv"), ("bv", "b_v"), ("wo", "Wo"),
                 ("bo", "b_o")):
        out["l1x_" + n] = a["L1_xattn_" + m]
    out["gate_wT"] = c(a["L0_ffn_gate_W"].T)
    out["lora_aT"] = c(a["L0_ffn_lora_A"].reshape(E * R, C).T)
    out["lora_bT"] = c(a["L0_ffn_lora_B"].transpose(0, 2, 1).reshape(E * R, F))
    out["wiT"], out["woT"] = c(a["L0_ffn_wi_W"].T), c(a["L0_ffn_wo_W"].T)
    out["in_projT"], out["out_projT"] = c(a["L1_attn_in_proj_w"].T), c(a["L1_attn_out_proj_w"].T)
    out["b_wT"], out["c_wT"], out["dt_wT"] = (c(a["L1_attn_" + n].T) for n in ("B_w", "C_w", "dt_w"))
    out["keysT"] = c(a["L1_ffn_keys_p"].transpose(3, 2, 0, 1).reshape(KD, 2 * NH, NK))
    cut = lambda w: w[:NK * NK].reshape(NK, 2, NK // 2, C)
    out["downT"] = c(cut(a["L1_ffn_down"]).transpose(3, 2, 1, 0).reshape(C, NK * NK))
    out["upT"] = c(cut(a["L1_ffn_up"]).transpose(1, 0, 2, 3).reshape(P, NK // 2, C))
    return out


def kernel(**inputs):
    import concourse.bacc as bacc
    from concourse.bass_utils import run_bass_kernel_spmd

    arrays = laid_out(inputs)
    nc = bacc.Bacc("TRN2", target_bir_lowering=False, num_devices=1)
    io = {n: nc.dram_tensor(n, a.shape, mybir.dt.from_np(a.dtype), kind="ExternalInput").ap() for n, a in arrays.items()}
    io["out"] = nc.dram_tensor("out", (B, T, C), F32, kind="ExternalOutput").ap()
    build(nc, io)
    r = run_bass_kernel_spmd(nc, [arrays], core_ids=[0])
    return r.results[0]["out"]
```

```python
import math
from contextlib import ExitStack

import numpy as np
import concourse.bass as bass
from concourse import mybir

ALU = mybir.AluOpType
ACT = mybir.ActivationFunctionType
AX = mybir.AxisListType
F32 = mybir.dt.float32
BF16 = mybir.dt.bfloat16
U32 = mybir.dt.uint32

P = 128
B, T, C = 16, 256, 256
NT = T // P
KC = C // P
H, D = 16, 16
E, R, F = 8, 4, 1024
INNER, N = 512, 64
IB = INNER // P
KW = 4
NH, NK, TK, KD = 8, 64, 8, 128
NEG = -1.0e30
RING = 2
QUEUES = 20


def rep(ap, axis, n):
    a = ap.unsqueeze(axis)
    shape = list(a.shape)
    shape[axis] = n
    return a.broadcast_to(shape)


class Lane:
    STEP = 1

    def __init__(self, eng, sem):
        self.eng, self.sem, self.count, self.seen = eng, sem, 0, {}

    def __call__(self, *marks):
        for m in marks:
            if m is not None and self.seen.get(m[0].name, 0) < m[1]:
                self.eng.wait_ge(m[0], m[1])
                self.seen[m[0].name] = m[1]
        return self

    def done(self, ins):
        ins.then_inc(self.sem, self.STEP)
        self.count += self.STEP
        return (self.sem, self.count)

    @property
    def last(self):
        return (self.sem, self.count) if self.count else None


class Queue(Lane):
    STEP = 16

    def __init__(self, lane, sem):
        self.lane, self.sem, self.count = lane, sem, 0

    def __call__(self, *marks):
        self.lane(*marks)
        return self


class Core:

    def __init__(self, nc, ctx):
        self.nc, self.ctx = nc, ctx
        sem = lambda n: ctx.enter_context(nc.semaphore(n))
        self.v = Lane(nc.vector, sem("vector_done"))
        self.s = Lane(nc.scalar, sem("scalar_done"))
        self.pe = Lane(nc.tensor, sem("tensor_done"))
        self.g = Lane(nc.gpsimd, sem("gpsimd_done"))
        self.sp = Lane(nc.sync, sem("sync_done"))
        self.queues = [Queue(self.sp, sem(f"dma_done{n}")) for n in range(QUEUES)]
        self.states = {n: sem("states_" + n) for n in ("b", "c", "copied", "decay", "input", "scan", "weighed", "summed")}
        self.bank = [ctx.enter_context(nc.psum_tensor(f"bank{n}", [P, 512], F32)) for n in range(8)]
        self.drained = {}

    def fence(self):
        lanes = [self.v, self.s, self.pe, self.g, self.sp]
        for lane in lanes:
            lane(lane.last)
        self.sp(*[q.last for q in self.queues])
        numbers = sorted([x.sem.num for x in lanes + self.queues] + [x.num for x in self.states.values()])
        self.nc.all_engine_barrier(sems_to_clear=range(numbers[0], numbers[-1] + 1))
        for x in lanes:
            x.count, x.seen = 0, {}
        for q in self.queues:
            q.count = 0
        self.drained = {}

    def sbuf(self, scope, name, shape, dt=F32):
        return scope.enter_context(self.nc.sbuf_tensor(name, shape, dt))


class Slot:

    def __init__(self, k, scope, tag, n, of=2):
        self.k, self.scope, self.tag, self.n = k, scope, f"{tag}{n}_", n
        self.banks = list(range(8))[n * 8 // of:(n + 1) * 8 // of]
        self.queues = k.queues[n * QUEUES // of:(n + 1) * QUEUES // of]
        self.ln_stats = self.sb("ln_stats", [P, NT, 6])
        self.ln_mv = self.sb("ln_mv", [P, NT, 2])

    def sb(self, name, shape, dt=F32):
        return self.k.sbuf(self.scope, self.tag + name, shape, dt)

    def load(self, q, dst, src, *ready):
        return self.queues[q](*ready).done(self.k.nc.sync.dma_start(dst, src))


def together(*passes, pace=(1, 1, 1, 1), lag=0):
    left, rounds = dict(enumerate(passes)), 0
    while left:
        rounds += 1
        for n in [n for n in left if rounds > n * lag]:
            for _ in range(pace[n]):
                if n in left and next(left[n], left) is left:
                    del left[n]


def sequences(k, slots, one, lag=0):
    with k.nc.Fori(0, B // len(slots)) as group:
        together(*(one(group * len(slots) + n, slot) for n, slot in enumerate(slots)), lag=lag)
        k.fence()


def staggered(k, slots, ahead, first, second, pace=(1, 1, 1)):
    a, b = slots
    together(ahead(0, a))
    k.fence()
    together(first(0, a), ahead(1, b))
    k.fence()
    with k.nc.Fori(0, B // 2 - 1) as pair:
        together(second(pair * 2, a), first(pair * 2 + 1, b), ahead(pair * 2 + 2, a), pace=pace)
        k.fence()
        together(second(pair * 2 + 1, b), first(pair * 2 + 2, a), ahead(pair * 2 + 3, b), pace=pace)
        k.fence()
    together(second(B - 2, a), first(B - 1, b), pace=pace)
    k.fence()
    together(second(B - 1, b))
    k.fence()


def constants(k):
    nc, g, v = k.nc, k.g, k.v
    k.ident = k.sbuf(k.ctx, "ident", [P, P])
    k.identb = k.sbuf(k.ctx, "identb", [P, P], BF16)
    k.iota64 = k.sbuf(k.ctx, "iota64", [P, 64])
    m = g().done(nc.gpsimd.memset(k.ident[:, :], 0.0))
    m = g(m).done(nc.gpsimd.affine_select(out=k.ident[:, :], in_=k.ident[:, :], compare_op=ALU.not_equal,
                                          fill=1.0, base=0, pattern=[[-1, P]], channel_multiplier=1))
    v(m).done(nc.vector.tensor_copy(k.identb[:, :], k.ident[:, :]))
    g().done(nc.gpsimd.iota(k.iota64[:, :], [[1, 64]], base=0, channel_multiplier=0,
                            allow_small_or_imprecise_dtypes=True))
    k.fence()


def layer_norm(k, z, x, h, ready, eps=1e-5, tiles=NT):
    V, v, s = k.nc.vector, k.v, k.s
    st, mv = z.ln_stats, z.ln_mv
    for t in range(tiles):
        m = v(ready).done(V.bn_stats(st[:, t, :], x[:, t, :]))
    yield
    for t in range(tiles):
        m = v(m).done(V.bn_aggr(mv[:, t, :], st[:, t, :]))
    yield
    m = v(m).done(V.tensor_scalar(mv[:, 0:tiles, 1:2], mv[:, 0:tiles, 1:2], eps, None, ALU.add))
    m = s(m).done(k.nc.scalar.activation(mv[:, 0:tiles, 1:2], mv[:, 0:tiles, 1:2], ACT.Sqrt))
    yield
    m = v(m).done(V.reciprocal(mv[:, 0:tiles, 1:2], mv[:, 0:tiles, 1:2]))
    yield
    for t in range(tiles):
        r = v(m).done(V.tensor_scalar(h[:, t, :], x[:, t, :], mv[:, t, 0:1], mv[:, t, 1:2],
                                      ALU.subtract, ALU.mult))
    yield
    return r


def turn(k, src, bank, ready, tiles=NT, blocks=KC):
    k.pe(ready, k.drained.get(bank))
    for kt in range(blocks):
        for t in range(tiles):
            o = (kt * tiles + t) * P
            m = k.pe.done(k.nc.tensor.transpose(k.bank[bank][:, o:o + P], src[:, t, kt * P:(kt + 1) * P],
                                                k.ident[:, :]))
    return m


def evacuated(k, bank, mark):
    k.drained[bank] = mark
    return mark


def project(k, bank, lhsT, rhs, ready, col=0, stop=True):
    n = rhs[0].shape[-1]
    k.pe(ready, k.drained.get(bank))
    for i, (a, b) in enumerate(zip(lhsT, rhs)):
        m = k.pe.done(k.nc.tensor.matmul(k.bank[bank][0:a.shape[-1], col:col + n], a, b,
                                         start=(i == 0), stop=stop and i == len(rhs) - 1))
    return m


def load_weight(k, tile, dram):
    return k.queues[0]().done(k.nc.sync.dma_start(tile, dram))


def row_to_all(dram, n):
    return dram.unsqueeze(0).broadcast_to([n, dram.shape[0]])


def mixer_inputs(k, io, dr):
    nc, v, s, pe = k.nc, k.v, k.s, k.pe
    V, A = nc.vector, nc.scalar
    with ExitStack() as scope:
        sb = lambda n, sh, dt=F32: k.sbuf(scope, "mi_" + n, sh, dt)
        w = sb("w", [P, 4, KC, C])
        bias = sb("bias", [P, 4, C])
        mixw, unmix = sb("mixw", [P, 4, KC]), sb("unmix", [P, 4, KC])
        slots = [Slot(k, scope, "mi", n, of=4) for n in range(4)]
        for z in slots:
            z.x, z.h = z.sb("x", [P, NT, C]), z.sb("h", [P, NT, C])
            z.hT = z.sb("hT", [P, KC, T + 1])
            z.tmp, z.mix = z.sb("tmp", [P, 4, KC, T]), z.sb("mix", [P, 4, KC, T])
            z.out, z.res = z.sb("out", [P, 4, NT, C]), z.sb("res", [P, 4, NT, C])
            z.sq, z.n2 = z.sb("sq", [P, 2 * NT * C]), z.sb("n2", [P, 2 * NT * H])
            v().done(V.memset(z.hT[:, :, 0:1], 0.0))
        for i, c in enumerate("rkvg"):
            load_weight(k, w[:, i, :, :], io[f"w_{c}"].rearrange("(k p) n -> p k n", p=P))
            load_weight(k, bias[:, i, :], row_to_all(io[f"L0_attn_b_{c}"], P))
            m = load_weight(k, mixw[:, i, :], io[f"time_mix_{c}"].rearrange("(k p) -> p k", p=P))
        v(m).done(V.tensor_scalar(unmix[:, :, :], mixw[:, :, :], -1.0, 1.0, ALU.mult, ALU.add))
        k.fence()

        def one(b, z):
            m = z.load(0, z.x[:, :, :], io["x"][b].rearrange("(t p) c -> p t c", p=P))
            m = yield from layer_norm(k, z, z.x, z.h, m)
            m = turn(k, z.h, z.banks[0], m)
            yield
            m = evacuated(k, z.banks[0], v(m).done(V.tensor_copy(
                z.hT[:, :, 1:T + 1], k.bank[z.banks[0]][:, :].rearrange("p (k t) -> p k t", k=KC))))
            yield
            for i in range(4):
                bank = z.banks[i % 2]
                for kt in range(KC):
                    a = s(m).done(A.activation(z.tmp[:, i, kt, :], z.hT[:, kt, 0:T], ACT.Copy,
                                               scale=unmix[:, i, kt:kt + 1]))
                yield
                for kt in range(KC):
                    a = v(a).done(V.scalar_tensor_tensor(z.mix[:, i, kt, :], z.hT[:, kt, 1:T + 1],
                                                         mixw[:, i, kt:kt + 1], z.tmp[:, i, kt, :],
                                                         ALU.mult, ALU.add))
                for t in range(NT):
                    p = project(k, bank, [z.mix[:, i, kt, t * P:(t + 1) * P] for kt in range(KC)],
                                [w[:, i, kt, :] for kt in range(KC)], a, col=t * C)
                yield
                r = evacuated(k, bank, v(p).done(V.tensor_tensor(
                    z.out[:, i, :, :], two(k.bank[bank][:, :]), rep(bias[:, i, :], 1, NT), ALU.add)))
                if i == 0:
                    r_act = s(r).done(A.activation(z.res[:, 0, :, :], z.out[:, 0, :, :], ACT.Sigmoid))
                yield
            g_act = s(r).done(A.activation(z.res[:, 3, :, :], z.out[:, 3, :, :], ACT.Silu))
            kv = z.out[:, 1:3, :, :].rearrange("p a t c -> p (a t c)")
            a = v(r).done(V.tensor_tensor(z.sq[:, :], kv, kv, ALU.mult))
            yield
            a = v(a).done(V.tensor_reduce(z.n2[:, :], z.sq[:, :].rearrange("p (n d) -> p n d", d=D), AX.X, ALU.add))
            yield
            a = v(a).done(V.tensor_scalar(z.n2[:, :], z.n2[:, :], 1e-24, None, ALU.max))
            a = s(a).done(A.activation(z.n2[:, :], z.n2[:, :], ACT.Sqrt))
            yield
            a = v(a).done(V.reciprocal(z.n2[:, :], z.n2[:, :]))
            yield
            a = v(a).done(V.tensor_tensor(
                z.res[:, 1:3, :, :].rearrange("p a t c -> p (a t c)").rearrange("p (n d) -> p n d", d=D),
                kv.rearrange("p (n d) -> p n d", d=D), rep(z.n2[:, :], 2, D), ALU.mult))
            for i, c in enumerate("rkvg"):
                z.load(1, dr[c][b].rearrange("(t p) c -> p t c", p=P), z.res[:, i, :, :], a, r_act, g_act)

        sequences(k, slots, one, lag=2)


class Context:

    def __init__(self, k, io, dr, scope):
        nc, v = k.nc, k.v
        self.k, self.io, self.dr = k, io, dr
        sb = lambda n, sh: k.sbuf(scope, "cx_" + n, sh)
        self.c, self.cT = sb("c", [P, NT, C]), sb("cT", [P, KC, T])
        self.w, self.bias = sb("w", [P, 4, KC, C]), sb("bias", [P, 3, C])
        self.ones = sb("ones", [P, P])
        self.keys = [sb("keys", [P, NT, C]), self.c]
        self.values = sb("values", [P, 2, NT, H, D + 1])
        v().done(nc.vector.memset(self.ones[:, :], 1.0))
        v().done(nc.vector.memset(self.values[:, :, :, :, :], 1.0))
        zero = v().done(nc.vector.memset(self.bias[:, :, :], 0.0))
        for n, name in enumerate(("l0x_wk", "l0x_wv", "l1x_wk", "l1x_wv")):
            load_weight(k, self.w[:, n, :, :], kp(io[name]))
            bias = name.replace("w", "b")
            if n:
                k.queues[1](zero).done(nc.sync.dma_start(self.bias[0:1, n - 1, :], io[bias].unsqueeze(0)))

    def run(self, b):
        k, nc = self.k, self.k.nc
        s, copy = k.s, k.nc.scalar.copy
        m = k.queues[2]().done(nc.sync.dma_start(self.c[:, :, :], rows(self.io["ctx_1024"][b])))
        yield
        m = turn(k, self.c, 0, m)
        yield
        cT = evacuated(k, 0, s(m).done(copy(self.cT[:, :, :].rearrange("p k t -> p (k t)"), k.bank[0][:, :])))
        yield

        def projected(n):
            for t in range(NT):
                lhsT = [self.cT[:, kt, t * P:(t + 1) * P] for kt in range(KC)]
                rhs = [self.w[:, n, kt, :] for kt in range(KC)]
                if n:
                    lhsT, rhs = lhsT + [self.ones[:, :]], rhs + [self.bias[:, n - 1, :]]
                m = project(k, 1 + n, lhsT, rhs, cT, col=t * C)
            return m

        m = projected(0)
        yield
        for n in range(4):
            following = projected(n + 1) if n < 3 else None
            layer, bank = n // 2, k.bank[1 + n]
            if n % 2 == 0:
                dst, src = self.keys[layer][:, :, :].rearrange("p t c -> p (t c)"), bank[:, :]
                out, tile = self.dr[f"k{layer}"], self.keys[layer][:, :, :]
            else:
                dst = self.values[:, layer, :, :, 0:D].rearrange("p t h d -> p (t h) d")
                src = bank[:, :].rearrange("p (n d) -> p n d", d=D)
                out, tile = self.dr[f"v{layer}"], self.values[:, layer, :, :, :].rearrange("p t h d -> p t (h d)")
            m = evacuated(k, 1 + n, s(m).done(copy(dst, src)))
            k.queues[3](m).done(nc.sync.dma_start(rows(out[b]), tile))
            m = following
            yield


def mixer_scan(k, io, dr):
    nc, v, s, g = k.nc, k.v, k.s, k.g
    V, A = nc.vector, nc.scalar
    HP = H // 2
    max_norm = math.sqrt(D) * 2.0
    UN = T // B
    STATES = 4
    with ExitStack() as scope:
        sb = lambda n, sh, dt=F32: k.sbuf(scope, "ms_" + n, sh, dt)
        KR = sb("KR", [P, T + 1, 2, 2, D])
        VV = sb("VV", [P, T, 2, D])
        PR = sb("PR", [P, T + 1, 2, 2 * D])
        FF = sb("FF", [P, T + 1, 2])
        CO = sb("CO", [P, T, 2, 2])
        S = sb("S", [P, STATES, 2, D, D])
        prod, outer = sb("prod", [P, 2, D, D]), sb("outer", [P, 2, D, D])
        rprod, rsum = sb("rprod", [P, 2 * D, D]), sb("rsum", [P, 2 * D, D])
        context = Context(k, io, dr, scope)
        pred_err, ek = sb("prederr", [P, 2, 2 * D]), sb("ek", [P, 2, D])
        Q, terms = sb("Q", [P, 2, 2 * D]), sb("terms", [P, 3, 2])
        R4, N2 = sb("R4", [P, 4]), sb("N2", [P, 2])
        root, inv, fdec = sb("root", [P, 2]), sb("inv", [P, 2]), sb("fdec", [P, 2])
        dec, et, et32, dec2 = sb("dec", [P, 2]), sb("et", [P, 2]), sb("et32", [P, 2, D]), sb("dec2", [P, 2])
        cst, one32 = sb("cst", [P, 2, 2]), sb("one32", [P, 2, D])
        stat = sb("stat", [P, 4, 2])
        v().done(V.memset(KR[:, 0, 1, :, :], 0.0))
        v().done(V.memset(KR[:, T, 0, :, :], 0.0))
        v().done(V.memset(S[:, 0, :, :, :], 0.0))
        v().done(V.memset(FF[:, 0, :], 1.0))
        v().done(V.memset(N2[:, :], 0.0))
        z = v().done(V.memset(one32[:, :, :], 1.0))

        def load_steps(part):
            for b in range(B):
                ps, tokens = slice(b * HP, (b + 1) * HP), bass.ds(part * UN, UN)
                for q, (name, dst) in enumerate((("k", KR[ps, tokens, 0, :, :]), ("r", KR[ps, bass.ds(part * UN + 1, UN), 1, :, :]),
                                                 ("v", VV[ps, tokens, :, :])), 5):
                    k.queues[q]().done(nc.sync.dma_start(dst.rearrange("h t e d -> h t (e d)"),
                                                         dr[name][b][tokens].rearrange("t (h x) -> h t x", h=HP)))

        load_steps(0)
        for b in range(B):
            ps = slice(b * HP, (b + 1) * HP)
            k.queues[0]().done(nc.sync.dma_start(dec[ps, :], io["L0_attn_decay"].rearrange("(h e) a b -> h (e a b)", e=2)))
            m = k.queues[0]().done(nc.sync.dma_start(et[ps, :], io["L0_attn_eta"].rearrange("(h e) a b -> h (e a b)", e=2)))
        a = s(m).done(A.activation(dec[:, :], dec[:, :], ACT.Sigmoid))
        a = s().done(A.activation(et[:, :], et[:, :], ACT.Sigmoid))
        v(a, z).done(V.tensor_tensor(et32[:, :, :], one32[:, :, :], rep(et[:, :], 2, D), ALU.mult))
        v().done(V.tensor_tensor(dec2[:, :], dec[:, :], dec[:, :], ALU.mult))
        c2 = v().done(V.tensor_tensor(cst[:, 0, :], dec[:, :], et[:, :], ALU.mult))
        c2 = v(c2).done(V.tensor_scalar(cst[:, 0, :], cst[:, 0, :], -2.0, None, ALU.mult))
        v().done(V.tensor_tensor(cst[:, 1, :], et[:, :], et[:, :], ALU.mult))
        a = v().done(V.memset(CO[:, :, 0, :], 1.0))
        a = v(a).done(V.tensor_tensor(CO[:, :, 0, :], CO[:, :, 0, :], rep(cst[:, 0, :], 1, T), ALU.mult))
        k.fence()
        def r_product(t, state, ready):
            m = g(ready).done(nc.gpsimd.tensor_tensor(rprod[:, :, :].rearrange("p (e i) j -> p e i j", e=2), state,
                                                      rep(KR[:, t, 1, :, :], 2, D), ALU.mult))
            src, dst, width = rprod, rsum, D // 2
            while width:
                out = dst[:, :, 0:width] if width > 1 else PR[:, t, 1, :].unsqueeze(2)
                read = m = g(m).done(nc.gpsimd.tensor_tensor(out, src[:, :, 0:width], src[:, :, width:2 * width], ALU.add))
                src, dst, width = dst, src, width // 2
            return read

        with nc.Fori(0, T // UN) as it:
            f_ready, n_ready = None, None
            body = bass.ds(it * UN, UN)
            kk = PR[:, body, 0, :].rearrange("p t (e d) -> p t e d", e=2)
            a = v().done(V.tensor_tensor(kk, KR[:, body, 0, :, :], KR[:, body, 0, :, :], ALU.mult))
            a = v(a).done(V.tensor_reduce(CO[:, body, 1, :], kk, AX.X, ALU.add))
            v(a).done(V.tensor_tensor(CO[:, body, 1, :], CO[:, body, 1, :], rep(cst[:, 1, :], 1, UN), ALU.mult))
            v(v.last)
            now, state, read = S[:, 0, :, :, :], None, {}
            work = context.run(it)
            for u in range(UN):
                t = it * UN + u
                key = KR[:, t, 0, :, :]
                read[u] = r_product(t, now, state)
                m = v(state).done(V.tensor_tensor(prod[:, :, :, :], now, rep(key, 2, D), ALU.mult))
                if f_ready is not None:
                    f_ready = v(f_ready).done(V.reciprocal(inv[:, :], root[:, :]))
                m = v(m).done(V.tensor_reduce(PR[:, t, 0, :], prod[:, :, :, :].rearrange("p e i j -> p (e i) j"),
                                              AX.X, ALU.add))
                if f_ready is not None:
                    f_ready = v(f_ready).done(V.tensor_scalar(FF[:, t, :], inv[:, :], max_norm, 1.0, ALU.mult, ALU.min))
                f_done = f_ready
                tn = v(n_ready).done(V.scalar_tensor_tensor(terms[:, 2, :], N2[:, :], max_norm * max_norm, dec2[:, :],
                                                            ALU.min, ALU.mult))
                m = v(m, f_ready).done(V.tensor_tensor(
                    pred_err[:, 0, :].rearrange("p (e i) -> p e i", e=2),
                    PR[:, t, 0, :].rearrange("p (e i) -> p e i", e=2), rep(FF[:, t, :], 2, D), ALU.mult))
                fd = v(f_ready).done(V.tensor_tensor(fdec[:, :], FF[:, t, :], dec[:, :], ALU.mult))
                e_ = v().done(V.tensor_tensor(ek[:, :, :], key, et32[:, :, :], ALU.mult))
                m = v(m).done(V.tensor_tensor(pred_err[:, 1, :], pred_err[:, 0, :],
                                              VV[:, t, :, :].rearrange("p e i -> p (e i)"), ALU.subtract))
                q = v(m).done(V.tensor_tensor(Q[:, :, :], pred_err[:, :, :], rep(pred_err[:, 1, :], 1, 2), ALU.mult))
                o = v(e_).done(V.tensor_tensor(outer[:, :, :, :], rep(pred_err[:, 1, :].rearrange("p (e i) -> p e i", e=2), 3, D),
                                               rep(ek[:, :, :], 2, D), ALU.mult))
                q = v(q).done(V.tensor_reduce(R4[:, :], Q[:, :, :].rearrange("p a (e i) -> p (a e) i", e=2), AX.X, ALU.add))
                after = S[:, (u + 1) % STATES, :, :, :]
                for e in range(2):
                    state = v(o, fd, read.get(u + 1 - STATES)).done(V.scalar_tensor_tensor(
                        after[:, e, :, :].rearrange("p i j -> p (i j)"), now[:, e, :, :].rearrange("p i j -> p (i j)"),
                        fdec[:, e:e + 1], outer[:, e, :, :].rearrange("p i j -> p (i j)"), ALU.mult, ALU.subtract))
                    if e == 0:
                        q = v(q).done(V.tensor_tensor(terms[:, 0:2, :].rearrange("p a e -> p (a e)"), R4[:, :],
                                                      CO[:, t, :, :].rearrange("p a e -> p (a e)"), ALU.mult))
                now = after
                n_ready = v(q, tn).done(V.tensor_reduce(N2[:, :], terms[:, :, :].rearrange("p a e -> p e a"), AX.X, ALU.add))
                q = v(n_ready).done(V.tensor_scalar(inv[:, :], N2[:, :], 1e-16, None, ALU.max))
                f_ready = s(q).done(A.activation(root[:, :], inv[:, :], ACT.Sqrt))
                next(work, None)
                if u == 0:
                    load_steps((it + 1) % B)
                if u == UN - 1:
                    wkv = PR[:, body, 1, :].rearrange("p t (e d) -> p t e d", e=2)
                    g(read[u], f_done).done(nc.gpsimd.tensor_tensor(wkv, wkv, rep(FF[:, body, :], 3, D), ALU.mult))
            r = v(f_ready).done(V.reciprocal(inv[:, :], root[:, :]))
            v(r).done(V.tensor_scalar(FF[:, it * UN + UN, :], inv[:, :], max_norm, 1.0, ALU.mult, ALU.min))
            for _ in work:
                pass
            k.fence()
        m = r_product(T, S[:, 0, :, :, :], None)
        wkv = PR[:, 1:T + 1, 1, :].rearrange("p t (e d) -> p t e d", e=2)
        m = g(m).done(nc.gpsimd.tensor_tensor(wkv[:, T - 1, :, :], wkv[:, T - 1, :, :], rep(FF[:, T, :], 2, D), ALU.mult))
        m = v(m).done(V.tensor_reduce(stat[:, 0, :], wkv.rearrange("p t e d -> p e t d"), AX.XY, ALU.add))
        mean, negated, spread, rstd = (stat[:, i, :] for i in range(4))
        m = v(m).done(V.tensor_scalar(negated, mean, -1.0 / (T * D), None, ALU.mult))
        for e in range(2):
            m = s(m).done(A.activation(KR[:, 0:T, 0, e, :], wkv[:, :, e, :], ACT.Square, bias=negated[:, e:e + 1],
                                       accum_out=spread[:, e:e + 1]))
        m = v(m).done(V.tensor_scalar(spread, spread, 1.0 / (T * D), 1e-5, ALU.mult, ALU.add))
        m = s(m).done(A.activation(rstd, spread, ACT.Sqrt))
        m = v(m).done(V.reciprocal(rstd, rstd))
        shift = v(m).done(V.tensor_tensor(mean, negated, rstd, ALU.mult))
        m = v(m).done(V.tensor_scalar(VV[:, :, 0, :], wkv[:, :, 0, :], negated[:, 0:1], rstd[:, 0:1], ALU.add, ALU.mult))
        m2 = s(shift).done(A.activation(VV[:, :, 1, :], wkv[:, :, 1, :], ACT.Identity, scale=rstd[:, 1:2], bias=mean[:, 1:2]))
        with nc.allow_non_contiguous_dma("heads of a sequence come from partitions"):
            for b in range(B):
                k.queues[1](m, m2).done(nc.sync.dma_start(dr["wkv"][b].rearrange("t (h x) -> h t x", h=HP),
                                                      VV[b * HP:(b + 1) * HP, :, :, :].rearrange("h t e d -> h t (e d)")))
        k.fence()


class Attention:
    Q_PARTS, K_PARTS = (0, 0, 0, 1, 1, 1, 2, 2), (0, 1, 2, 0, 1, 2, 0, 1)

    def __init__(self, k, io, scope, tag, causal, slots):
        nc, self.k, self.causal = k.nc, k, causal
        sb = lambda n, sh, dt=F32: k.sbuf(scope, "at_" + tag + n, sh, dt)
        self.w = {c: sb("w" + c, [P, KC, C]) for c in "qo"}
        self.bq, self.bo = sb("bq", [P, C]), sb("bo", [P, C])
        for z in slots:
            z.kf, z.qf = z.sb("kf", [P, NT, C]), z.sb("qf", [P, NT, C])
            z.kp, z.qp = (z.sb(n, [P, NT * H, 8, D], BF16) for n in ("kp", "qp"))
            z.kT, z.qT = (z.sb(n, [P, H, T], BF16) for n in ("kT", "qT"))
            z.va = z.sb("va", [P, NT, H, D + 1])
            z.nmax = z.sb("nmax", [P, NT, P])
            z.nmaxT = z.sb("nmaxT", [P, T], BF16)
            z.pT = z.sb("pT", [P, RING, NT, 2, T])
            z.rden = z.sb("rden", [P, NT, H])
            z.att, z.attT = z.sb("att", [P, NT, C]), z.sb("attT", [P, KC, T])
        g, v = k.g, k.v
        for z in slots:
            g().done(nc.gpsimd.memset(z.nmax[:, :, :], 0.0))
        zero = v().done(nc.vector.memset(self.bq[:, :], 0.0))
        for c in "qo":
            load_weight(k, self.w[c][:, :, :], io[tag + "w" + c].rearrange("(k p) n -> p k n", p=P))
        if tag + "bq" in io:
            k.queues[5](zero).done(nc.sync.dma_start(self.bq[:, :], row_to_all(io[tag + "bq"], P)))
        load_weight(k, self.bo[:, :], row_to_all(io[tag + "bo"], P))
        if causal:
            self.mask, self.maskT = sb("mask", [P, NT, T], BF16), sb("maskT", [P, NT, T], BF16)
            m1 = g().done(nc.gpsimd.memset(self.mask[:, :, :], 0.0))
            m2 = g().done(nc.gpsimd.memset(self.maskT[:, :, :], 0.0))
            for t in range(NT):
                g(m1).done(nc.gpsimd.affine_select(out=self.mask[:, t, :], in_=self.mask[:, t, :], compare_op=ALU.is_gt,
                                                   fill=NEG, base=t * P, pattern=[[-1, T]], channel_multiplier=1))
                m = g(m2).done(nc.gpsimd.affine_select(out=self.maskT[:, t, :], in_=self.maskT[:, t, :], compare_op=ALU.is_gt,
                                                       fill=NEG, base=-t * P, pattern=[[1, T]], channel_multiplier=-1))
            v(m).done(nc.vector.memset(self.mask[0:1, 0, 0:1], 0.0))
            v(m).done(nc.vector.memset(self.maskT[0:1, 0, 0:1], 0.0))

    def split(self, lane, x, parts, slots, ready):
        x = x[:, :, :].rearrange("p t (h d) -> p (t h) d", h=H)
        m = ready
        for n in range(3):
            part = parts[:, :, slots.index(n), :]
            m = lane(m).done(lane.eng.tensor_copy(part, x))
            yield m
            if n < 2:
                m = lane(m).done(lane.eng.tensor_tensor(x, x, part, ALU.subtract))
                yield m

    def keys(self, z, keys):
        g, G = self.k.g, self.k.nc.gpsimd
        m_k = z.load(1, z.kf[:, :, :], rows(keys))
        for m in self.split(g, z.kf, z.kp, self.K_PARTS, m_k):
            yield
        flat = z.kp[:, :, :, :].rearrange("p n s d -> p n (s d)")
        g(m).done(G.tensor_copy(flat[:, :, 3 * D:6 * D], flat[:, :, 0:3 * D]))
        yield
        g(m).done(G.tensor_copy(flat[:, :, 6 * D:8 * D], flat[:, :, 0:2 * D]))
        yield

    def heads_down(self, z, parts, dst, ready, banks, by_act=False):
        k, nc = self.k, self.k.nc
        for c in range(0, H, 2):
            bank = banks[c // 2 % len(banks)]
            k.pe(ready, k.drained.get(bank))
            for n in range(2):
                for t in range(NT):
                    m = k.pe.done(nc.tensor.matmul(
                        k.bank[bank][:, n * T + t * P:n * T + (t + 1) * P],
                        parts[:, t * H + c + n, :, :].rearrange("p s d -> p (s d)"), k.identb[:, :], start=True, stop=True))
            out, src = dst[:, c:c + 2, :].rearrange("p n t -> p (n t)"), k.bank[bank][:, :]
            m = k.s(m).done(nc.scalar.copy(out, src)) if c // 2 % 2 or by_act else k.v(m).done(nc.vector.tensor_copy(out, src))
            evacuated(k, bank, m)
            yield m

    def maxima(self, z, hT, ready):
        k, nc = self.k, self.k.nc
        v, s, pe, V, A = k.v, k.s, k.pe, k.nc.vector, k.nc.scalar
        b0, b1, b2, b3 = z.banks
        for t in range(NT):
            m = project(k, b2, [hT[:, kt, t * P:(t + 1) * P] for kt in range(KC)],
                        [self.w["q"][:, kt, :] for kt in range(KC)], ready, col=t * C)
        yield
        turning = self.heads_down(z, z.kp, z.kT, None, (b0, b1))
        km = [next(turning)]
        m = evacuated(k, b2, v(m).done(V.tensor_tensor(z.qf[:, :, :], two(k.bank[b2][:, :]), rep(self.bq[:, :], 1, NT),
                                                       ALU.add)))
        yield
        for m in self.split(v, z.qf, z.qp, self.Q_PARTS, m):
            km.append(next(turning))
            yield
        copies = lambda at, n: (z.qp[:, :, at:at + n, :], rep(z.qp[:, :, at - 1, :], 2, n))
        m1 = s(m).done(A.copy(*copies(1, 2)))
        m2 = v(m).done(V.tensor_copy(*copies(4, 2)))
        m1 = s().done(A.copy(*copies(7, 1)))
        yield
        for m in turning:
            km.append(m)
            yield
        pe(m1, *km[-2:])
        turning = self.heads_down(z, z.qp, z.qT, m2, (b2, b3), by_act=True)
        ahead = next(turning)
        yield
        for c in range(0, H, 2):
            qm, ahead = ahead, next(turning, None)
            yield
            for it in range(NT):
                cols = slice(0, (it + 1) * P if self.causal else T)
                m = self.scores(z, z.banks[it], c, it, False, cols, ready=qm)
                evacuated(k, z.banks[it], v(m).done(V.tensor_reduce(
                    z.nmax[:, it, c:c + 2], k.bank[z.banks[it]][:, :].rearrange("p (n j) -> p n j", n=2)[:, :, cols],
                    AX.X, ALU.max, negate=True)))
                yield

    def scores(self, z, bank, c, tile, keys_down, cols, last=None, ready=None):
        k, nc = self.k, self.k.nc
        k.pe(ready, k.drained.get(bank))
        both = k.bank[bank][:, :].rearrange("p (n t) -> p n t", n=2)
        todo = []
        if self.causal:
            mask = (self.maskT if keys_down else self.mask)[:, tile, cols]
            todo.append((both[:, :, cols], k.identb[:, :], rep(mask, 1, 2)))
        for n in range(2):
            q, kk = z.qT[:, c + n, :], z.kT[:, c + n, :]
            down, row = (kk, q) if keys_down else (q, kk)
            todo.append((both[:, n, cols], down[:, tile * P:(tile + 1) * P], row[:, cols]))
            if last:
                todo.append((both[:, n, cols], *last(c + n)))
        for i, (dst, a, b) in enumerate(todo):
            m = k.pe.done(nc.tensor.matmul(dst, a, b, start=i == 0, stop=i == len(todo) - 1))
        return m

    def weighed(self, z):
        k, nc = self.k, self.k.nc
        v, s, pe, V, A = k.v, k.s, k.pe, k.nc.vector, k.nc.scalar
        b0, b1, b2, b3 = z.banks
        pe(k.drained.get(b2))
        for it in range(NT):
            m = pe.done(nc.tensor.transpose(k.bank[b2][:, it * P:(it + 1) * P], z.nmax[:, it, :], k.ident[:, :]))
        yield
        nt = evacuated(k, b2, v(m).done(V.tensor_copy(z.nmaxT[:, :], k.bank[b2][:, 0:T])))
        yield
        pe(nt)
        pick = lambda cols: lambda head: (k.identb[:, head:head + 1].broadcast_to([P, P]), z.nmaxT[:, cols])
        ex, weighed = {}, {}

        def weigh(c):
            pe(ex[c], k.drained.get(b2) if c == 0 else None, k.drained.get(b3) if c == 0 else None)
            for it in range(NT):
                keys = range(it + 1 if self.causal else NT)
                for jt in keys:
                    m = pe.done(nc.tensor.matmul(k.bank[z.banks[2 + it]][:, c * (D + 1):(c + 1) * (D + 1)],
                                                 z.pT[:, c // 2 % RING, jt, c % 2, it * P:(it + 1) * P], z.va[:, jt, c, :],
                                                 start=jt == 0, stop=jt == keys[-1]))
            weighed[c - c % 2] = m
            return m

        for c in range(0, H, 2):
            for jt in range(NT):
                cols = slice(jt * P if self.causal else 0, T)
                bank = z.banks[jt]
                m = self.scores(z, bank, c, jt, True, cols, pick(cols))
                ex[c] = ex[c + 1] = evacuated(k, bank, s(m, weighed.get(c - 2 * RING)).done(A.activation(
                    z.pT[:, c // 2 % RING, jt, :, cols], k.bank[bank][:, :].rearrange("p (n i) -> p n i", n=2)[:, :, cols],
                    ACT.Exp, scale=1.0 / math.sqrt(D))))
                yield
            if c:
                weigh(c - 2)
                weigh(c - 1)
        weigh(H - 2)
        m = weigh(H - 1)
        yield
        for it in range(NT):
            bank = z.banks[2 + it]
            o = k.bank[bank][:, 0:H * (D + 1)].rearrange("p (c d) -> p c d", c=H)
            r = v(m).done(V.reciprocal(z.rden[:, it, :], o[:, :, D:D + 1].rearrange("p c o -> p (c o)")))
            yield
            at = v(r).done(V.tensor_tensor(z.att[:, it, :].rearrange("p (h d) -> p h d", h=H), o[:, :, 0:D],
                                           rep(z.rden[:, it, :], 2, D), ALU.mult))
            evacuated(k, bank, at)
        m = yield from hidden_turned(k, z.att, z.attT, at, b0)
        for t in range(NT):
            m = project(k, b1, [z.attT[:, kt, t * P:(t + 1) * P] for kt in range(KC)],
                        [self.w["o"][:, kt, :] for kt in range(KC)], m if t == 0 else None, col=t * C)
        yield
        return m


def two(ap):
    return ap.rearrange("p (t c) -> p t c", t=NT)


def flat2(ap):
    return ap.rearrange("p t c -> p (t c)")


def add_rows(k, x, bank, bias, mark):
    v, V = k.v, k.nc.vector
    m = evacuated(k, bank, v(mark).done(V.tensor_tensor(x[:, :, :], x[:, :, :], two(k.bank[bank][:, :]), ALU.add)))
    yield
    if bias is not None:
        m = v(m).done(V.tensor_tensor(x[:, :, :], x[:, :, :], rep(bias[:, :], 1, NT), ALU.add))
        yield
    return m


def hidden_turned(k, h, hT, m, bank):
    m = turn(k, h, bank, m)
    yield
    m = evacuated(k, bank, k.s(m).done(k.nc.scalar.copy(hT[:, :, :].rearrange("p k t -> p (k t)"), k.bank[bank][:, :])))
    yield
    return m


rows = lambda a: a.rearrange("(t p) c -> p t c", p=P)
kp = lambda a: a.rearrange("(k p) n -> p k n", p=P)


def layer0_rest(k, io, dr):
    nc, v, s, pe = k.nc, k.v, k.s, k.pe
    V, A = nc.vector, nc.scalar
    FB = F // P
    with ExitStack() as scope:
        sb = lambda n, sh, dt=F32: k.sbuf(scope, "l0_" + n, sh, dt)
        slots = [Slot(k, scope, "l0", n) for n in range(2)]
        at = Attention(k, io, scope, "l0x_", True, slots)
        wo, bo = sb("wo", [P, KC, C]), sb("bo", [P, C])
        gnw, gnb = sb("gnw", [P, KC]), sb("gnb", [P, KC])
        ga, gb = sb("ga", [P, KC, E + E * R]), sb("gb", [P, E])
        wi, wib = sb("wi", [P, KC, F]), sb("wib", [P, FB])
        lb = sb("lb", [P, F])
        w2, w2b = sb("w2", [P, FB, C]), sb("w2b", [P, C])
        for z in slots:
            z.x, z.h, z.hT = z.sb("x", [P, NT, C]), z.sb("h", [P, NT, C]), z.sb("hT", [P, KC, T])
            z.wkv, z.gate, z.wT = z.sb("wkv", [P, NT, C]), z.sb("gate", [P, NT, C]), z.sb("wT", [P, KC, T])
            z.lg, z.mx, z.ix = z.sb("lg", [P, NT, E]), z.sb("mx", [P, NT, 8]), z.sb("ix", [P, NT, 8], U32)
            z.ixf, z.oh = z.sb("ixf", [P, NT]), z.sb("oh", [P, NT, E])
            z.am, z.amT = z.sb("am", [P, NT, P]), z.sb("amT", [P, T])
            z.mid = z.sb("mid", [P, FB, T])
            v().done(V.memset(z.am[:, :, :], 0.0))
        load_weight(k, wo[:, :, :], kp(io["w_o"]))
        load_weight(k, bo[:, :], row_to_all(io["L0_attn_b_o"], P))
        load_weight(k, gnw[:, :], io["L0_attn_gn_weight"].rearrange("(k p) -> p k", p=P))
        load_weight(k, gnb[:, :], io["L0_attn_gn_bias"].rearrange("(k p) -> p k", p=P))
        load_weight(k, wib[:, :], io["L0_ffn_wi_b"].rearrange("(k p) -> p k", p=P))
        load_weight(k, ga[:, :, 0:E], kp(io["gate_wT"]))
        load_weight(k, ga[:, :, E:], kp(io["lora_aT"]))
        load_weight(k, gb[:, :], row_to_all(io["L0_ffn_gate_b"], P))
        load_weight(k, wi[:, :, :], kp(io["wiT"]))
        zero = v().done(V.memset(lb[:, :], 0.0))
        k.queues[0](zero).done(nc.sync.dma_start(lb[0:E * R, :], io["lora_bT"]))
        load_weight(k, w2[:, :, :], kp(io["woT"]))
        load_weight(k, w2b[:, :], row_to_all(io["L0_ffn_wo_b"], P))
        k.fence()

        def ahead(b, z):
            z.load(0, z.wkv[:, :, :], rows(dr["wkv"][b]))
            z.load(2, z.gate[:, :, :], rows(dr["g"][b]))
            yield from at.keys(z, dr["k0"][b])

        def first(b, z):
            b0, b1, b2, b3 = z.banks
            z.load(4, z.va[:, :, :, :].rearrange("p t h d -> p t (h d)"), rows(dr["v0"][b]))
            m_x = z.load(3, z.x[:, :, :], rows(io["x"][b]))
            m = turn(k, z.wkv, b0, None)
            yield
            for kt in range(KC):
                a = v(m).done(V.tensor_scalar(z.wT[:, kt, :], k.bank[b0][:, kt * T:(kt + 1) * T], gnw[:, kt:kt + 1],
                                              gnb[:, kt:kt + 1], ALU.mult, ALU.add))
            evacuated(k, b0, a)
            yield
            for t in range(NT):
                m = project(k, b1, [z.wT[:, kt, t * P:(t + 1) * P] for kt in range(KC)], [wo[:, kt, :] for kt in range(KC)],
                            a, col=t * C)
            m = evacuated(k, b1, v(m).done(V.tensor_tensor(z.wkv[:, :, :], two(k.bank[b1][:, :]), rep(bo[:, :], 1, NT), ALU.add)))
            yield
            m = v(m).done(V.tensor_tensor(z.wkv[:, :, :], z.wkv[:, :, :], z.gate[:, :, :], ALU.mult))
            yield
            m = v(m, m_x).done(V.tensor_tensor(z.x[:, :, :], z.x[:, :, :], z.wkv[:, :, :], ALU.add))
            yield
            m = yield from layer_norm(k, z, z.x, z.h, m)
            m = yield from hidden_turned(k, z.h, z.hT, m, b0)
            yield from at.maxima(z, z.hT, m)

        def second(b, z):
            b0, b1, b2, b3 = z.banks
            m = yield from at.weighed(z)
            m = yield from add_rows(k, z.x, b1, at.bo, m)
            m = yield from layer_norm(k, z, z.x, z.h, m)
            m = yield from hidden_turned(k, z.h, z.hT, m, b0)
            for t in range(NT):
                p = project(k, b1, [z.hT[:, kt, t * P:(t + 1) * P] for kt in range(KC)], [ga[:, kt, :] for kt in range(KC)],
                            m, col=t * 64)
            yield
            cut = k.bank[b1][:, 0:NT * 64].rearrange("p (t c) -> p t c", t=NT)
            a = v(p).done(V.tensor_tensor(z.lg[:, :, :], cut[:, :, 0:E], rep(gb[:, :], 1, NT), ALU.add))
            yield
            for t in range(NT):
                q = v(a).done(V.max(z.mx[:, t, :], z.lg[:, t, :]))
            yield
            for t in range(NT):
                q = v(q).done(V.max_index(z.ix[:, t, :], z.mx[:, t, :], z.lg[:, t, :]))
            yield
            q = v(q).done(V.tensor_copy(z.ixf[:, :], z.ix[:, :, 0:1].rearrange("p t o -> p (t o)")))
            yield
            q = v(q).done(V.tensor_tensor(z.oh[:, :, :], rep(k.iota64[:, 0:E], 1, NT), rep(z.ixf[:, :], 2, E), ALU.is_equal))
            yield
            for t in range(NT):
                q = v(q).done(V.tensor_tensor(z.am[:, t, 0:E * R].rearrange("p (e r) -> p e r", e=E),
                                              cut[:, t, E:E + E * R].rearrange("p (e r) -> p e r", e=E),
                                              rep(z.oh[:, t, :], 2, R), ALU.mult))
            evacuated(k, b1, q)
            yield
            pe(q, k.drained.get(b2))
            for t in range(NT):
                q = pe.done(nc.tensor.transpose(k.bank[b2][:, t * P:(t + 1) * P], z.am[:, t, :], k.ident[:, :]))
            yield
            q = evacuated(k, b2, v(q).done(V.tensor_copy(z.amT[:, :], k.bank[b2][:, 0:T])))
            yield
            for f in range(FB):
                bank = z.banks[1 + f % 3]
                fs = slice(f * P, (f + 1) * P)
                p = project(k, bank, [wi[:, kt, fs] for kt in range(KC)] + [lb[:, fs]],
                            [z.hT[:, kt, :] for kt in range(KC)] + [z.amT[:, :]], q)
                r = evacuated(k, bank, v(p).done(V.tensor_scalar(z.mid[:, f, :], k.bank[bank][:, 0:T], wib[:, f:f + 1], 0.0,
                                                                 ALU.add, ALU.max)))
                yield
            for t in range(NT):
                p = project(k, b0, [z.mid[:, f, t * P:(t + 1) * P] for f in range(FB)], [w2[:, f, :] for f in range(FB)],
                            r, col=t * C)
                yield
            m = yield from add_rows(k, z.x, b0, w2b, p)
            z.load(5, rows(dr["x1"][b]), z.x[:, :, :], m)

        staggered(k, slots, ahead, first, second)


def ssm_inputs(k, io, dr):
    nc, v, s, pe = k.nc, k.v, k.s, k.pe
    V, A = nc.vector, nc.scalar
    with ExitStack() as scope:
        sb = lambda n, sh, dt=F32: k.sbuf(scope, "si_" + n, sh, dt)
        nw = sb("nw", [P, KC])
        win = sb("win", [P, KC, 2 * INNER])
        cw, cb, db = sb("cw", [P, IB, KW]), sb("cb", [P, IB]), sb("db", [P, IB])
        wdt, wbc = sb("wdt", [P, IB, INNER]), sb("wbc", [P, IB, 2 * N])
        slots = [Slot(k, scope, "si", n, of=4) for n in range(4)]
        for z in slots:
            z.x, z.h, z.hT = z.sb("x", [P, NT, C]), z.sb("h", [P, NT, C]), z.sb("hT", [P, KC, T])
            z.sq, z.ms = z.sb("sq", [P, NT, C]), z.sb("ms", [P, NT])
            z.xpad = z.sb("xpad", [P, IB, T + KW - 1])
            z.acc = z.sb("acc", [P, 2, IB, T])
            z.xc, z.zs, z.ub = z.sb("xc", [P, IB, T]), z.sb("zs", [P, IB, T]), z.sb("ub", [P, IB, T])
            z.dt, z.dx = z.acc[:, 0, :, :], z.acc[:, 1, :, :]
            z.bc, z.rest = z.sb("bc", [P, 3, T], BF16), z.sb("rest", [P, 2, T])
            v().done(V.memset(z.xpad[:, :, 0:KW - 1], 0.0))
        load_weight(k, nw[:, :], io["L1_attn_norm_w"].rearrange("(k p) -> p k", p=P))
        load_weight(k, cw[:, :, :], io["L1_attn_conv_w"].rearrange("(k p) o w -> p k (o w)", p=P))
        load_weight(k, cb[:, :], io["L1_attn_conv_b"].rearrange("(k p) -> p k", p=P))
        load_weight(k, db[:, :], io["L1_attn_dt_b"].rearrange("(k p) -> p k", p=P))
        load_weight(k, wbc[:, :, 0:N], kp(io["b_wT"]))
        load_weight(k, wbc[:, :, N:], kp(io["c_wT"]))
        load_weight(k, win[:, :, :], kp(io["in_projT"]))
        load_weight(k, wdt[:, :, :], kp(io["dt_wT"]))
        k.fence()
        fl = lambda a: a[:, :, :].rearrange("p j t -> p (j t)")

        def one(b, z):
            b0, b1 = z.banks
            m = z.load(0, z.x[:, :, :], rows(dr["x1"][b]))
            m = hm = yield from layer_norm(k, z, z.x, z.h, m)
            m = v(m).done(V.tensor_tensor(z.sq[:, :, :], z.h[:, :, :], z.h[:, :, :], ALU.mult))
            yield
            m = v(m).done(V.tensor_reduce(z.ms[:, :], z.sq[:, :, :], AX.X, ALU.add))
            yield
            m = v(m).done(V.tensor_scalar(z.ms[:, :], z.ms[:, :], 1.0 / C, 1e-6, ALU.mult, ALU.add))
            m = s(m).done(A.activation(z.ms[:, :], z.ms[:, :], ACT.Sqrt))
            yield
            m = v(m).done(V.reciprocal(z.ms[:, :], z.ms[:, :]))
            yield
            m = v(m).done(V.tensor_tensor(z.sq[:, :, :], z.h[:, :, :], rep(z.ms[:, :], 2, C), ALU.mult))
            q = v(hm).done(V.tensor_tensor(z.x[:, :, :], z.x[:, :, :], z.h[:, :, :], ALU.add))
            z.load(1, rows(dr["x2"][b]), z.x[:, :, :], q)
            m = turn(k, z.sq, b0, m)
            yield
            for kt in range(KC):
                a = v(m).done(V.tensor_scalar(z.hT[:, kt, :], k.bank[b0][:, kt * T:(kt + 1) * T], nw[:, kt:kt + 1], None, ALU.mult))
            evacuated(k, b0, a)
            yield
            for j in range(IB):
                bank = z.banks[j % 2]
                for i, o in ((0, 0), (1, INNER)):
                    p = project(k, bank, [win[:, kt, o + j * P:o + (j + 1) * P] for kt in range(KC)],
                                [z.hT[:, kt, :] for kt in range(KC)], a, col=i * T)
                yield
                c = v(p).done(V.tensor_copy(z.xpad[:, j, KW - 1:], k.bank[bank][:, 0:T]))
                zm = evacuated(k, bank, s(c).done(A.activation(z.zs[:, j, :], k.bank[bank][:, T:2 * T], ACT.Silu)))
                yield
                c = v(c).done(V.tensor_scalar(z.acc[:, 0, j, :], z.xpad[:, j, 0:T], cw[:, j, 0:1], None, ALU.mult))
                for w in range(1, KW):
                    yield
                    c = v(c).done(V.scalar_tensor_tensor(z.acc[:, w % 2, j, :], z.xpad[:, j, w:w + T], cw[:, j, w:w + 1],
                                                         z.acc[:, 1 - w % 2, j, :], ALU.mult, ALU.add))
                cx = s(c).done(A.activation(z.xc[:, j, :], z.acc[:, (KW - 1) % 2, j, :], ACT.Silu, bias=cb[:, j:j + 1]))
            z.load(2, dr["xc"][b], fl(z.xc), cx)
            z.load(2, dr["zs"][b], fl(z.zs), zm)
            yield
            for j in range(IB):
                bank = z.banks[j % 2]
                p = project(k, bank, [wdt[:, kt, j * P:(j + 1) * P] for kt in range(IB)], [z.xc[:, kt, :] for kt in range(IB)], cx)
                yield
                p = evacuated(k, bank, v(p).done(V.tensor_scalar(z.ub[:, j, :], k.bank[bank][:, 0:T], db[:, j:j + 1],
                                                                 None, ALU.add)))
            m = v(p).done(V.tensor_scalar(fl(z.dt), fl(z.ub), -1.0, None, ALU.mult))
            yield
            m = v(m).done(V.tensor_tensor(fl(z.dx), fl(z.ub), fl(z.dt), ALU.min))
            m = s(m).done(A.activation(fl(z.dx), fl(z.dx), ACT.Exp))
            yield
            n_ = v(m).done(V.tensor_scalar(fl(z.dt), fl(z.ub), 0.0, 1e-4, ALU.max, ALU.add))
            m = s(m).done(A.activation(fl(z.dx), fl(z.dx), ACT.Ln, bias=1.0))
            yield
            p = project(k, b0, [wbc[:, kt, :] for kt in range(IB)], [z.xc[:, kt, :] for kt in range(IB)], cx)
            m = v(n_, m).done(V.tensor_tensor(fl(z.dt), fl(z.dt), fl(z.dx), ALU.add))
            yield
            q = v(m).done(V.tensor_tensor(fl(z.dx), fl(z.dt), fl(z.xc), ALU.mult))
            z.load(3, dr["dt"][b], fl(z.dt), m)
            z.load(3, dr["dx"][b], fl(z.dx), q)
            src = k.bank[b0][:, 0:T]
            m = v(p).done(V.tensor_copy(z.bc[:, 0, :], src))
            yield
            m = v(m).done(V.tensor_tensor(z.rest[:, 0, :], src, z.bc[:, 0, :], ALU.subtract))
            yield
            m = v(m).done(V.tensor_copy(z.bc[:, 1, :], z.rest[:, 0, :]))
            yield
            m = v(m).done(V.tensor_tensor(z.rest[:, 1, :], z.rest[:, 0, :], z.bc[:, 1, :], ALU.subtract))
            yield
            m = v(m).done(V.tensor_copy(z.bc[:, 2, :], z.rest[:, 1, :]))
            z.load(4, dr["bc"][b], z.bc[:, :, :].rearrange("p a t -> p (a t)"), m)

        sequences(k, slots, one, lag=1)


def ssm_scan(k, io, dr):
    nc, v, s, pe, g = k.nc, k.v, k.s, k.pe, k.g
    V, A = nc.vector, nc.scalar
    G = 2
    W = G * T
    UN = 4
    with ExitStack() as scope:
        sb = lambda n, sh, dt=F32: k.sbuf(scope, "ss_" + n, sh, dt)
        neg_a = sb("neg_a", [P, IB, N])
        dpar = sb("dpar", [P, IB])
        ROWS = 3 * N // 2
        inputs = [(sb(f"dt{i}", [P, IB, G, T]), sb(f"dx{i}", [P, IB, G, T]), sb(f"bc{i}", [ROWS, 2, 2, G, T], BF16))
                  for i in range(2)]
        xc, zs = sb("xc", [P, IB, G, T]), sb("zs", [P, IB, G, T])
        pick = sb("pick", [ROWS, N // 2], BF16)
        decay = [sb(f"decay{i}", [P, IB, G, T]) for i in range(UN)]
        b_all = [sb(f"b_all{i}", [P, W]) for i in range(2)]
        inp = [sb(f"inp{i}", [P, IB, W]) for i in range(UN)]
        h = [sb(f"h{i}", [P, IB, W]) for i in range(UN)]
        ch = [sb(f"ch{i}", [P, IB, W]) for i in range(UN)]
        load_weight(k, neg_a[:, :, :], io["L1_attn_A_log"].rearrange("(j p) n -> p j n", p=P))
        m = load_weight(k, dpar[:, :], io["L1_attn_D_param"].rearrange("(j p) -> p j", p=P))
        m = s(m).done(A.activation(neg_a[:, :, :], neg_a[:, :, :], ACT.Exp))
        v(m).done(V.tensor_scalar(neg_a[:, :, :], neg_a[:, :, :], -1.0, None, ALU.mult))
        z = g().done(nc.gpsimd.memset(pick[:, :], 0.0))
        for part in range(3):
            z = g(z).done(nc.gpsimd.affine_select(out=pick[:, :], in_=pick[:, :], compare_op=ALU.not_equal, fill=1.0,
                                                  base=-part * N // 2, pattern=[[-1, N // 2]], channel_multiplier=1))
        for t in decay:
            g().done(nc.gpsimd.memset(t[:, :, :, 0:1], 0.0))
        k.fence()
        flat = lambda a: a.rearrange("p j w -> p (j w)")
        done = k.states

        def wait(lane, step, count, static):
            if not static or count > 0:
                lane.eng.wait_ge(done[step], count)

        def load_ahead(pair, buffers):
            dt, dx, bc = buffers
            for i in range(G):
                seq = pair * G + i
                for q, (name, t) in enumerate((("dt", dt), ("dx", dx))):
                    k.queues[q]().done(nc.sync.dma_start(t[:, :, i, :], dr[name][seq].rearrange("p (j t) -> p j t", j=IB)))
                parts = dr["bc"][seq].rearrange("(c r s) (a t) -> a r c s t", c=2, s=2, a=3)
                for part in range(3):
                    for which in range(2):
                        k.queues[4]().done(nc.sync.dma_start(bc[part * N // 2:(part + 1) * N // 2, which, :, i, :],
                                                             parts[part, :, which]))
            return [k.queues[q].last for q in (0, 1, 4)]

        def entered(i, n, u, static):
            dt, dx, bc = inputs[i % 2]
            m = i * N + n
            wait(pe, "copied", m - 1, static)
            spread(bc, n, u, 0, 4 + u % 2, "b")
            wait(s, "input", m - 1, static)
            wait(s, "b", m + 1, static)
            A.copy(b_all[u % 2][:, :], k.bank[4 + u % 2][:, :]).then_inc(done["copied"], 1)
            wait(s, "scan", m - 3, static)
            for j in range(IB):
                last = A.activation(decay[u][:, j, :, 1:T], dt[:, j, :, 1:T], ACT.Exp, scale=neg_a[:, j, bass.ds(n, 1)])
            last.then_inc(done["decay"], 1)
            wait(g, "copied", m + 1, static)
            wait(g, "scan", m - 3, static)
            nc.gpsimd.tensor_tensor(inp[u][:, :, :], dx[:, :, :, :].rearrange("p j g t -> p j (g t)"),
                                    rep(b_all[u % 2][:, :], 1, IB), ALU.mult).then_inc(done["input"], 1)

        def spread(bc, n, u, which, bank, step):
            nc.tensor.matmul(k.bank[bank][:, :], pick[:, bass.ds(n // 2, 1)].broadcast_to([ROWS, P]),
                             bc[:, which, u % 2, :, :].rearrange("p g t -> p (g t)"), start=True,
                             stop=True).then_inc(done[step], 1)

        def scanned(i, n, u, static):
            m = i * N + n
            wait(v, "input", m + 1, static)
            wait(v, "decay", m + 1, static)
            wait(v, "weighed", m - 3, static)
            V.tensor_tensor_scan(flat(h[u][:, :, :]), decay[u][:, :, :, :].rearrange("p j g t -> p (j g t)"),
                                 flat(inp[u][:, :, :]), 0.0, ALU.mult, ALU.add).then_inc(done["scan"], 1)

        def weighed(i, n, u, static):
            m = i * N + n
            wait(pe, "weighed", m - 1, static)
            spread(inputs[i % 2][2], n, u, 1, 6 + u % 2, "c")
            wait(v, "scan", m + 1, static)
            wait(v, "c", m + 1, static)
            wait(v, "summed", m - 3, static)
            V.tensor_tensor(ch[u][:, :, :], h[u][:, :, :], rep(k.bank[6 + u % 2][:, :], 1, IB),
                            ALU.mult).then_inc(done["weighed"], 1)

        def summed(i, n, u, static):
            wait(pe, "weighed", i * N + n + 1, static)
            for j in range(IB):
                last = nc.tensor.matmul(k.bank[j][:, :], k.ident[:, :], ch[u][:, j, :], start=static and n == 0, stop=False,
                                        skip_group_check=True)
            last.then_inc(done["summed"], 1)

        def step(i, n, u, static):
            for behind, stage in enumerate((entered, scanned, weighed, summed)):
                if static and n < behind:
                    if i:
                        stage(i - 1, N + n - behind, (u - behind) % UN, static)
                elif i < GROUP:
                    stage(i, n - behind, (u - behind) % UN, static)

        def gated(group, i):
            v(k.queues[2].last, k.queues[3].last)
            v.eng.wait_ge(done["summed"], (i + 1) * N)
            flat_w = lambda a: a.rearrange("p g t -> p (g t)")
            for j in range(IB):
                m = v().done(V.scalar_tensor_tensor(flat_w(xc[:, j, :, :]), flat_w(xc[:, j, :, :]), dpar[:, j:j + 1],
                                                    k.bank[j][:, :], ALU.mult, ALU.add))
            pe(m)
            for j in range(IB):
                m = v(m).done(V.tensor_tensor(flat_w(zs[:, j, :, :]), flat_w(xc[:, j, :, :]), flat_w(zs[:, j, :, :]), ALU.mult))
            for g_ in range(G):
                m = k.queues[5](m).done(nc.sync.dma_start(
                    dr["ys"][(group * GROUP + i) * G + g_].rearrange("p (j t) -> p j t", j=IB), zs[:, :, g_, :]))
            return m

        PAIRS, GROUP = B // G, 4
        load_ahead(0, inputs[0])
        k.fence()
        with nc.Fori(0, PAIRS // GROUP) as group:
            stored = loaded = None
            for i in range(GROUP + 1):
                if loaded and i < GROUP:
                    s(loaded[0])
                    g(loaded[1])
                    pe(loaded[2])
                for n in range(2 * UN if i < GROUP else UN):
                    if n == 3 and i:
                        stored = gated(group, i - 1)
                    step(i, n, n % UN, True)
                    if n == 3 and i < GROUP:
                        for name in ("b", "c", "decay", "input"):
                            wait(k.sp, name, i * N, True)
                        loaded = load_ahead((group * GROUP + i + 1) % PAIRS, inputs[1 - i % 2])
                        k.sp(stored)
                        for q, (name, t) in enumerate((("xc", xc), ("zs", zs)), 2):
                            for g_ in range(G):
                                k.queues[q]().done(nc.sync.dma_start(
                                    t[:, :, g_, :], dr[name][(group * GROUP + i) * G + g_].rearrange("p (j t) -> p j t", j=IB)))
                if i < GROUP:
                    with nc.Fori(2, N // UN) as block:
                        for u in range(UN):
                            step(i, block * UN + u, u, False)
            k.fence()


def layer1_attention(k, io, dr, keep):
    nc, v, s, pe = k.nc, k.v, k.s, k.pe
    V = nc.vector
    with ExitStack() as scope:
        slots = [Slot(k, scope, "l1", n) for n in range(2)]
        at = Attention(k, io, scope, "l1x_", False, slots)
        wout = k.sbuf(scope, "l1_wout", [P, IB, C])
        for z in slots:
            z.x, z.h, z.hT = z.sb("x", [P, NT, C]), z.sb("h", [P, NT, C]), z.sb("hT", [P, KC, T])
            z.ys = z.sb("ys", [P, IB, T])
        load_weight(k, wout[:, :, :], kp(io["out_projT"]))
        k.fence()

        def ahead(b, z):
            z.load(0, z.ys[:, :, :].rearrange("p j t -> p (j t)"), dr["ys"][b])
            yield from at.keys(z, dr["k1"][b])

        def first(b, z):
            b0, b1, b2, b3 = z.banks
            mx = z.load(2, z.x[:, :, :], rows(dr["x2"][b]))
            z.load(4, z.va[:, :, :, :].rearrange("p t h d -> p t (h d)"), rows(dr["v1"][b]))
            for t in range(NT):
                m = project(k, b1, [z.ys[:, j, t * P:(t + 1) * P] for j in range(IB)], [wout[:, j, :] for j in range(IB)],
                            None, col=t * C)
            yield
            v(mx)
            m = yield from add_rows(k, z.x, b1, None, m)
            m = yield from layer_norm(k, z, z.x, z.h, m)
            m = yield from hidden_turned(k, z.h, z.hT, m, b0)
            yield from at.maxima(z, z.hT, m)

        def second(b, z):
            b0, b1, b2, b3 = z.banks
            m = yield from at.weighed(z)
            m = yield from add_rows(k, z.x, b1, at.bo, m)
            z.load(3, rows(dr["x3"][b]), z.x[:, :, :], m)
            m = yield from layer_norm(k, z, z.x, z.h, m)
            m = yield from hidden_turned(k, z.h, z.hT, m, b0)
            for kt in range(KC):
                v(m).done(V.bn_stats(keep["stats"][:, kt, bass.ds(b * 6, 6)], z.hT[:, kt, :]))

        staggered(k, slots, ahead, first, second)


def product_keys(k, io, dr, keep):
    nc, v, s, pe, g = k.nc, k.v, k.s, k.pe, k.g
    V, A = nc.vector, nc.scalar
    NE = NK * NK
    EB = NE // P
    HK = NH * TK
    TILES = B * NT
    with ExitStack() as scope:
        sb = lambda n, sh, dt=F32: k.sbuf(scope, "pk_" + n, sh, dt)
        wk = sb("wk", [P, KC, 2 * NH * NK])
        bg, bb, mv = sb("bg", [P, KC]), sb("bb", [P, KC]), sb("mv", [P, KC, 2])
        bscale, bshift = sb("bscale", [P, KC]), sb("bshift", [P, KC])
        iota128 = sb("iota128", [P, P])
        g().done(nc.gpsimd.iota(iota128[:, :], [[1, P]], base=0, channel_multiplier=0,
                                allow_small_or_imprecise_dtypes=True))
        with ExitStack() as first:
            wq = k.sbuf(first, "pk_wq", [P, 2 * NH, C])
            keys = k.sbuf(first, "pk_keys", [P, 2 * NH, NK])
            load_weight(k, bg[:, :], io["L1_ffn_bn_gamma"].rearrange("(k p) -> p k", p=P))
            load_weight(k, bb[:, :], io["L1_ffn_bn_beta"].rearrange("(k p) -> p k", p=P))
            load_weight(k, wq[:, :, :], io["L1_ffn_w_q"].rearrange("(g p) n -> p g n", p=P))
            m = load_weight(k, keys[:, :, :], io["keysT"])
            for kt in range(KC):
                for half in range(2):
                    bank = kt * 2 + half
                    pe(m)
                    for q in range(NH):
                        p = pe.done(nc.tensor.matmul(k.bank[bank][:, q * NK:(q + 1) * NK],
                                                     wq[:, half * NH + q, kt * P:(kt + 1) * P], keys[:, half * NH + q, :],
                                                     start=True, stop=True))
                    v(p).done(V.tensor_copy(wk[:, kt, half * 512:(half + 1) * 512], k.bank[bank][:, :]))
            for kt in range(KC):
                m = v().done(V.bn_aggr(mv[:, kt, :], keep["stats"][:, kt, :]))
            m = v(m).done(V.tensor_scalar(bscale[:, :], mv[:, :, 1:2].rearrange("p k o -> p (k o)"), 1e-5, None, ALU.add))
            m = s(m).done(A.activation(bscale[:, :], bscale[:, :], ACT.Sqrt))
            m = v(m).done(V.reciprocal(bscale[:, :], bscale[:, :]))
            m = v(m).done(V.tensor_tensor(bscale[:, :], bscale[:, :], bg[:, :], ALU.mult))
            m = v(m).done(V.tensor_tensor(bshift[:, :], mv[:, :, 0:1].rearrange("p k o -> p (k o)"), bscale[:, :], ALU.mult))
            m = v(m).done(V.tensor_tensor(bshift[:, :], bb[:, :], bshift[:, :], ALU.subtract))
            k.fence()
        down, up = sb("down", [P, KC, EB, P]), sb("up", [P, EB, C])
        slots = [Slot(k, scope, "pk", n) for n in range(2)]
        for z in slots:
            z.x, z.h, z.hT = z.sb("x", [P, 1, C]), z.sb("h", [P, 1, C]), z.sb("hT", [P, KC, P])
            z.rowhot = z.sb("rowhot", [P, 64, P], BF16)
            z.blockhot = z.sb("blockhot", [P, 3, 64, EB], BF16)
        xn = sb("xn", [P, KC, P])
        sim = sb("sim", [P, 2, NH, NK])
        top, tix, tif = sb("top", [P, 2, NH, TK]), sb("tix", [P, 2 * NH, TK], U32), sb("tif", [P, 2, NH, TK])
        comb = sb("comb", [P, NH, TK, TK])
        sc, pk = sb("sc", [P, NH, TK]), sb("pk", [P, NH, TK], U32)
        sel, self_ = sb("sel", [P, 2, HK], U32), sb("self", [P, 2, HK])
        eq = sb("eq", [P, HK, TK])
        chosen, upper = sb("chosen", [P, 2, HK]), sb("upper", [P, HK])
        vals = sb("vals", [P, 3, 2, HK])
        turned = sb("turned", [P, 3, 64])
        onehot, parts, left_ = sb("onehot", [P, 64, EB], BF16), sb("parts", [P, 3, 64], BF16), sb("left", [P, 2, 64])
        act = sb("act", [P, EB, P])
        load_weight(k, down[:, :, :, :], io["downT"].rearrange("(k p) (j e) -> p k j e", p=P, e=P))
        load_weight(k, up[:, :, :], io["upT"])
        k.fence()
        by_token = lambda a: a.rearrange("b t c -> (b t) c")

        def choose(tile, z):
            m = z.load(0, z.x[:, 0, :], by_token(dr["x3"])[bass.ds(tile * P, P), :])
            m = yield from layer_norm(k, z, z.x, z.h, m, tiles=1)
            m = turn(k, z.h, 0, m, tiles=1)
            yield
            ht = v(m).done(V.tensor_copy(z.hT[:, :, :].rearrange("p k t -> p (k t)"), k.bank[0][:, 0:KC * P]))
            yield
            for kt in range(KC):
                m = v(ht).done(V.tensor_scalar(xn[:, kt, :], z.hT[:, kt, :], bscale[:, kt:kt + 1], bshift[:, kt:kt + 1],
                                               ALU.mult, ALU.add))
            evacuated(k, 0, m)
            for half in range(2):
                p = project(k, 1 + half, [xn[:, kt, :] for kt in range(KC)],
                            [wk[:, kt, half * 512:(half + 1) * 512] for kt in range(KC)], m)
                yield
                q = evacuated(k, 1 + half, s(p).done(A.copy(sim[:, half, :, :].rearrange("p h n -> p (h n)"), k.bank[1 + half][:, :])))
            yield
            m = q
            for i in range(2 * NH):
                t_ = v(m).done(V.max(top[:, i // NH, i % NH, :], sim[:, i // NH, i % NH, :]))
                if i % 4 == 3:
                    yield
            for i in range(2 * NH):
                x_ = v(t_).done(V.max_index(tix[:, i, :], top[:, i // NH, i % NH, :], sim[:, i // NH, i % NH, :]))
                if i % 4 == 3:
                    yield
            ti = s(x_).done(A.copy(tif[:, :, :, :].rearrange("p a h n -> p (a h n)"),
                                   tix[:, :, :].rearrange("p a n -> p (a n)")))
            m = v(t_).done(V.tensor_tensor(comb[:, :, :, :], rep(top[:, 0, :, :], 3, TK), rep(top[:, 1, :, :], 2, TK),
                                           ALU.add))
            yield
            cflat = comb[:, :, :, :].rearrange("p h a b -> p h (a b)")
            for hd in range(NH):
                m2 = v(m).done(V.max(sc[:, hd, :], cflat[:, hd, :]))
            yield
            for two_ in range(2):
                gate = s(m2).done(A.activation(vals[:, 2, two_, :], sc[:, :, :].rearrange("p h n -> p (h n)"), ACT.Sigmoid))
            for hd in range(NH):
                m3 = v(m2).done(V.max_index(pk[:, hd, :], sc[:, hd, :], cflat[:, hd, :]))
            yield
            pkf = pk[:, :, :].rearrange("p h n -> p (h n)")
            a = v(m3).done(V.tensor_scalar(sel[:, 0, :], pkf, 3, None, ALU.logical_shift_right))
            a = v(m3).done(V.tensor_scalar(sel[:, 1, :], pkf, 7, None, ALU.bitwise_and))
            yield
            a = v(a).done(V.tensor_copy(self_[:, :, :], sel[:, :, :]))
            yield
            for i in range(2):
                e = v(a).done(V.tensor_tensor(eq[:, :, :], rep(self_[:, i, :], 2, TK), rep(iota128[:, 0:TK], 1, HK), ALU.is_equal))
                yield
                by_head = eq[:, :, :].rearrange("p (h n) j -> p h n j", h=NH)
                e2 = v(e, ti).done(V.tensor_tensor(by_head, by_head, rep(tif[:, i, :, :], 2, TK), ALU.mult))
                yield
                e2 = a = v(e2).done(V.tensor_reduce(chosen[:, i, :], eq[:, :, :], AX.X, ALU.add))
                yield
            u_ = v(e2).done(V.tensor_scalar(upper[:, :], chosen[:, 1, :], float(EB), None, ALU.is_ge))
            yield
            for two_ in range(2):
                vl = v(u_).done(V.scalar_tensor_tensor(vals[:, 0, two_, :], upper[:, :], float(NK), chosen[:, 0, :],
                                                       ALU.mult, ALU.add))
                vl = v(u_).done(V.scalar_tensor_tensor(vals[:, 1, two_, :], upper[:, :], -float(EB), chosen[:, 1, :],
                                                       ALU.mult, ALU.add))
            pe(vl, gate, k.drained.get(0))
            for i in range(3):
                p = pe.done(nc.tensor.transpose(k.bank[0][:, i * P:(i + 1) * P],
                                                vals[:, i, :, :].rearrange("p a n -> p (a n)"), k.ident[:, :]))
            yield
            tb = k.bank[0][:, 0:3 * P].rearrange("p (i t) -> p i t", i=3)
            v(p).done(V.tensor_copy(turned[0:64, :, :], tb[0:64, :, 0:64]))
            m = evacuated(k, 0, v(p).done(V.tensor_copy(turned[64:P, :, :], tb[64:P, :, 64:P])))
            yield
            o2 = v(m).done(V.tensor_tensor(onehot[:, :, :], rep(turned[:, 1, :], 2, EB), rep(iota128[:, 0:EB], 1, 64),
                                           ALU.is_equal))
            yield
            for part in range(3):
                if part:
                    rest = turned[:, 2, :] if part == 1 else left_[:, 0, :]
                    m = v(m).done(V.tensor_tensor(left_[:, part - 1, :], rest, parts[:, part - 1, :], ALU.subtract))
                m = v(m).done(V.tensor_copy(parts[:, part, :], left_[:, part - 1, :] if part else turned[:, 2, :]))
                mul = g(o2, m).done(nc.gpsimd.tensor_tensor(z.blockhot[:, part, :, :], onehot[:, :, :],
                                                            rep(parts[:, part, :], 2, EB), ALU.mult))
                yield
            for cut in range(4):
                ts = slice(cut * 16, cut * 16 + 16)
                rh = v().done(V.tensor_tensor(z.rowhot[:, ts, :], rep(turned[:, 0, ts], 2, P), rep(iota128[:, :], 1, 16), ALU.is_equal))
                yield
            z.chosen, z.rowhot_done, z.ready = mul, rh, ht

        def apply(tile, z):
            chosen_, rows_, ht = z.chosen, z.rowhot_done, z.ready
            for jb in range(EB // 4):
                bank = 3 + jb % 2
                pe(ht, k.drained.get(bank))
                for j in range(4 * jb, 4 * jb + 4):
                    p = project(k, bank, [down[:, kt, j, :] for kt in range(KC)], [z.hT[:, kt, :] for kt in range(KC)],
                                None, col=(j % 4) * P)
                ga = evacuated(k, bank, s(p).done(A.activation(
                    act[:, 4 * jb:4 * jb + 4, :].rearrange("p j t -> p (j t)"), k.bank[bank][:, :], ACT.Gelu)))
                yield
            per = 512 // EB
            for tg in range(P // per):
                bank = 6 + tg % 2
                pe(chosen_, rows_, k.drained.get(bank))
                for u in range(per):
                    tok = tg * per + u
                    ps = slice(0, 64) if tok < 64 else slice(64, P)
                    for part in range(3):
                        p = pe.done(nc.tensor.matmul(k.bank[bank][:, u * EB:(u + 1) * EB], z.rowhot[ps, tok % 64, :],
                                                     z.blockhot[ps, part, tok % 64, :], start=part == 0, stop=part == 2))
                yield
                a_ = act[:, :, tg * per:(tg + 1) * per].rearrange("p j t -> p t j")
                w = evacuated(k, bank, v(p, ga).done(V.tensor_tensor(
                    a_, a_, k.bank[bank][:, :].rearrange("p (t n) -> p t n", n=EB), ALU.mult)))
            yield
            pe(w, k.drained.get(5))
            for j in range(EB):
                m = pe.done(nc.tensor.matmul(k.bank[5][:, 0:C], act[:, j, :], up[:, j, :], start=j == 0, stop=j == EB - 1))
                if j % 4 == 3:
                    yield
            k.s(m)
            yield
            m = evacuated(k, 5, v(m).done(V.tensor_tensor(z.x[:, 0, :], z.x[:, 0, :], k.bank[5][:, 0:C], ALU.add)))
            z.stored = z.load(1, by_token(io["out"])[bass.ds(tile * P, P), :], z.x[:, 0, :], m)

        PACE, LAG = (1, 2), 2
        together(choose(0, slots[0]))
        k.fence()
        a, b = slots
        a.chosen = a.rowhot_done = a.ready = None
        with nc.Fori(0, TILES // 2 - 1) as pair:
            together(apply(pair * 2, a), choose(pair * 2 + 1, b), pace=PACE, lag=LAG)
            k.sp(a.stored)
            together(apply(pair * 2 + 1, b), choose(pair * 2 + 2, a), pace=PACE, lag=LAG)
            k.fence()
            a.chosen = a.rowhot_done = a.ready = None
        together(apply(TILES - 2, a), choose(TILES - 1, b), pace=PACE, lag=LAG)
        together(apply(TILES - 1, b))
        k.fence()


def build(nc, io):
    dram = lambda n, sh, dt=F32: nc.dram_tensor("keep_" + n, sh, dt, kind="Internal").ap()
    dr = {n: dram(n, (B, T, C)) for n in ("r", "k", "v", "g", "wkv", "x1", "x2", "x3")}
    dr |= {n: dram(n, (B, T, C)) for n in ("k0", "k1")}
    dr |= {n: dram(n, (B, T, H * (D + 1))) for n in ("v0", "v1")}
    dr |= {n: dram(n, (B, P, IB * T)) for n in ("xc", "zs", "dt", "dx", "ys")}
    dr["bc"] = dram("bc", (B, P, 3 * T), BF16)
    with ExitStack() as ctx:
        ctx.enter_context(nc.allow_non_contiguous_dma("small vectors and head slices go to partitions"))
        k = Core(nc, ctx)
        constants(k)
        keep = {"stats": k.sbuf(ctx, "bn_statistics", [P, KC, B * 6])}
        todo = [lambda: mixer_inputs(k, io, dr), lambda: mixer_scan(k, io, dr), lambda: layer0_rest(k, io, dr),
                lambda: ssm_inputs(k, io, dr), lambda: ssm_scan(k, io, dr),
                lambda: layer1_attention(k, io, dr, keep), lambda: product_keys(k, io, dr, keep)]
        for stage in todo:
            stage()


def laid_out(i):
    c = np.ascontiguousarray
    a = {n: c(np.asarray(x)) for n, x in i.items()}
    out = {n: a[n] for n in (
        "x", "ctx_1024", "L0_attn_b_r", "L0_attn_b_k", "L0_attn_b_v", "L0_attn_b_g", "L0_attn_b_o", "L0_attn_decay",
        "L0_attn_eta", "L0_attn_gn_weight", "L0_attn_gn_bias", "L0_ffn_gate_b", "L0_ffn_wi_b", "L0_ffn_wo_b",
        "L1_attn_conv_w", "L1_attn_conv_b", "L1_attn_A_log", "L1_attn_D_param", "L1_attn_dt_b", "L1_attn_norm_w",
        "L1_ffn_bn_gamma", "L1_ffn_bn_beta", "L1_ffn_w_q")}
    for n in "rkvgo":
        out["w_" + n] = c(a["L0_attn_W_" + n].T)
    for n in "rkvg":
        out["time_mix_" + n] = c(a["L0_attn_time_mix_" + n].reshape(C))
    for n, m in (("wq", "W_q"), ("wk", "W_k"), ("wv", "W_v"), ("bv", "b_v"), ("wo", "W_o"), ("bo", "b_o")):
        out["l0x_" + n] = a["L0_xattn_" + m]
    for n, m in (("wq", "Wq"), ("bq", "b_q"), ("wk", "Wk"), ("bk", "b_k"), ("wv", "Wv"), ("bv", "b_v"), ("wo", "Wo"),
                 ("bo", "b_o")):
        out["l1x_" + n] = a["L1_xattn_" + m]
    out["gate_wT"] = c(a["L0_ffn_gate_W"].T)
    out["lora_aT"] = c(a["L0_ffn_lora_A"].reshape(E * R, C).T)
    out["lora_bT"] = c(a["L0_ffn_lora_B"].transpose(0, 2, 1).reshape(E * R, F))
    out["wiT"], out["woT"] = c(a["L0_ffn_wi_W"].T), c(a["L0_ffn_wo_W"].T)
    out["in_projT"], out["out_projT"] = c(a["L1_attn_in_proj_w"].T), c(a["L1_attn_out_proj_w"].T)
    out["b_wT"], out["c_wT"], out["dt_wT"] = (c(a["L1_attn_" + n].T) for n in ("B_w", "C_w", "dt_w"))
    out["keysT"] = c(a["L1_ffn_keys_p"].transpose(3, 2, 0, 1).reshape(KD, 2 * NH, NK))
    cut = lambda w: w[:NK * NK].reshape(NK, 2, NK // 2, C)
    out["downT"] = c(cut(a["L1_ffn_down"]).transpose(3, 2, 1, 0).reshape(C, NK * NK))
    out["upT"] = c(cut(a["L1_ffn_up"]).transpose(1, 0, 2, 3).reshape(P, NK // 2, C))
    return out


def kernel(**inputs):
    import concourse.bacc as bacc
    from concourse.bass_utils import run_bass_kernel_spmd

    arrays = laid_out(inputs)
    nc = bacc.Bacc("TRN2", target_bir_lowering=False, num_devices=1)
    io = {n: nc.dram_tensor(n, a.shape, mybir.dt.from_np(a.dtype), kind="ExternalInput").ap() for n, a in arrays.items()}
    io["out"] = nc.dram_tensor("out", (B, T, C), F32, kind="ExternalOutput").ap()
    build(nc, io)
    r = run_bass_kernel_spmd(nc, [arrays], core_ids=[0])
    return r.results[0]["out"]
```
